# Optimizing a Trainium2 kernel written in Bass

```python
import numpy as np
import jax
import jax.numpy as jnp

def _softmax(x, axis=-1):
    return jax.nn.softmax(x, axis=axis)

def _gelu(x):
    return jax.nn.gelu(x, approximate=True)

def _silu(x):
    return jax.nn.silu(x)

def _sigmoid(x):
    return jax.nn.sigmoid(x)

def _layernorm(x, axis=-1, eps=1e-05):
    m = jnp.mean(x, axis=axis, keepdims=True)
    v = jnp.var(x, axis=axis, keepdims=True)
    return (x - m) / jnp.sqrt(v + eps)

def _scatter_add(tgt, idx, src, axis=0):
    return tgt.at[idx].add(src)

def _segment_sum(src, seg, n):
    return jax.ops.segment_sum(src, seg, n)
kernel_name = 'mk_gnn_ffn_d2_gnn_r16_77ecbb'

def setup_inputs(seed: int=0):
    np.random.seed(seed)
    _w = jnp.asarray

    def _rec_inputs():
        import jax
        import jax.numpy as jnp
        _gk = jax.random.key(seed)
        x = -0.0003713 + 1 * jax.random.normal(jax.random.fold_in(_gk, 1), (3125, 256), jnp.float32)
        _s = jax.random.randint(jax.random.fold_in(_gk, 2), (50000,), 0, 3125, jnp.int32)
        _d = jax.random.randint(jax.random.fold_in(_gk, 3), (50000,), 0, 3125, jnp.int32)
        _loop = jnp.arange(3125, dtype=jnp.int32)
        src = jnp.concatenate([_s, _d, _loop])
        dst = jnp.concatenate([_d, _s, _loop])
        _o = jnp.argsort(dst, stable=True)
        src = src[_o]
        dst = dst[_o]
        edge_type_500 = jax.random.randint(jax.random.fold_in(_gk, 12), (103125,), 0, 500, jnp.int32)
        return (x, src, dst, edge_type_500)
    x, src, dst, edge_type_500 = _rec_inputs()

    def _L0_gnn_setup():
        import jax, jax.numpy as jnp
        import numpy as np
        N, E, D, L = (3125, 100000, 256, 3)
        EPS = 1e-05
        key = jax.random.key(seed)
        ks = jax.random.split(key, 10)
        x = jax.random.normal(ks[0], (N, D), dtype=jnp.float32)
        edge_index = jax.random.randint(ks[1], (2, E), 0, N, dtype=jnp.int32)
        mask_embed = jax.random.normal(ks[2], (D,), dtype=jnp.float32)
        s = 1.0 / np.sqrt(D)
        Wl = jax.random.normal(ks[3], (L, D, D), dtype=jnp.float32) * s
        Wr = jax.random.normal(ks[4], (L, D, D), dtype=jnp.float32) * s
        b = jax.random.normal(ks[5], (L, D), dtype=jnp.float32) * 0.01
        gamma = 1.0 + 0.1 * jax.random.normal(ks[6], (L, D), dtype=jnp.float32)
        beta = 0.1 * jax.random.normal(ks[7], (L, D), dtype=jnp.float32)
        rmean = 0.1 * jax.random.normal(ks[8], (L, D), dtype=jnp.float32)
        rvar = 0.5 + jax.random.uniform(ks[9], (L, D), dtype=jnp.float32)
        return {'x': x, 'edge_index': edge_index, 'mask_embed': mask_embed, 'Wl': Wl, 'Wr': Wr, 'b': b, 'gamma': gamma, 'beta': beta, 'rmean': rmean, 'rvar': rvar}
    _L0_gnn_all = _L0_gnn_setup()
    _L0_gnn_in = {k: v for k, v in _L0_gnn_all.items() if k in ('mask_embed', 'Wl', 'Wr', 'b', 'gamma', 'beta', 'rmean', 'rvar')}
    del _L0_gnn_all

    def _L0_ffn_setup():
        import jax, jax.numpy as jnp
        import numpy as np
        B, S, H, F, E, K = (8, 256, 256, 512, 16, 2)
        EPS = 1e-05
        key = jax.random.key(seed)
        ks = jax.random.split(key, 9)
        sc = 0.02
        return {'x': jax.random.normal(ks[0], (B, S, H), dtype=jnp.float32), 'gate_w': jax.random.normal(ks[1], (H, E), dtype=jnp.float32) * sc, 'gate_b': jnp.zeros((E,), dtype=jnp.float32), 'w1': jax.random.normal(ks[2], (E, H, F), dtype=jnp.float32) * sc, 'b1': jnp.zeros((E, F), dtype=jnp.float32), 'w2': jax.random.normal(ks[3], (E, F, H), dtype=jnp.float32) * sc, 'b2': jnp.zeros((E, H), dtype=jnp.float32), 'gamma': jnp.ones((H,), dtype=jnp.float32), 'beta': jnp.zeros((H,), dtype=jnp.float32)}
    _L0_ffn_all = _L0_ffn_setup()
    _L0_ffn_in = {k: v for k, v in _L0_ffn_all.items() if k in ('gate_w', 'gate_b', 'w1', 'b1', 'w2', 'b2', 'gamma', 'beta')}
    del _L0_ffn_all

    def _L1_gnn_setup():
        import jax, jax.numpy as jnp
        import numpy as np
        G = (1.0, 1.0)

        def to_hypercomplex(x, n_blades):
            return x.reshape(*x.shape[:-1], n_blades, -1).swapaxes(-2, -1)

        def clifford_kernel_2d(w, g):
            g0, g1 = g
            k0 = jnp.concatenate([w[0], g0 * w[1], g1 * w[2], -g0 * g1 * w[3]], axis=1)
            k1 = jnp.concatenate([w[1], w[0], -g1 * w[3], g1 * w[2]], axis=1)
            k2 = jnp.concatenate([w[2], g0 * w[3], w[0], -g0 * w[1]], axis=1)
            k3 = jnp.concatenate([w[3], w[2], w[1], w[0]], axis=1)
            return jnp.concatenate([k0, k1, k2, k3], axis=0)

        def clifford_linear(x, w, b, g=G):
            N = x.shape[0]
            k = clifford_kernel_2d(w, g)
            xf = x.swapaxes(-2, -1).reshape(N, -1)
            out = xf @ k.T + b.reshape(-1)
            C_out = w.shape[1]
            return out.reshape(N, 4, C_out).swapaxes(-2, -1)
        key = jax.random.key(seed)
        ks = jax.random.split(key, 10)
        N, E, R, emb_dim = (6250, 37500, 500, 256)
        C = emb_dim // 4
        s = 0.05
        return {'h': jax.random.normal(ks[0], (N, emb_dim), jnp.float32), 'edge_index': jax.random.randint(ks[1], (2, E), 0, N, jnp.int64), 'edge_type': jax.random.randint(ks[2], (E,), 0, R, jnp.int64), 'relation_emb': jax.random.normal(ks[3], (R, emb_dim), jnp.float32), 'msg_w': jax.random.normal(ks[4], (4, C, C), jnp.float32) * s, 'msg_b': jax.random.normal(ks[5], (4, C), jnp.float32) * s, 'upd_w': jax.random.normal(ks[6], (4, C, C), jnp.float32) * s, 'upd_b': jax.random.normal(ks[7], (4, C), jnp.float32) * s, 'gate_w': jax.random.normal(ks[8], (1, emb_dim), jnp.float32) * s, 'gate_b': jax.random.normal(ks[9], (1,), jnp.float32) * s}
    _L1_gnn_all = _L1_gnn_setup()
    _L1_gnn_in = {k: v for k, v in _L1_gnn_all.items() if k in ('relation_emb', 'msg_w', 'msg_b', 'upd_w', 'upd_b', 'gate_w', 'gate_b')}
    del _L1_gnn_all

    def _L1_ffn_setup():
        import jax, jax.numpy as jnp
        import numpy as np
        TOP_K = 2
        LN_EPS = 1e-05
        key = jax.random.key(seed)
        ks = jax.random.split(key, 8)
        B, S, D, E, H = (16, 1024, 256, 8, 1024)
        x = jax.random.normal(ks[0], (B, S, D), dtype=jnp.float32)
        Wr = jax.random.normal(ks[1], (D, E), dtype=jnp.float32) * 0.1
        br = jnp.zeros((E,), dtype=jnp.float32)
        ln_g = jnp.ones((E, D), dtype=jnp.float32)
        ln_b = jnp.zeros((E, D), dtype=jnp.float32)
        W1 = jax.random.normal(ks[2], (E, D, H), dtype=jnp.float32) * (1.0 / np.sqrt(D))
        b1 = jnp.zeros((E, H), dtype=jnp.float32)
        W2 = jax.random.normal(ks[3], (E, H, D), dtype=jnp.float32) * (1.0 / np.sqrt(H))
        b2 = jnp.zeros((E, D), dtype=jnp.float32)
        return {'x': x, 'Wr': Wr, 'br': br, 'ln_g': ln_g, 'ln_b': ln_b, 'W1': W1, 'b1': b1, 'W2': W2, 'b2': b2}
    _L1_ffn_all = _L1_ffn_setup()
    _L1_ffn_in = {k: v for k, v in _L1_ffn_all.items() if k in ('Wr', 'br', 'ln_g', 'ln_b', 'W1', 'b1', 'W2', 'b2')}
    del _L1_ffn_all
    return {'x': x, 'src': src, 'dst': dst, 'edge_type_500': edge_type_500, 'L0_gnn_mask_embed': _L0_gnn_in['mask_embed'], 'L0_gnn_Wl': _L0_gnn_in['Wl'], 'L0_gnn_Wr': _L0_gnn_in['Wr'], 'L0_gnn_b': _L0_gnn_in['b'], 'L0_gnn_gamma': _L0_gnn_in['gamma'], 'L0_gnn_beta': _L0_gnn_in['beta'], 'L0_gnn_rmean': _L0_gnn_in['rmean'], 'L0_gnn_rvar': _L0_gnn_in['rvar'], 'L0_ffn_gate_w': _L0_ffn_in['gate_w'], 'L0_ffn_gate_b': _L0_ffn_in['gate_b'], 'L0_ffn_w1': _L0_ffn_in['w1'], 'L0_ffn_b1': _L0_ffn_in['b1'], 'L0_ffn_w2': _L0_ffn_in['w2'], 'L0_ffn_b2': _L0_ffn_in['b2'], 'L0_ffn_gamma': _L0_ffn_in['gamma'], 'L0_ffn_beta': _L0_ffn_in['beta'], 'L1_gnn_relation_emb': _L1_gnn_in['relation_emb'], 'L1_gnn_msg_w': _L1_gnn_in['msg_w'], 'L1_gnn_msg_b': _L1_gnn_in['msg_b'], 'L1_gnn_upd_w': _L1_gnn_in['upd_w'], 'L1_gnn_upd_b': _L1_gnn_in['upd_b'], 'L1_gnn_gate_w': _L1_gnn_in['gate_w'], 'L1_gnn_gate_b': _L1_gnn_in['gate_b'], 'L1_ffn_Wr': _L1_ffn_in['Wr'], 'L1_ffn_br': _L1_ffn_in['br'], 'L1_ffn_ln_g': _L1_ffn_in['ln_g'], 'L1_ffn_ln_b': _L1_ffn_in['ln_b'], 'L1_ffn_W1': _L1_ffn_in['W1'], 'L1_ffn_b1': _L1_ffn_in['b1'], 'L1_ffn_W2': _L1_ffn_in['W2'], 'L1_ffn_b2': _L1_ffn_in['b2']}

def reference(x, src, dst, edge_type_500, L0_gnn_mask_embed, L0_gnn_Wl, L0_gnn_Wr, L0_gnn_b, L0_gnn_gamma, L0_gnn_beta, L0_gnn_rmean, L0_gnn_rvar, L0_ffn_gate_w, L0_ffn_gate_b, L0_ffn_w1, L0_ffn_b1, L0_ffn_w2, L0_ffn_b2, L0_ffn_gamma, L0_ffn_beta, L1_gnn_relation_emb, L1_gnn_msg_w, L1_gnn_msg_b, L1_gnn_upd_w, L1_gnn_upd_b, L1_gnn_gate_w, L1_gnn_gate_b, L1_ffn_Wr, L1_ffn_br, L1_ffn_ln_g, L1_ffn_ln_b, L1_ffn_W1, L1_ffn_b1, L1_ffn_W2, L1_ffn_b2):
    import jax
    import jax.numpy as jnp

    def _L0_gnn_ref(x, edge_index, mask_embed, Wl, Wr, b, gamma, beta, rmean, rvar):
        import jax, jax.numpy as jnp
        import numpy as np
        N, E, D, L = (3125, 100000, 256, 3)
        EPS = 1e-05
        src, dst = (edge_index[0], edge_index[1])
        h = x.at[0].set(mask_embed)
        deg = jax.ops.segment_sum(jnp.ones((src.shape[0],), h.dtype), dst, num_segments=N)
        deg = jnp.maximum(deg, 1.0)[:, None]
        for i in range(L):
            agg = jax.ops.segment_sum(h[src], dst, num_segments=N) / deg
            z = agg @ Wl[i] + b[i] + h @ Wr[i]
            z = (z - rmean[i]) * jax.lax.rsqrt(rvar[i] + EPS) * gamma[i] + beta[i]
            if i != L - 1:
                z = jax.nn.relu(z)
            z = z + h
            h = z
        return h

    def _L0_ffn_ref(x, gate_w, gate_b, w1, b1, w2, b2, gamma, beta):
        import jax, jax.numpy as jnp
        import numpy as np
        B, S, H, F, E, K = (8, 256, 256, 512, 16, 2)
        EPS = 1e-05
        gate_logits = x @ gate_w + gate_b
        topk_vals, topk_idx = jax.lax.top_k(gate_logits, K)
        topk_w = jax.nn.softmax(topk_vals, axis=-1)
        h = jax.nn.relu(jnp.einsum('bsh,ehf->bsef', x, w1) + b1)
        expert_out = jnp.einsum('bsef,efh->bseh', h, w2) + b2
        sel = jnp.take_along_axis(expert_out, topk_idx[:, :, :, None], axis=2)
        moe = jnp.sum(topk_w[..., None] * sel, axis=2)
        y = x + moe
        mu = jnp.mean(y, axis=-1, keepdims=True)
        var = jnp.var(y, axis=-1, keepdims=True)
        return (y - mu) / jnp.sqrt(var + EPS) * gamma + beta

    def _L1_gnn_ref(h, edge_index, edge_type, relation_emb, msg_w, msg_b, upd_w, upd_b, gate_w, gate_b):
        import jax, jax.numpy as jnp
        import numpy as np
        G = (1.0, 1.0)

        def to_hypercomplex(x, n_blades):
            return x.reshape(*x.shape[:-1], n_blades, -1).swapaxes(-2, -1)

        def clifford_kernel_2d(w, g):
            g0, g1 = g
            k0 = jnp.concatenate([w[0], g0 * w[1], g1 * w[2], -g0 * g1 * w[3]], axis=1)
            k1 = jnp.concatenate([w[1], w[0], -g1 * w[3], g1 * w[2]], axis=1)
            k2 = jnp.concatenate([w[2], g0 * w[3], w[0], -g0 * w[1]], axis=1)
            k3 = jnp.concatenate([w[3], w[2], w[1], w[0]], axis=1)
            return jnp.concatenate([k0, k1, k2, k3], axis=0)

        def clifford_linear(x, w, b, g=G):
            N = x.shape[0]
            k = clifford_kernel_2d(w, g)
            xf = x.swapaxes(-2, -1).reshape(N, -1)
            out = xf @ k.T + b.reshape(-1)
            C_out = w.shape[1]
            return out.reshape(N, 4, C_out).swapaxes(-2, -1)
        n_blades = 4
        num_nodes = h.shape[0]
        h_hc = to_hypercomplex(h, n_blades)
        r_hc = to_hypercomplex(relation_emb, n_blades)
        src, dst = (edge_index[0], edge_index[1])
        h_src = h_hc[src]
        r_uv = r_hc[edge_type]
        m = clifford_linear(h_src * r_uv, msg_w, msg_b)
        gate = jax.nn.sigmoid(r_uv.reshape(r_uv.shape[0], -1) @ gate_w.T + gate_b)
        m = m * gate[:, :, None]
        ones = jnp.ones_like(src, dtype=jnp.float32)
        deg_src = jax.ops.segment_sum(ones, src, num_segments=num_nodes)
        deg_dst = jax.ops.segment_sum(ones, dst, num_segments=num_nodes)
        norm = jnp.maximum(deg_src[src] * deg_dst[dst], 1.0) ** (-0.5)
        m = m * norm[:, None, None]
        h_agg = jax.ops.segment_sum(m, dst, num_segments=num_nodes)
        h_out = clifford_linear(h_hc + h_agg, upd_w, upd_b)
        return h_out.reshape(num_nodes, -1)

    def _L1_ffn_ref(x, Wr, br, ln_g, ln_b, W1, b1, W2, b2):
        import jax, jax.numpy as jnp
        import numpy as np
        TOP_K = 2
        LN_EPS = 1e-05
        B, S, D = x.shape
        N = B * S
        xt = x.reshape(N, D)
        logits = xt @ Wr + br
        probs = jax.nn.softmax(logits, axis=-1)
        top_p, top_idx = jax.lax.top_k(probs, TOP_K)
        weights = top_p / top_p.sum(axis=-1, keepdims=True)
        mu = xt.mean(axis=-1, keepdims=True)
        var = ((xt - mu) ** 2).mean(axis=-1, keepdims=True)
        xn = (xt - mu) * jax.lax.rsqrt(var + LN_EPS)
        xe = xn[None, :, :] * ln_g[:, None, :] + ln_b[:, None, :]
        h = jax.nn.gelu(jnp.einsum('end,edh->enh', xe, W1) + b1[:, None, :], approximate=False)
        y = jnp.einsum('enh,ehd->end', h, W2) + b2[:, None, :]
        y_tok = jnp.transpose(y, (1, 0, 2))
        sel = jnp.take_along_axis(y_tok, top_idx[:, :, None], axis=1)
        out = (weights[:, :, None] * sel).sum(axis=1)
        return out.reshape(B, S, D)
    edge_index = jnp.stack([src, dst])
    x = x + _L0_gnn_ref(_layernorm(x, axis=-1), edge_index, L0_gnn_mask_embed, L0_gnn_Wl, L0_gnn_Wr, L0_gnn_b, L0_gnn_gamma, L0_gnn_beta, L0_gnn_rmean, L0_gnn_rvar)
    x = x + _L0_ffn_ref(_layernorm(x, axis=-1)[None], L0_ffn_gate_w, L0_ffn_gate_b, L0_ffn_w1, L0_ffn_b1, L0_ffn_w2, L0_ffn_b2, L0_ffn_gamma, L0_ffn_beta)[0]
    x = x + _L1_gnn_ref(_layernorm(x, axis=-1), edge_index, edge_type_500, L1_gnn_relation_emb, L1_gnn_msg_w, L1_gnn_msg_b, L1_gnn_upd_w, L1_gnn_upd_b, L1_gnn_gate_w, L1_gnn_gate_b)
    x = x + _L1_ffn_ref(_layernorm(x, axis=-1)[None], L1_ffn_Wr, L1_ffn_br, L1_ffn_ln_g, L1_ffn_ln_b, L1_ffn_W1, L1_ffn_b1, L1_ffn_W2, L1_ffn_b2)[0]
    return x

_drawn_inputs = setup_inputs


def setup_inputs(seed=0):
    import zlib

    import numpy as np

    out = dict(_drawn_inputs(seed))
    spreads = {'L0_ffn_gate_b': (0.0, 0.411),
     'L0_ffn_b1': (0.0, 0.8),
     'L0_ffn_b2': (0.0, 0.415),
     'L0_ffn_gamma': (1.0, 0.2),
     'L0_ffn_beta': (0.0, 0.31),
     'L1_ffn_br': (0.0, 0.479),
     'L1_ffn_ln_g': (1.0, 0.6),
     'L1_ffn_ln_b': (0.0, 0.649),
     'L1_ffn_b1': (0.0, 0.662),
     'L1_ffn_b2': (0.0, 0.456)}
    factors = {'L0_gnn_mask_embed': 4.232,
     'L0_gnn_b': 6.605,
     'L0_ffn_w1': 3.475,
     'L0_ffn_w2': 2.798,
     'L1_gnn_relation_emb': 3.69,
     'L1_gnn_msg_w': 3.619,
     'L1_gnn_msg_b': 8.0,
     'L1_gnn_upd_b': 4.011,
     'L1_gnn_gate_w': 8.0}
    for name, (base, spread) in spreads.items():
        noise = np.random.default_rng([zlib.crc32(name.encode()), seed]).standard_normal(out[name].shape)
        drawn = base * np.exp(spread * noise) if base else spread * noise
        out[name] = jnp.asarray(drawn.astype(out[name].dtype))
    for name, factor in factors.items():
        out[name] = (out[name] * factor).astype(out[name].dtype)
    return out
```

```python
from contextlib import ExitStack, contextmanager

import numpy as np

import concourse.bass as bass
from concourse import mybir

ALU = mybir.AluOpType
ACT = mybir.ActivationFunctionType
AX = mybir.AxisListType
F32 = mybir.dt.float32
BF16 = mybir.dt.bfloat16
I32 = mybir.dt.int32
U32 = mybir.dt.uint32

P = 128
N, E, D = 3125, 103125, 256
NT = -(-N // P)
TAIL = N - (NT - 1) * P
NP = NT * P
KD = D // P
J = 5
NJ = NT // J
EPS = 1e-5

EDGE_TILES = -(-E // P)
G = 4
GE = G * P
RING = 4
GROUPS = -(-((E + NT * (GE - 1)) // GE) // RING) * RING
EDGE_ROWS = EDGE_TILES * P + GE
NOWHERE = 1 << 20
COUNT_CHUNK = 26

E0, F0, TILES0 = 16, 512, (2 * N + 16 * (P - 1)) // P
E1, F1, TILES1 = 8, 1024, (2 * N + 8 * (P - 1)) // P
TILES0 += TILES0 % 2
TILES1 += TILES1 % 2
RELATIONS = 500
RT = -(-RELATIONS // P)
W1 = 260


class Steps:

    def __init__(self, engine, sem):
        self.engine, self.sem, self.base, self.n = engine, sem, 0, 0

    def link(self, instruction):
        instruction.then_inc(self.sem, 1)
        self.n += 1
        self.engine.wait_ge(self.sem, self.base + self.n)
        return instruction

    @contextmanager
    def each(self, i, count, steps):
        start, self.base, self.n = self.base + self.n, self.base + self.n + i * steps, 0
        yield
        assert self.n == steps, (self.n, steps)
        self.base, self.n = start + count * steps, 0


class Core:

    def __init__(self, nc):
        self.nc, self.ctx, self.sems = nc, ExitStack(), []

    def __enter__(self):
        return self

    def __exit__(self, kind, *_):
        if kind is None and self.sems:
            with self.nc.Block() as block:

                @block.gpsimd
                def _(pool):
                    for sem in self.sems:
                        pool.sem_clear(sem)

        self.ctx.close()

    def sb(self, name, shape, dt=F32):
        return self.ctx.enter_context(self.nc.sbuf_tensor(name, shape, dt))

    def ps(self, name, shape, dt=F32):
        return self.ctx.enter_context(self.nc.psum_tensor(name, shape, dt))

    def sem(self, name):
        self.sems.append(self.ctx.enter_context(self.nc.semaphore(name)))
        return self.sems[-1]

    def pool_sem(self, name):
        return self.ctx.enter_context(self.nc.semaphore(name))

    def dram(self, name, shape, dt=F32):
        return self.nc.dram_tensor(name, shape, dt).ap()


def bc(ap, shape):
    return ap.to_broadcast(shape)


def constants(nc, c):
    c.ident = c.sb("ident", [P, P])
    c.ones = c.sb("ones", [P, P])
    c.before = c.sb("before", [P, P])
    c.iota_i = c.sb("iota_i", [P, GROUPS], I32)
    c.iota = c.sb("iota", [P, GROUPS])
    c.iota_b = c.sb("iota_b", [P, P], BF16)
    s_set, s_iota = c.sem("const_set"), c.sem("const_iota")
    with nc.Block() as block:

        @block.gpsimd
        def _(pool):
            pool.memset(c.ident[:, :], 0.0).then_inc(s_set, 1)
            pool.memset(c.ones[:, :], 1.0).then_inc(s_set, 1)
            pool.memset(c.before[:, :], 1.0).then_inc(s_set, 1)
            pool.iota(c.iota_i[:, :], pattern=[[1, GROUPS]], base=0, channel_multiplier=0).then_inc(s_iota, 1)
            pool.wait_ge(s_set, 3)
            pool.affine_select(out=c.ident[:, :], in_=c.ident[:, :], compare_op=ALU.not_equal, fill=1.0,
                               base=0, pattern=[[-1, P]], channel_multiplier=1)
            pool.affine_select(out=c.before[:, :], in_=c.before[:, :], compare_op=ALU.is_gt, fill=0.0,
                               base=0, pattern=[[1, P]], channel_multiplier=-1)

        @block.vector
        def _(dve):
            dve.wait_ge(s_iota, 1)
            nc.vector.tensor_copy(c.iota[:, :], c.iota_i[:, :])
            nc.vector.tensor_copy(c.iota_b[:, :], c.iota_i[:, 0:P])


def load_rows(dma, sem, dst, dram):
    full = (NT - 1) * P
    dma.dma_start(dst[:, 0:NT - 1, :], dram[0:full, :].rearrange("(t p) d -> p t d", p=P)).then_inc(sem, 16)
    dma.dma_start(dst[0:TAIL, NT - 1, :], dram[full:N, :]).then_inc(sem, 16)


def degrees(nc, c, edges):
    with Core(nc) as k:
        ed = k.sb("ed", [P, EDGE_TILES, 4], I32)
        CC, chunks = COUNT_CHUNK, EDGE_TILES // COUNT_CHUNK
        assert chunks * CC == EDGE_TILES
        hi = k.sb("hi", [P, EDGE_TILES, 2], I32)
        lo = k.sb("lo", [P, EDGE_TILES, 2], I32)
        hi_f = k.sb("hi_f", [P, EDGE_TILES, 2])
        lo_f = k.sb("lo_f", [P, EDGE_TILES, 2])
        oh_lo = [k.sb(f"oh_lo{s}", [P, CC, P], BF16) for s in range(2)]
        oh_hi = [k.sb(f"oh_hi{s}", [P, CC, NT], BF16) for s in range(2)]
        zero = k.sb("zero", [P, P], BF16)
        counts = k.sb("counts", [P, 2, NT])
        cnt = k.ps("cnt", [P, 2, 512])
        into = k.ps("into", [P, 512])
        s_edges, s_link = k.sem("deg_edges"), k.sem("deg_link")
        s_oh, s_used = k.sem("deg_onehot"), k.sem("deg_used")
        s_zero, s_counted, s_counts, s_into = (k.sem(f"deg_{x}") for x in ("zero", "counted", "counts", "into"))
        s_sqrt, s_root = k.sem("deg_sqrt"), k.sem("deg_root")
        clip = k.sb("clip", [P, 2, NT])
        root = k.sb("root", [P, 2, NT])
        per = k.sb("per", [P, 6, NT])
        per_i = k.sb("per_i", [P, 2, NT], I32)
        big = k.sb("big", [P, GROUPS, NT])
        start_f = k.sb("start_f", [P, GROUPS])
        with nc.Block() as block:

            @block.sync
            def _(sp):
                sp.dma_start(ed[:, :, :], edges[0:EDGE_TILES * P, :].rearrange("(p k) c -> p k c", p=P)).then_inc(s_edges, 16)

            @block.vector
            def _(dve):
                v, st = nc.vector, Steps(dve, s_link)
                v.memset(zero[:, :], 0.0).then_inc(s_zero, 1)
                dve.wait_ge(s_edges, 16)
                for col, field in ((0, 3), (1, 1)):
                    v.tensor_scalar(hi[:, :, col], ed[:, :, field], 7, None, ALU.arith_shift_right)
                    st.link(v.tensor_scalar(lo[:, :, col], ed[:, :, field], P - 1, None, ALU.bitwise_and))
                v.tensor_copy(hi_f[:, :, :], hi[:, :, :])
                st.link(v.tensor_copy(lo_f[:, :, :], lo[:, :, :]))
                with dve.Fori(0, chunks) as i:
                    for col in range(2):
                        dve.wait_ge(s_used, i + 1 if col == 0 else i + 1)
                        v.tensor_tensor(oh_lo[col][:, :, :], bc(c.iota_b[:, :].unsqueeze(1), [P, CC, P]),
                                        bc(lo_f[:, bass.ds(i * CC, CC), col].unsqueeze(2), [P, CC, P]), ALU.is_equal)
                        v.tensor_tensor(oh_hi[col][:, :, :], bc(c.iota_b[:, 0:NT].unsqueeze(1), [P, CC, NT]),
                                        bc(hi_f[:, bass.ds(i * CC, CC), col].unsqueeze(2), [P, CC, NT]), ALU.is_equal)\
                            .then_inc(s_oh, 1)
                dve.wait_ge(s_counted, 1)
                v.tensor_copy(counts[:, 0, :], cnt[:, 0, 0:NT])
                v.tensor_copy(counts[:, 1, :], cnt[:, 1, 0:NT]).then_inc(s_counts, 1)
                dve.wait_ge(s_counts, 1)
                st.link(v.tensor_scalar_max(clip[:, :, :], counts[:, :, :], 1.0))
                v.reciprocal(c.rdeg[:, :], clip[:, 1, :]).then_inc(s_sqrt, 1)
                dve.wait_ge(s_root, 1)
                v.reciprocal(c.norm_src[:, :], root[:, 0, :])
                v.reciprocal(c.norm_dst[:, :], root[:, 1, :])
                dve.wait_ge(s_into, 1)
                st.link(v.tensor_copy(per[:, 0, :], into[:, 0:NT]))
                group_table(v, st, per, per_i, NT, GE)
                st.link(v.tensor_tensor(big[:, :, :], bc(c.iota[:, :].unsqueeze(2), [P, GROUPS, NT]),
                                        bc(per[:, 3, :].unsqueeze(1), [P, GROUPS, NT]), ALU.is_ge))
                st.link(v.tensor_reduce(c.g_base[:, :], big[:, :, :], AX.X, ALU.add))
                st.link(v.tensor_tensor(big[:, :, :], big[:, :, :], bc(per[:, 4, :].unsqueeze(1), [P, GROUPS, NT]), ALU.mult))
                st.link(v.tensor_reduce(start_f[:, :], big[:, :, :], AX.X, ALU.add))
                st.link(v.scalar_tensor_tensor(start_f[:, :], c.iota[:, :], float(GE), start_f[:, :], ALU.mult, ALU.add))
                st.link(v.tensor_scalar_min(start_f[:, :], start_f[:, :], float(EDGE_TILES * P)))
                v.tensor_copy(c.g_start[:, :], start_f[0:1, :])
                st.link(v.tensor_copy(c.g_tile[:, :], c.g_base[0:1, :]))
                v.tensor_scalar_mul(c.g_base[:, :], c.g_base[:, :], float(P))

            @block.scalar
            def _(act):
                act.wait_ge(s_sqrt, 1)
                nc.scalar.activation(root[:, :, :], clip[:, :, :], ACT.Sqrt).then_inc(s_root, 1)

            @block.tensor
            def _(pe):
                pe.wait_ge(s_zero, 1)
                for col in range(2):
                    nc.tensor.matmul(cnt[:, col, 0:NT], zero[:, :], zero[:, 0:NT], start=True, stop=False)
                pe.sem_inc(s_used, 1)
                with pe.Fori(0, chunks) as i:
                    for col in range(2):
                        pe.wait_ge(s_oh, 2 * i + col + 1)
                        for t in range(CC):
                            last = nc.tensor.matmul(cnt[:, col, 0:NT], oh_lo[col][:, t, :], oh_hi[col][:, t, :],
                                                    start=False, stop=False)
                    last.then_inc(s_used, 1)
                for col in range(2):
                    last = nc.tensor.matmul(cnt[:, col, 0:NT], zero[:, :], zero[:, 0:NT], start=False, stop=True)
                last.then_inc(s_counted, 1)
                pe.wait_ge(s_counts, 1)
                nc.tensor.matmul(into[:, 0:NT], c.ones[:, :], counts[:, 1, :], start=True, stop=True).then_inc(s_into, 1)


def group_table(v, st, per, per_i, n, size):
    st.link(v.tensor_scalar_add(per[:, 1, 0:n], per[:, 0, 0:n], float(size - 1)))
    st.link(v.tensor_copy(per_i[:, 0, 0:n], per[:, 1, 0:n]))
    bits = size.bit_length() - 1
    st.link(v.tensor_scalar(per_i[:, 1, 0:n], per_i[:, 0, 0:n], bits, bits, ALU.arith_shift_right, ALU.logical_shift_left))
    st.link(v.tensor_copy(per[:, 1, 0:n], per_i[:, 1, 0:n]))
    st.link(v.tensor_tensor(per[:, 4, 0:n], per[:, 0, 0:n], per[:, 1, 0:n], ALU.subtract))
    st.link(v.tensor_scalar_mul(per[:, 1, 0:n], per[:, 1, 0:n], 1.0 / size))
    st.link(v.memset(per[:, 2, 0:n], 0.0))
    st.link(v.tensor_tensor_scan(per[:, 3, 0:n], per[:, 1, 0:n], per[:, 2, 0:n], 0.0, ALU.add, ALU.add))
    st.link(v.tensor_tensor(per[:, 5, 0:n], per[:, 3, 0:n], per[:, 1, 0:n], ALU.subtract))
    st.link(v.tensor_scalar_mul(per[:, 5, 0:n], per[:, 5, 0:n], float(size)))


def layernorm(nc, c, name, src, dst, after=None):
    with Core(nc) as k:
        stats = k.sb(f"{name}_stats", [P, NT, 6])
        mean = k.sb(f"{name}_mean", [P, NT])
        var = k.sb(f"{name}_var", [P, NT])
        tmp = k.sb(f"{name}_tmp", [P, NT])
        s_link, s_var, s_root, s_done, s_store = (k.sem(f"{name}_{x}") for x in ("link", "var", "root", "done", "store"))
        with nc.Block() as block:

            @block.vector
            def _(dve):
                v, st = nc.vector, Steps(dve, s_link)
                with dve.Fori(0, NT) as t:
                    last = v.bn_stats(stats[:, bass.ds(t, 1), :].rearrange("p a s -> p (a s)"),
                                      src[:, bass.ds(t, 1), :].rearrange("p a d -> p (a d)"))
                v.drain().then_inc(s_done, 1)
                dve.wait_ge(s_done, 1)
                v.tensor_tensor(mean[:, :], stats[:, :, 1], stats[:, :, 4], ALU.add)
                v.tensor_tensor(tmp[:, :], stats[:, :, 1], stats[:, :, 4], ALU.subtract)
                st.link(v.tensor_tensor(var[:, :], stats[:, :, 2], stats[:, :, 5], ALU.add))
                v.tensor_scalar_mul(mean[:, :], mean[:, :], 0.5)
                st.link(v.tensor_tensor(tmp[:, :], tmp[:, :], tmp[:, :], ALU.mult))
                st.link(v.tensor_scalar(var[:, :], var[:, :], 1.0 / D, EPS, ALU.mult, ALU.add))
                v.scalar_tensor_tensor(var[:, :], tmp[:, :], 0.25, var[:, :], ALU.mult, ALU.add).then_inc(s_var, 1)
                dve.wait_ge(s_root, 1)
                st.link(v.reciprocal(var[:, :], tmp[:, :]))
                with dve.Fori(0, NT) as t:
                    v.tensor_scalar(dst[:, bass.ds(t, 1), 0:D].rearrange("p a d -> p (a d)"),
                                    src[:, bass.ds(t, 1), :].rearrange("p a d -> p (a d)"),
                                    mean[:, bass.ds(t, 1)], var[:, bass.ds(t, 1)], ALU.subtract, ALU.mult)
                if after:
                    v.drain().then_inc(s_done, 1)

            @block.scalar
            def _(act):
                act.wait_ge(s_var, 1)
                nc.scalar.activation(tmp[:, :], var[:, :], ACT.Sqrt).then_inc(s_root, 1)

            if after:

                @block.sync
                def _(sp):
                    sp.wait_ge(s_done, 2)
                    after(sp, s_store)


def aggregate(nc, c, name, edges, table, width, acc, relations=None):
    used = width if relations is None else D + 1
    with Core(nc) as k:
        ed = k.sb(f"{name}_ed", [P, RING, G, 4], I32)
        dst_f = k.sb(f"{name}_dst_f", [P, RING, G])
        rows = k.sb(f"{name}_rows", [P, RING, G, width])
        rel = k.sb(f"{name}_rel", [P, RING, G, width]) if relations is not None else None
        onehot = k.sb(f"{name}_onehot", [P, RING, G, P])
        sums = k.ps(f"{name}_sums", [P, 2, 512])
        s_edges = [k.sem(f"{name}_edges{s}") for s in range(RING)]
        s_rows = [c.pool_sem(f"{name}_rows{s}") for s in range(RING)]
        s_link, s_ready, s_sum, s_acc, s_gate = (k.sem(f"{name}_{x}") for x in ("link", "ready", "sum", "acc", "gate"))
        tables = [(table, rows)] + ([(relations, rel)] if relations is not None else [])
        with nc.Block() as block:

            @block.sync
            def _(sp):
                with sp.Fori(0, GROUPS // RING) as i:
                    for s in range(RING):
                        start = sp.value_load(c.g_start[0:1, bass.ds(i * RING + s, 1)], min_val=0, max_val=EDGE_TILES * P)
                        src = edges[bass.ds(start, GE), :].rearrange("(p k) c -> p k c", p=P)
                        sp.wait_ge(s_sum, i * RING + s + 1)
                        sp.dma_start(ed[:, s, :, :], src).then_inc(s_edges[s], 16)

            @block.gpsimd
            def _(pool):
                with pool.Fori(0, GROUPS // RING) as i:
                    for s in range(RING):
                        pool.wait_ge(s_edges[s], i * 16 + 16)
                        pool.sem_inc(s_gate, 1)
                        for g in range(G):
                            for field, (tab, out) in zip((0, 2), tables):
                                pool.indirect_dma_start(out[:, s, g, :], None, tab,
                                                        bass.IndirectOffsetOnAxis(ap=ed[:, s, g, field:field + 1], axis=0))\
                                    .then_inc(s_rows[s], 16)

            landed = 16 * G * len(tables)

            @block.vector
            def _(dve):
                v, st = nc.vector, Steps(dve, s_link)
                v.memset(acc[:, :, :], 0.0).then_inc(s_acc, 1)
                with dve.Fori(0, GROUPS // RING) as i, st.each(i, GROUPS // RING, 2 * RING):
                    for s in range(RING):
                        g = i * RING + s
                        tile = dve.value_load(c.g_tile[0:1, bass.ds(g, 1)], min_val=0, max_val=NT)
                        dve.wait_ge(s_edges[s], i * 16 + 16)
                        st.link(v.tensor_copy(dst_f[:, s, :], ed[:, s, :, 1]))
                        st.link(v.tensor_scalar(dst_f[:, s, :], dst_f[:, s, :], c.g_base[:, bass.ds(g, 1)], None, ALU.subtract))
                        for t in range(G):
                            last = v.tensor_scalar(onehot[:, s, t, :], c.iota[:, 0:P], dst_f[:, s, t:t + 1], None, ALU.is_equal)
                        if rel is not None:
                            dve.wait_ge(s_rows[s], i * landed + landed)
                            last = v.tensor_tensor(rows[:, s, :, 0:used], rows[:, s, :, 0:used], rel[:, s, :, 0:used], ALU.mult)
                        last.then_inc(s_ready, 1)
                        dve.wait_ge(s_acc, g + 1)
                        dve.wait_ge(s_sum, g + RING + 1)
                        here = acc[:, bass.ds(tile, 1), 0:used].rearrange("p a d -> p (a d)")
                        v.tensor_tensor(here, here, sums[:, s % 2, 0:used], ALU.add).then_inc(s_acc, 1)

            @block.tensor
            def _(pe):
                pe.sem_inc(s_sum, RING)
                with pe.Fori(0, GROUPS // RING) as i:
                    for s in range(RING):
                        pe.wait_ge(s_rows[s], i * landed + landed)
                        pe.wait_ge(s_ready, i * RING + s + 1)
                        for t in range(G):
                            last = nc.tensor.matmul(sums[:, s % 2, 0:used], onehot[:, s, t, :], rows[:, s, t, 0:used],
                                                    start=t == 0, stop=t == G - 1)
                        last.then_inc(s_sum, 1)


def dense(nc, c, name, sources, M, finish, steps, after=None):
    with Core(nc) as k:
        n = len(sources)
        own = [k.sb(f"{name}_own{q}", [P, J, D]) for q in range(n)]
        turned = [k.sb(f"{name}_turned{q}", [P, J, KD, P]) for q in range(n)]
        bank = [k.ps(f"{name}_bank{q}", [P, 3 * 512]) for q in range(n)]
        s_own, s_t, s_turned, s_z, s_free, s_link, s_store = (
            k.sem(f"{name}_{x}") for x in ("own", "t", "turned", "z", "free", "link", "store"))
        with nc.Block() as block:

            @block.scalar
            def _(act):
                with act.Fori(0, NJ) as i:
                    for q, (rows, _, factor) in enumerate(sources):
                        act.wait_ge(s_t, i * n + q + 1)
                        for j in range(J):
                            at = bass.ds(i * J + j, 1)
                            last = nc.scalar.activation(own[q][:, j, :], rows[:, at, 0:D].rearrange("p a d -> p (a d)"), ACT.Copy,
                                                        scale=1.0 if factor is None else factor[:, at])
                        last.then_inc(s_own, 1)

            @block.tensor
            def _(pe):
                pe.sem_inc(s_t, n)
                with pe.Fori(0, NJ) as i:
                    pe.wait_ge(s_free, i + 1)
                    for q in range(n):
                        pe.wait_ge(s_own, i * n + q + 1)
                        for j in range(J):
                            for h in range(KD):
                                at = (j * KD + h) * P
                                last = nc.tensor.transpose(bank[q][:, at:at + P], own[q][:, j, h * P:(h + 1) * P], c.ident[:, :])
                        last.then_inc(s_t, 1)
                    pe.wait_ge(s_turned, i + 1)
                    for j in range(J):
                        for q, (_, weight, _) in enumerate(sources):
                            for h in range(KD):
                                last = nc.tensor.matmul(bank[0][:, j * D:j * D + M], turned[q][:, j, h, :], weight[:, h, :],
                                                        start=q == 0 and h == 0, stop=q == n - 1 and h == KD - 1)
                    last.then_inc(s_z, 1)

            @block.vector
            def _(dve):
                v, st = nc.vector, Steps(dve, s_link)
                dve.sem_inc(s_free, 1)
                with dve.Fori(0, NJ) as i, st.each(i, NJ, steps):
                    for q in range(n):
                        dve.wait_ge(s_t, i * n + q + 1 + n)
                        last = v.tensor_copy(turned[q][:, :, :, :].rearrange("p j h c -> p (j h c)"), bank[q][:, 0:J * D])
                    last.then_inc(s_turned, 1)
                    dve.wait_ge(s_z, i + 1)
                    z = bank[0][:, 0:J * D].rearrange("p (j d) -> p j d", d=D)[:, :, 0:M]
                    finish(v, st, i * J, z).then_inc(s_free, 1)
                if after:
                    dve.wait_ge(s_free, NJ + 1)

            if after:

                @block.sync
                def _(sp):
                    sp.wait_ge(s_free, NJ + 1)
                    after(sp, s_store)


def load_all(nc, name, loads):
    with Core(nc) as k:
        s = k.sem(f"{name}_loads")
        with nc.Block() as block:

            @block.sync
            def _(sp):
                for out, src in loads:
                    sp.dma_start(out, src, allow_slow_non_contiguous=True).then_inc(s, 16)
                sp.wait_ge(s, 16 * len(loads))


def row(ap):
    return ap.rearrange("(a n) -> a n", a=1).to_broadcast([P, ap.shape[0]])


def gnn0(nc, c, I, edges):
    h_table = c.dram("h_table", [NP, D])
    with Core(nc) as k:
        h = k.sb("h", [P, NT, D])
        s_fix = k.sem("mask_row")

        def store(sp, s_store, n=0):
            sp.dma_start(h_table.rearrange("(t p) d -> p t d", p=P), h[:, :, :]).then_inc(s_store, 16)
            sp.wait_ge(s_store, 16)

        def first(sp, s_store):
            sp.dma_start(h[0:1, 0, :], I["L0_gnn_mask_embed"].rearrange("(a n) -> a n", a=1)).then_inc(s_fix, 16)
            sp.wait_ge(s_fix, 16)
            store(sp, s_store)

        layernorm(nc, c, "ln0", c.x, h, first)
        acc = k.sb("acc", [P, NT + 1, D])
        wl, wr = k.sb("wl", [P, KD, D]), k.sb("wr", [P, KD, D])
        vecs = k.sb("vecs", [P, 5, D])
        mul, add = k.sb("bn_mul", [P, D]), k.sb("bn_add", [P, D])
        z1 = k.sb("z1", [P, J, D])
        for layer in range(3):
            aggregate(nc, c, f"agg{layer}", edges, h_table, D, acc)
            load_all(nc, f"gw{layer}", [
                (wl[:, :, :], I["L0_gnn_Wl"][layer].rearrange("(k p) n -> p k n", p=P)),
                (wr[:, :, :], I["L0_gnn_Wr"][layer].rearrange("(k p) n -> p k n", p=P)),
                *[(vecs[:, q, :], row(I[f"L0_gnn_{v}"][layer])) for q, v in enumerate(("b", "gamma", "beta", "rmean", "rvar"))]])
            with Core(nc) as inner:
                s_link, s_var, s_root = (inner.sem(f"bn{layer}_{x}") for x in ("link", "var", "root"))
                with nc.Block() as block:

                    @block.vector
                    def _(dve):
                        v, st = nc.vector, Steps(dve, s_link)
                        v.tensor_scalar_add(vecs[:, 4, :], vecs[:, 4, :], EPS).then_inc(s_var, 1)
                        dve.wait_ge(s_root, 1)
                        st.link(v.reciprocal(mul[:, :], add[:, :]))
                        st.link(v.tensor_tensor(mul[:, :], mul[:, :], vecs[:, 1, :], ALU.mult))
                        st.link(v.tensor_tensor(add[:, :], vecs[:, 0, :], vecs[:, 3, :], ALU.subtract))
                        st.link(v.tensor_tensor(add[:, :], add[:, :], mul[:, :], ALU.mult))
                        v.tensor_tensor(add[:, :], add[:, :], vecs[:, 2, :], ALU.add)

                    @block.scalar
                    def _(act):
                        act.wait_ge(s_var, 1)
                        nc.scalar.activation(add[:, :], vecs[:, 4, :], ACT.Sqrt).then_inc(s_root, 1)

            def finish(v, st, t0, z, layer=layer):
                wide = [P, J, D]
                st.link(v.tensor_tensor(z1[:, :, :], z, bc(mul[:, :].unsqueeze(1), wide), ALU.mult))
                st.link(v.tensor_tensor(z1[:, :, :], z1[:, :, :], bc(add[:, :].unsqueeze(1), wide), ALU.add))
                now = h[:, bass.ds(t0, J), :].rearrange("p j d -> p (j d)")
                flat = z1[:, :, :].rearrange("p j d -> p (j d)")
                if layer < 2:
                    return v.scalar_tensor_tensor(now, flat, 0.0, now, ALU.max, ALU.add)
                out = c.x[:, bass.ds(t0, J), :].rearrange("p j d -> p (j d)")
                st.link(v.tensor_tensor(flat, flat, now, ALU.add))
                return v.tensor_tensor(out, out, flat, ALU.add)

            dense(nc, c, f"upd{layer}", [(acc, wl, c.rdeg), (h, wr, None)], D, finish, 2 if layer < 2 else 3,
                  store if layer < 2 else None)


def experts(nc, c, I, name, ne, nf, tiles, which, w1, b1, w2, b2, gate_w, gate_b, norm, act_fn, finish_rows):
    FC = nf // P
    xs = c.dram(f"{name}_xs", [(tiles + 1) * P, D])
    ys = c.dram(f"{name}_ys", [tiles * P, D])
    with Core(nc) as k:
        xn = k.sb(f"{name}_xn", [P, NT, D])
        layernorm(nc, c, f"{name}_ln", c.x, xn)
        gate = k.sb(f"{name}_gate", [P, KD, ne])
        gate_bias = k.sb(f"{name}_gate_bias", [P, ne])
        logits = k.sb(f"{name}_logits", [P, NT, ne])
        load_all(nc, f"{name}_g", [(gate[:, :, :], gate_w.rearrange("(k p) n -> p k n", p=P)),
                                   (gate_bias[:, :], row(gate_b))])

        def keep(v, st, t0, z):
            return v.tensor_tensor(logits[:, bass.ds(t0, J), :], z, bc(gate_bias[:, :].unsqueeze(1), [P, J, ne]), ALU.add)

        dense(nc, c, f"{name}_gd", [(xn, gate, None)], ne, keep, 0)
        weight = k.sb(f"{name}_weight", [P, 2, NT])
        slot = k.sb(f"{name}_slot", [P, 2, NT], I32)
        e_tab = k.sb(f"{name}_etab", [1, tiles], I32)
        route(nc, c, name, ne, tiles, which, logits, weight, slot, e_tab, xn, xs)
        run_experts(nc, c, name, ne, nf, FC, tiles, xs, ys, e_tab, w1, b1, w2, b2, norm, act_fn)
        combine(nc, c, name, ys, weight, slot, c.x if norm else xn, xn, finish_rows)


def route(nc, c, name, ne, tiles, softmax_first, logits, weight, slot, e_tab, xn, xs):
    with Core(nc) as k:
        top = k.sb(f"{name}_top", [P, NT, 8])
        idx = k.sb(f"{name}_idx", [P, NT, 8], U32)
        idx_f = k.sb(f"{name}_idx_f", [P, 2, NT])
        pick = k.sb(f"{name}_pick", [P, 2, NT, ne])
        both = k.sb(f"{name}_both", [P, NT, ne])
        place = k.sb(f"{name}_place", [P, NT, ne])
        sums = k.sb(f"{name}_sums", [P, NT + 1, ne])
        small = k.sb(f"{name}_small", [P, 4, NT])
        per = k.sb(f"{name}_per", [P, 6, ne])
        per_i = k.sb(f"{name}_per_i", [P, 2, ne], I32)
        done = k.sb(f"{name}_done", [1, tiles, ne])
        done_f = k.sb(f"{name}_done_f", [1, tiles])
        slot_f = k.sb(f"{name}_slot_f", [P, 2, NT])
        zero = k.sb(f"{name}_zero", [P, 2048])
        rank = k.ps(f"{name}_rank", [P, 512])
        total = k.ps(f"{name}_total", [P, 512])
        s_link, s_a, s_b, s_m, s_rank, s_slot, s_z, s_zd = (
            k.sem(f"{name}_r{x}") for x in ("link", "to_act", "to_dve", "both", "rank", "slot", "zero", "zeroed"))
        s_sc = c.pool_sem(f"{name}_scatter")
        wide = [P, NT, ne]
        rows_total = (tiles + 1) * P * D
        with nc.Block() as block:

            @block.vector
            def _(dve):
                v, st = nc.vector, Steps(dve, s_link)
                v.memset(zero[:, :], 0.0).then_inc(s_z, 1)
                if softmax_first:
                    st.link(v.tensor_reduce(small[:, 0, :], logits[:, :, :], AX.X, ALU.max))
                    v.tensor_tensor(logits[:, :, :], logits[:, :, :], bc(small[:, 0, :].unsqueeze(2), wide), ALU.subtract)\
                        .then_inc(s_a, 1)
                    dve.wait_ge(s_b, 1)
                    st.link(v.tensor_reduce(small[:, 1, :], logits[:, :, :], AX.X, ALU.add))
                    st.link(v.reciprocal(small[:, 2, :], small[:, 1, :]))
                    st.link(v.tensor_tensor(logits[:, :, :], logits[:, :, :], bc(small[:, 2, :].unsqueeze(2), wide), ALU.mult))
                for t in range(NT):
                    last = v.max(top[:, t, :], logits[:, t, :])
                st.link(last)
                for t in range(NT):
                    last = v.max_index(idx[:, t, :], top[:, t, :], logits[:, t, :])
                st.link(last)
                if softmax_first:
                    st.link(v.tensor_tensor(small[:, 0, :], top[:, :, 0], top[:, :, 1], ALU.add))
                    st.link(v.reciprocal(small[:, 1, :], small[:, 0, :]))
                    for q in range(2):
                        v.tensor_tensor(weight[:, q, :], top[:, :, q], small[:, 1, :], ALU.mult)
                else:
                    v.tensor_tensor(small[:, 0, :], top[:, :, 1], top[:, :, 0], ALU.subtract).then_inc(s_a, 1)
                    dve.wait_ge(s_b, 1)
                    st.link(v.tensor_scalar_add(small[:, 2, :], small[:, 1, :], 1.0))
                    st.link(v.reciprocal(weight[:, 0, :], small[:, 2, :]))
                    v.tensor_tensor(weight[:, 1, :], weight[:, 0, :], small[:, 1, :], ALU.mult)
                for q in range(2):
                    last = v.tensor_copy(idx_f[:, q, :], idx[:, :, q])
                st.link(last)
                for q in range(2):
                    last = v.tensor_tensor(pick[:, q, :, :], bc(c.iota[:, 0:ne].unsqueeze(1), wide),
                                           bc(idx_f[:, q, :].unsqueeze(2), wide), ALU.is_equal)
                st.link(last)
                st.link(v.tensor_tensor(both[:, :, :], pick[:, 0, :, :], pick[:, 1, :, :], ALU.add))
                v.tensor_scalar(both[:, NT - 1, :], both[:, NT - 1, :], c.alive[:, 0:1], None, ALU.mult).then_inc(s_m, 1)
                dve.wait_ge(s_rank, 1)
                st.link(v.memset(sums[:, 0, :], 0.0))
                for t in range(NT):
                    st.link(v.tensor_tensor(sums[:, t + 1, :], sums[:, t, :], total[:, t * ne:(t + 1) * ne], ALU.add))
                st.link(v.tensor_copy(per[:, 0, :], sums[:, NT, :]))
                group_table(v, st, per, per_i, ne, P)
                st.link(v.tensor_tensor(place[:, :, :], rank[:, 0:NT * ne].rearrange("p (t e) -> p t e", e=ne), sums[:, 0:NT, :], ALU.add))
                st.link(v.tensor_tensor(place[:, :, :], place[:, :, :], bc(per[:, 5, :].unsqueeze(1), wide), ALU.add))
                for q in range(2):
                    last = v.tensor_tensor(pick[:, q, :, :], pick[:, q, :, :], place[:, :, :], ALU.mult)
                st.link(last)
                st.link(v.tensor_reduce(slot_f[:, :, :], pick[:, :, :, :], AX.X, ALU.add))
                v.tensor_copy(slot[:, :, :], slot_f[:, :, :]).then_inc(s_slot, 1)
                st.link(v.tensor_tensor(done[:, :, :], bc(c.iota[0:1, 0:tiles].unsqueeze(2), [1, tiles, ne]),
                                        bc(per[0:1, 3, :].unsqueeze(1), [1, tiles, ne]), ALU.is_ge))
                st.link(v.tensor_reduce(done_f[:, :], done[:, :, :], AX.X, ALU.add))
                st.link(v.tensor_scalar_min(done_f[:, :], done_f[:, :], float(ne - 1)))
                v.tensor_copy(e_tab[:, :], done_f[:, :])

            @block.scalar
            def _(act):
                act.wait_ge(s_a, 1)
                if softmax_first:
                    nc.scalar.activation(logits[:, :, :], logits[:, :, :], ACT.Exp).then_inc(s_b, 1)
                else:
                    nc.scalar.activation(small[:, 1, :], small[:, 0, :], ACT.Exp).then_inc(s_b, 1)

            @block.tensor
            def _(pe):
                pe.wait_ge(s_m, 1)
                flat = both[:, :, :].rearrange("p t e -> p (t e)")
                nc.tensor.matmul(rank[:, 0:NT * ne], c.before[:, :], flat, start=True, stop=True)
                nc.tensor.matmul(total[:, 0:NT * ne], c.ones[:, :], flat, start=True, stop=True).then_inc(s_rank, 1)

            @block.sync
            def _(sp):
                sp.wait_ge(s_z, 1)
                view = xs.rearrange("(p a) d -> p (a d)", p=P)
                n, at = rows_total // P, 0
                for at in range(0, n, 2048):
                    w = min(2048, n - at)
                    sp.dma_start(view[:, at:at + w], zero[:, 0:w]).then_inc(s_zd, 16)

            @block.gpsimd
            def _(pool):
                pool.wait_ge(s_zd, 16 * -(-(rows_total // P) // 2048))
                pool.wait_ge(s_slot, 1)
                for t in range(NT):
                    n = P if t < NT - 1 else TAIL
                    for q in range(2):
                        pool.indirect_dma_start(xs, bass.IndirectOffsetOnAxis(ap=slot[0:n, q, t:t + 1], axis=0),
                                                xn[0:n, t, :], None).then_inc(s_sc, 16)
                pool.wait_ge(s_sc, 16 * 2 * NT)


def run_experts(nc, c, name, ne, nf, FC, tiles, xs, ys, e_tab, w1, b1, w2, b2, norm, act_fn):
    with Core(nc) as k:
        w1b = k.sb(f"{name}_w1", [P, 2, KD, nf])
        w2b = k.sb(f"{name}_w2", [P, 2, FC, D])
        xb = k.sb(f"{name}_xb", [P, 2, D])
        xT = k.sb(f"{name}_xT", [P, 2, KD, P])
        hT = k.sb(f"{name}_hT", [P, 2, FC, P])
        yb = k.sb(f"{name}_yb", [P, 2, D])
        b1s = k.sb(f"{name}_b1", [P, ne, FC])
        b2s = k.sb(f"{name}_b2", [P, ne, D])
        pX = [k.ps(f"{name}_pX{s}", [P, 512]) for s in range(2)]
        pH = [k.ps(f"{name}_pH{s}", [P, max(nf, 512)]) for s in range(2)]
        pY = [k.ps(f"{name}_pY{s}", [P, 512]) for s in range(2)]
        loads = [(b1s[:, :, :], b1), (b2s[:, :, :], b2.rearrange("(a e) d -> a e d", a=1).to_broadcast([P, ne, D]))]
        if norm:
            lg, lb = k.sb(f"{name}_lg", [P, ne, KD]), k.sb(f"{name}_lb", [P, ne, KD])
            loads += [(lg[:, :, :], norm[0]), (lb[:, :, :], norm[1])]
        load_all(nc, f"{name}_b", loads)
        s_w1 = [k.sem(f"{name}_w1_{s}") for s in range(2)]
        s_w2 = [k.sem(f"{name}_w2_{s}") for s in range(2)]
        s_x = [k.sem(f"{name}_x{s}") for s in range(2)]
        s_st = [c.pool_sem(f"{name}_st{s}") for s in range(2)]
        s_xt, s_xT, s_h, s_hT, s_y, s_yb, s_yfree, s_gate = (
            k.sem(f"{name}_e{x}") for x in ("xt", "xT", "h", "hT", "y", "yb", "yfree", "gate"))
        BF = 512 // P
        HB = FC // BF
        with nc.Block() as block:

            @block.sync
            def _(sp):
                sp.dma_start(xb[:, 0, :], xs[0:P, :]).then_inc(s_x[0], 16)
                with sp.Fori(0, tiles // 2) as i:
                    for s in range(2):
                        t = 2 * i + s
                        e = sp.value_load(e_tab[0:1, bass.ds(t, 1)], min_val=0, max_val=ne - 1)
                        a1 = w1[bass.ds(e, 1), :, :].rearrange("a (k p) f -> p (a k) f", p=P)
                        a2 = w2[bass.ds(e, 1), :, :].rearrange("a (k p) f -> p (a k) f", p=P)
                        ax = xs[bass.ds(t * P + P, P), :]
                        sp.wait_ge(s_h, t * HB + HB)
                        sp.dma_start(w1b[:, s, :, :], a1).then_inc(s_w1[s], 16)
                        sp.wait_ge(s_xt, t + 1)
                        sp.dma_start(xb[:, 1 - s, :], ax).then_inc(s_x[1 - s], 16)
                        sp.wait_ge(s_y, t + 1)
                        sp.dma_start(w2b[:, s, :, :], a2).then_inc(s_w2[s], 16)

            @block.tensor
            def _(pe):
                def turn(t, s, u):
                    pe.wait_ge(s_x[s], u * 16)
                    for h in range(KD):
                        last = nc.tensor.transpose(pX[s][:, h * P:(h + 1) * P], xb[:, s, h * P:(h + 1) * P], c.ident[:, :])
                    last.then_inc(s_xt, 1)

                def hidden(t, s, u):
                    pe.wait_ge(s_w1[s], u * 16)
                    pe.wait_ge(s_xT, t + 1)
                    for f in range(FC):
                        for h in range(KD):
                            last = nc.tensor.matmul(pH[s][:, f * P:(f + 1) * P], w1b[:, s, h, f * P:(f + 1) * P],
                                                    xT[:, s, h, :], start=h == 0, stop=h == KD - 1)
                        if f % BF == BF - 1:
                            last.then_inc(s_h, 1)

                def result(t, s, u):
                    pe.wait_ge(s_w2[s], u * 16)
                    pe.wait_ge(s_yb, t + 1)
                    for f in range(FC):
                        pe.wait_ge(s_hT, t * FC + f + 1)
                        last = nc.tensor.matmul(pY[s][:, 0:D], hT[:, s, f, :], w2b[:, s, f, :], start=f == 0, stop=f == FC - 1)
                    last.then_inc(s_y, 1)

                pe.sem_inc(s_xt, 1)
                pe.sem_inc(s_h, 2 * HB)
                pe.sem_inc(s_y, 2)
                turn(0, 0, 1)
                hidden(0, 0, 1)
                turn(1, 1, 1)
                with pe.Fori(0, tiles // 2 - 1) as i:
                    t = 2 * i
                    hidden(t + 1, 1, i + 1)
                    turn(t + 2, 0, i + 2)
                    result(t, 0, i + 1)
                    hidden(t + 2, 0, i + 2)
                    turn(t + 3, 1, i + 2)
                    result(t + 1, 1, i + 1)
                hidden(tiles - 1, 1, tiles // 2)
                turn(tiles, 0, tiles // 2 + 1)
                result(tiles - 2, 0, tiles // 2)
                result(tiles - 1, 1, tiles // 2)

            @block.scalar
            def _(act):
                with act.Fori(0, tiles // 2) as i:
                    for s in range(2):
                        t = 2 * i + s
                        e = act.value_load(e_tab[0:1, bass.ds(t, 1)], min_val=0, max_val=ne - 1)
                        act.wait_ge(s_xt, t + 2)
                        for h in range(KD):
                            src = pX[s][:, h * P:(h + 1) * P]
                            if norm:
                                last = nc.scalar.activation(xT[:, s, h, :], src, ACT.Identity, bias=lb[:, bass.ds(e, 1), h],
                                                            scale=lg[:, bass.ds(e, 1), h])
                            else:
                                last = nc.scalar.activation(xT[:, s, h, :], src, ACT.Copy)
                        last.then_inc(s_xT, 1)
                        for f in range(FC):
                            if f % BF == 0:
                                act.wait_ge(s_h, t * HB + f // BF + 1 + 2 * HB)
                            nc.scalar.activation(hT[:, s, f, :], pH[s][:, f * P:(f + 1) * P], act_fn,
                                                 bias=b1s[:, bass.ds(e, 1), f]).then_inc(s_hT, 1)

            @block.vector
            def _(dve):
                dve.sem_inc(s_yb, 2)
                with dve.Fori(0, tiles // 2) as i:
                    for s in range(2):
                        t = 2 * i + s
                        e = dve.value_load(e_tab[0:1, bass.ds(t, 1)], min_val=0, max_val=ne - 1)
                        dve.wait_ge(s_y, t + 3)
                        dve.wait_ge(s_yfree, t + 1)
                        nc.vector.tensor_tensor(yb[:, s, :], pY[s][:, 0:D], b2s[:, bass.ds(e, 1), :].rearrange("p a d -> p (a d)"), ALU.add)\
                            .then_inc(s_yb, 1)

            @block.gpsimd
            def _(pool):
                pool.sem_inc(s_yfree, 2)
                with pool.Fori(0, tiles // 2) as i:
                    for s in range(2):
                        t = 2 * i + s
                        pool.wait_ge(s_yb, t + 3)
                        pool.sem_inc(s_gate, 1)
                        pool.dma_start(ys[bass.ds(t * P, P), :], yb[:, s, :]).then_inc(s_st[s], 16)
                        pool.wait_ge(s_st[s], i * 16 + 16)
                        pool.sem_inc(s_yfree, 1)


def combine(nc, c, name, ys, weight, slot, base, xn, finish_rows):
    with Core(nc) as k:
        got = k.sb(f"{name}_got", [P, 2, NT, D])
        s_got, s_done = c.pool_sem(f"{name}_cgot"), k.sem(f"{name}_cdone")
        with nc.Block() as block:

            @block.gpsimd
            def _(pool):
                for q in range(2):
                    for t in range(NT):
                        n = P if t < NT - 1 else TAIL
                        pool.indirect_dma_start(got[0:n, q, t, :], None, ys,
                                                bass.IndirectOffsetOnAxis(ap=slot[0:n, q, t:t + 1], axis=0)).then_inc(s_got, 16)

            @block.vector
            def _(dve):
                v = nc.vector
                start = TAIL // 32 * 32
                dve.wait_ge(s_got, 16 * 2 * NT)
                wide = [P, NT, D]
                v.tensor_tensor(got[:, 0, 0:NT - 1, :], got[:, 0, 0:NT - 1, :], bc(weight[:, 0, 0:NT - 1].unsqueeze(2), [P, NT - 1, D]), ALU.mult)
                v.tensor_tensor(got[0:TAIL, 0, NT - 1, :], got[0:TAIL, 0, NT - 1, :], bc(weight[0:TAIL, 0, NT - 1:NT], [TAIL, D]), ALU.mult)
                v.tensor_tensor(got[:, 1, 0:NT - 1, :], got[:, 1, 0:NT - 1, :], bc(weight[:, 1, 0:NT - 1].unsqueeze(2), [P, NT - 1, D]), ALU.mult)
                v.tensor_tensor(got[0:TAIL, 1, NT - 1, :], got[0:TAIL, 1, NT - 1, :], bc(weight[0:TAIL, 1, NT - 1:NT], [TAIL, D]), ALU.mult).then_inc(s_done, 1)
                dve.wait_ge(s_done, 1)
                for n, a, b in ((P, 0, NT - 1), (TAIL, NT - 1, NT)):
                    last = v.tensor_tensor(got[0:n, 0, a:b, :], got[0:n, 0, a:b, :], got[0:n, 1, a:b, :], ALU.add)
                last.then_inc(s_done, 1)
                dve.wait_ge(s_done, 2)
                for n, a, b in ((P, 0, NT - 1), (TAIL, NT - 1, NT)):
                    v.tensor_tensor(xn[0:n, a:b, :], base[0:n, a:b, :], got[0:n, 0, a:b, :], ALU.add)
        finish_rows(xn)


def clifford(nc, c, name, w, bias, out, bias_out, split):
    C = D // 4
    table = ((0, 1, 2, -3), (1, 0, -3, 2), (2, 3, 0, -1), (3, 2, 1, 0))
    with Core(nc) as k:
        raw = k.sb(f"{name}_raw", [P, KD, 4, C])
        raw_b = k.sb(f"{name}_raw_b", [P, D])
        s_l = k.sem(f"{name}_load")
        with nc.Block() as block:

            @block.sync
            def _(sp):
                for bo in range(4):
                    for bi in range(4):
                        at = (bi % 2) * C
                        sp.dma_start(raw[at:at + C, bi // 2, bo, :], w[abs(table[bo][bi])]).then_inc(s_l, 16)
                sp.dma_start(raw_b[:, :], row(bias)).then_inc(s_l, 16)

            @block.vector
            def _(dve):
                dve.wait_ge(s_l, 16 * 17)
                v = nc.vector
                for h in range(KD):
                    view = out[:, h, :]
                    view = view.rearrange("p (c b) -> p b c", b=4) if split else view.rearrange("p (b c) -> p b c", b=4)
                    for bo in range(4):
                        for half in range(2):
                            at = half * C
                            sign = -1.0 if table[bo][2 * h + half] < 0 else 1.0
                            v.tensor_scalar_mul(view[at:at + C, bo, :], raw[at:at + C, h, bo, :], sign)
                b = bias_out[:, :].rearrange("p (c b) -> p b c", b=4) if split else bias_out[:, :].rearrange("p (b c) -> p b c", b=4)
                v.tensor_copy(b, raw_b[:, :].rearrange("p (b c) -> p b c", b=4))


def gnn1(nc, c, I, edges):
    h_table = c.dram("h1_table", [NP, W1])
    r_table = c.dram("r1_table", [RT * P, W1])
    with Core(nc) as k:
        h = k.sb("h1", [P, NT, D])
        layernorm(nc, c, "ln1", c.x, h)
        with Core(nc) as m:
            out = m.sb("h1_out", [P, NT, W1])
            rel = m.sb("rel", [P, RT, W1])
            raw = m.sb("rel_raw", [P, RT, D])
            gw = m.sb("rel_gw", [P, D])
            gb = m.sb("rel_gb", [P, 1])
            prod = m.sb("rel_prod", [P, RT, D])
            gate = m.sb("rel_gate", [P, RT])
            s_l, s_link, s_a, s_b, s_r, s_h, s_st = (m.sem(f"g1_{x}") for x in ("load", "link", "a", "b", "rel", "hout", "st"))
            last_rel = RELATIONS - (RT - 1) * P
            with nc.Block() as block:

                @block.sync
                def _(sp):
                    src = I["L1_gnn_relation_emb"]
                    sp.wait_ge(s_a, 1)
                    sp.dma_start(raw[:, 0:RT - 1, :], src[0:(RT - 1) * P, :].rearrange("(t p) d -> p t d", p=P)).then_inc(s_l, 16)
                    sp.dma_start(raw[0:last_rel, RT - 1, :], src[(RT - 1) * P:RELATIONS, :]).then_inc(s_l, 16)
                    sp.dma_start(gw[:, :], row(I["L1_gnn_gate_w"].rearrange("a n -> (a n)"))).then_inc(s_l, 16)
                    sp.dma_start(gb[:, :], row(I["L1_gnn_gate_b"])).then_inc(s_l, 16)
                    sp.wait_ge(s_r, 1)
                    sp.dma_start(r_table.rearrange("(t p) d -> p t d", p=P), rel[:, :, :]).then_inc(s_st, 16)
                    sp.wait_ge(s_h, 1)
                    sp.dma_start(h_table.rearrange("(t p) d -> p t d", p=P), out[:, :, :]).then_inc(s_st, 16)
                    sp.wait_ge(s_st, 32)

                @block.vector
                def _(dve):
                    v, st = nc.vector, Steps(dve, s_link)
                    v.memset(rel[:, :, :], 0.0)
                    v.memset(out[:, :, :], 0.0)
                    v.memset(raw[:, :, :], 0.0).then_inc(s_a, 1)
                    dve.wait_ge(s_l, 64)
                    st.link(v.tensor_tensor(prod[:, :, :].rearrange("p t (b c) -> p t b c", b=4),
                                            raw[:, :, :].rearrange("p t (b c) -> p t b c", b=4),
                                            bc(gw[:, :].rearrange("p (c b) -> p b c", b=4).unsqueeze(1), [P, RT, 4, D // 4]), ALU.mult))
                    st.link(v.tensor_reduce(gate[:, :], prod[:, :, :], AX.X, ALU.add))
                    v.tensor_scalar(gate[:, :], gate[:, :], gb[:, 0:1], None, ALU.add).then_inc(s_a, 1)
                    dve.wait_ge(s_b, 1)
                    v.tensor_tensor(rel[:, :, 0:D], raw[:, :, :], bc(gate[:, :].unsqueeze(2), [P, RT, D]), ALU.mult)
                    v.tensor_copy(rel[:, :, D], gate[:, :]).then_inc(s_r, 1)
                    v.tensor_tensor(out[:, :, 0:D], h[:, :, :], bc(c.norm_src[:, :].unsqueeze(2), [P, NT, D]), ALU.mult)
                    v.tensor_copy(out[:, :, D], c.norm_src[:, :]).then_inc(s_h, 1)

                @block.scalar
                def _(act):
                    act.wait_ge(s_a, 2)
                    nc.scalar.activation(gate[:, :], gate[:, :], ACT.Sigmoid).then_inc(s_b, 1)

        acc = k.sb("acc1", [P, NT + 1, D + 1])
        aggregate(nc, c, "agg_r", edges, h_table, W1, acc, r_table)
        wm, bm = k.sb("msg", [P, KD, D]), k.sb("msg_bias", [P, D])
        wu, bu = k.sb("upd", [P, KD, D]), k.sb("upd_bias", [P, D])
        tmp = k.sb("g1_tmp", [P, J, D])
        weighted = k.sb("g1_weighted", [P, NT])
        clifford(nc, c, "cm", I["L1_gnn_msg_w"], I["L1_gnn_msg_b"].rearrange("b c -> (b c)"), wm, bm, False)
        clifford(nc, c, "cu", I["L1_gnn_upd_w"], I["L1_gnn_upd_b"].rearrange("b c -> (b c)"), wu, bu, True)

        with nc.Block() as block:

            @block.vector
            def _(dve):
                nc.vector.tensor_tensor(weighted[:, :], acc[:, 0:NT, D], c.norm_dst[:, :], ALU.mult)

        def messages(v, st, t0, z):
            wide = [P, J, D]
            now = h[:, bass.ds(t0, J), :]
            flat = now.rearrange("p j d -> p (j d)")
            st.link(v.tensor_tensor(tmp[:, :, :], bc(bm[:, :].unsqueeze(1), wide),
                                    bc(weighted[:, bass.ds(t0, J)].unsqueeze(2), wide), ALU.mult))
            st.link(v.tensor_tensor(tmp[:, :, :], tmp[:, :, :], z, ALU.add))
            return v.tensor_tensor(flat, flat, tmp[:, :, :].rearrange("p j d -> p (j d)"), ALU.add)

        dense(nc, c, "msgs", [(acc, wm, c.norm_dst)], D, messages, 2)

        def update(v, st, t0, z):
            wide = [P, J, D]
            out = c.x[:, bass.ds(t0, J), :].rearrange("p j d -> p (j d)")
            st.link(v.tensor_tensor(tmp[:, :, :], z, bc(bu[:, :].unsqueeze(1), wide), ALU.add))
            return v.tensor_tensor(out, out, tmp[:, :, :].rearrange("p j d -> p (j d)"), ALU.add)

        dense(nc, c, "updg", [(h, wu, None)], D, update, 1)


def build(nc, I, out):
    with Core(nc) as c:
        c.x = c.sb("x", [P, NT, D])
        c.rdeg = c.sb("rdeg", [P, NT])
        c.norm_src, c.norm_dst = c.sb("norm_src", [P, NT]), c.sb("norm_dst", [P, NT])
        c.g_base = c.sb("g_base", [P, GROUPS])
        c.g_start = c.sb("g_start", [1, GROUPS], I32)
        c.g_tile = c.sb("g_tile", [1, GROUPS], I32)
        c.alive = c.sb("alive", [P, 1])
        constants(nc, c)
        s_z, s_x, s_al = c.sem("x_zero"), c.sem("x_load"), c.sem("alive_set")
        with nc.Block() as block:

            @block.vector
            def _(dve):
                nc.vector.memset(c.x[:, :, :], 0.0).then_inc(s_z, 1)

            @block.gpsimd
            def _(pool):
                pool.memset(c.alive[:, :], 1.0).then_inc(s_al, 1)
                pool.wait_ge(s_al, 1)
                pool.affine_select(out=c.alive[:, :], in_=c.alive[:, :], compare_op=ALU.is_gt, fill=0.0,
                                   base=TAIL, pattern=[[0, 1]], channel_multiplier=-1)

            @block.sync
            def _(sp):
                sp.wait_ge(s_z, 1)
                load_rows(sp, s_x, c.x, I["x"])
                sp.wait_ge(s_x, 32)

        edges = I["edges"]
        degrees(nc, c, edges)
        gnn0(nc, c, I, edges)

        def norm_and_add(y):
            with Core(nc) as m:
                g, b = m.sb("ffn0_gamma", [P, D]), m.sb("ffn0_beta", [P, D])
                load_all(nc, "ffn0_gb", [(g[:, :], row(I["L0_ffn_gamma"])), (b[:, :], row(I["L0_ffn_beta"]))])
                layernorm(nc, c, "ln_y", y, y)
                s_link = m.sem("ffn0_link")
                with nc.Block() as block:

                    @block.vector
                    def _(dve):
                        v, st = nc.vector, Steps(dve, s_link)
                        wide = [P, NT, D]
                        st.link(v.tensor_tensor(y[:, :, :], y[:, :, :], bc(g[:, :].unsqueeze(1), wide), ALU.mult))
                        st.link(v.tensor_tensor(y[:, :, :], y[:, :, :], bc(b[:, :].unsqueeze(1), wide), ALU.add))
                        v.tensor_tensor(c.x[:, :, :], c.x[:, :, :], y[:, :, :], ALU.add)

        experts(nc, c, I, "f0", E0, F0, TILES0, False, I["L0_ffn_w1"], I["L0_ffn_b1"], I["L0_ffn_w2"], I["L0_ffn_b2"],
                I["L0_ffn_gate_w"], I["L0_ffn_gate_b"], None, ACT.Relu, norm_and_add)
        gnn1(nc, c, I, edges)

        def store(y):
            with Core(nc) as inner:
                s_out = inner.sem("stored")
                with nc.Block() as block:

                    @block.sync
                    def _(sp):
                        full = (NT - 1) * P
                        sp.dma_start(out[0:full, :].rearrange("(t p) d -> p t d", p=P), y[:, 0:NT - 1, :]).then_inc(s_out, 16)
                        sp.dma_start(out[full:N, :], y[0:TAIL, NT - 1, :]).then_inc(s_out, 16)
                        sp.wait_ge(s_out, 32)

        experts(nc, c, I, "f1", E1, F1, TILES1, True, I["L1_ffn_W1"], I["L1_ffn_b1"], I["L1_ffn_W2"], I["L1_ffn_b2"],
                I["L1_ffn_Wr"], I["L1_ffn_br"], (I["L1_ffn_ln_g"], I["L1_ffn_ln_b"]), ACT.Gelu, store)


def kernel(**inputs):
    import concourse.bacc as _bacc
    from concourse.bass_utils import run_bass_kernel_spmd as _run

    nc = _bacc.Bacc("TRN2", target_bir_lowering=False, num_devices=1)
    arrays = {}
    edges = np.zeros((EDGE_ROWS, 4), np.int32)
    edges[:, 1] = edges[:, 3] = NOWHERE
    for col, name in ((0, "src"), (1, "dst"), (2, "edge_type_500"), (3, "src")):
        edges[:E, col] = np.asarray(inputs[name])
    arrays["edges"] = edges
    for name, a in inputs.items():
        a = np.asarray(a)
        if name in ("src", "dst", "edge_type_500"):
            continue
        if name in ("L0_ffn_b1", "L1_ffn_b1", "L1_ffn_ln_g", "L1_ffn_ln_b"):
            a = a.reshape(a.shape[0], -1, P).transpose(2, 0, 1)
        if name in ("L1_gnn_msg_w", "L1_gnn_upd_w"):
            a = a.transpose(0, 2, 1)
        arrays[name] = np.ascontiguousarray(a)
    args = {n: nc.dram_tensor(f"in_{n}", a.shape, mybir.dt.from_np(a.dtype), kind="ExternalInput").ap() for n, a in arrays.items()}
    out = nc.dram_tensor("out_0", (N, D), F32, kind="ExternalOutput").ap()
    build(nc, args, out)
    r = _run(nc, [{f"in_{n}": a for n, a in arrays.items()}], core_ids=[0])
    return r.results[0]["out_0"]
```

```python
from contextlib import ExitStack, contextmanager

import numpy as np

import concourse.bass as bass
from concourse import mybir

ALU = mybir.AluOpType
ACT = mybir.ActivationFunctionType
AX = mybir.AxisListType
F32 = mybir.dt.float32
BF16 = mybir.dt.bfloat16
I32 = mybir.dt.int32
U32 = mybir.dt.uint32

P = 128
N, E, D = 3125, 103125, 256
NT = -(-N // P)
TAIL = N - (NT - 1) * P
NP = NT * P
KD = D // P
J = 5
NJ = NT // J
EPS = 1e-5

CH = 4
EDGE_TILES = -(-E // (CH * P)) * CH
EDGE_ROWS = EDGE_TILES * P + 1024
NOWHERE = 1 << 20
RING = 4


def groups_for(classes, size):
    return -(-((E + classes * (size - 1)) // size) // RING) * RING


G = 4
GE = G * P
GROUPS = groups_for(NT, GE)
SW = 32
STRIPS = -(-N // SW)
GA = 2
GAE = GA * P
GROUPS_A = groups_for(STRIPS, GAE)
CODES = NT * SW
ND = STRIPS * SW
NCH = 7
DC = ND // NCH
LAG_A = 4
assert NCH * DC == ND and DC <= 512 and CODES // 2 <= 512 and GROUPS_A <= 512

E0, F0, TILES0 = 16, 512, (2 * N + 16 * (P - 1)) // P
E1, F1, TILES1 = 8, 1024, (2 * N + 8 * (P - 1)) // P
TILES0 += TILES0 % 2
TILES1 += TILES1 % 2
RELATIONS = 500
RT = -(-RELATIONS // P)
NTP = 28
PORTIONS = ((0, (512, 512, 512, 512), 16), (2048, (384, 384, 352), 12))
MW = 3168
J2 = 2
W1 = 260


class Steps:

    def __init__(self, engine, sem):
        self.engine, self.sem, self.base, self.n = engine, sem, 0, 0

    def link(self, instruction):
        instruction.then_inc(self.sem, 1)
        self.n += 1
        self.engine.wait_ge(self.sem, self.base + self.n)
        return instruction

    @contextmanager
    def each(self, i, count, steps):
        start, self.base, self.n = self.base + self.n, self.base + self.n + i * steps, 0
        yield
        assert self.n == steps, (self.n, steps)
        self.base, self.n = start + count * steps, 0


class Core:

    def __init__(self, nc):
        self.nc, self.ctx, self.sems = nc, ExitStack(), []

    def __enter__(self):
        return self

    def __exit__(self, kind, *_):
        if kind is None and self.sems:
            with self.nc.Block() as block:

                @block.gpsimd
                def _(pool):
                    for sem in self.sems:
                        pool.sem_clear(sem)

        self.ctx.close()

    def sb(self, name, shape, dt=F32):
        return self.ctx.enter_context(self.nc.sbuf_tensor(name, shape, dt))

    def ps(self, name, shape, dt=F32):
        return self.ctx.enter_context(self.nc.psum_tensor(name, shape, dt))

    def sem(self, name):
        self.sems.append(self.ctx.enter_context(self.nc.semaphore(name)))
        return self.sems[-1]

    def pool_sem(self, name):
        return self.ctx.enter_context(self.nc.semaphore(name))

    def dram(self, name, shape, dt=F32):
        return self.nc.dram_tensor(name, shape, dt).ap()


def bc(ap, shape):
    return ap.to_broadcast(shape)


def constants(nc, c):
    c.ident = c.sb("ident", [P, P])
    c.ones = c.sb("ones", [P, P])
    c.before = c.sb("before", [P, P])
    c.iota = c.sb("iota", [P, GROUPS_A])
    with Core(nc) as k:
        iota_i = k.sb("iota_i", [P, GROUPS_A], I32)
        constants_set(nc, c, iota_i, k.sem("const_set"), k.sem("const_iota"))


def constants_set(nc, c, iota_i, s_set, s_iota):
    with nc.Block() as block:

        @block.gpsimd
        def _(pool):
            pool.memset(c.ident[:, :], 0.0).then_inc(s_set, 1)
            pool.memset(c.ones[:, :], 1.0).then_inc(s_set, 1)
            pool.memset(c.before[:, :], 1.0).then_inc(s_set, 1)
            pool.iota(iota_i[:, :], pattern=[[1, GROUPS_A]], base=0, channel_multiplier=0).then_inc(s_iota, 1)
            pool.wait_ge(s_set, 3)
            pool.affine_select(out=c.ident[:, :], in_=c.ident[:, :], compare_op=ALU.not_equal, fill=1.0,
                               base=0, pattern=[[-1, P]], channel_multiplier=1)
            pool.affine_select(out=c.before[:, :], in_=c.before[:, :], compare_op=ALU.is_gt, fill=0.0,
                               base=0, pattern=[[1, P]], channel_multiplier=-1)

        @block.vector
        def _(dve):
            dve.wait_ge(s_iota, 1)
            nc.vector.tensor_copy(c.iota[:, :], iota_i[:, :])


def load_rows(dma, sem, dst, dram):
    full = (NT - 1) * P
    dma.dma_start(dst[:, 0:NT - 1, :], dram[0:full, :].rearrange("(t p) d -> p t d", p=P)).then_inc(sem, 16)
    dma.dma_start(dst[0:TAIL, NT - 1, :], dram[full:N, :]).then_inc(sem, 16)


def prepare_edges(nc, c, edges, records):
    with Core(nc) as k:
        ed = k.sb("ed", [P, EDGE_TILES, 4], I32)
        ints = k.sb("ed_ints", [P, EDGE_TILES, 4], I32)
        rec = k.sb("rec", [P, EDGE_TILES, 4])
        low = k.sb("low", [P, EDGE_TILES])
        key = k.sb("key", [P, EDGE_TILES], BF16)
        hit = k.sb("hit", [P, EDGE_TILES], BF16)
        counts = k.sb("counts", [P, NT * P // SW])
        tile_counts = k.sb("tile_counts", [P, NT])
        none = k.sb("none", [P, 8, 4])
        s_edges, s_link, s_rec, s_stored = (k.sem(f"prep_{x}") for x in ("edges", "link", "rec", "stored"))
        with nc.Block() as block:

            @block.sync
            def _(sp):
                sp.dma_start(ed[:, :, :], edges[0:EDGE_TILES * P, :].rearrange("(p k) c -> p k c", p=P)).then_inc(s_edges, 16)
                sp.wait_ge(s_rec, 1)
                sp.dma_start(records[0:EDGE_TILES * P, :].rearrange("(p k) c -> p k c", p=P), rec[:, :, :]).then_inc(s_stored, 16)
                sp.dma_start(records[EDGE_TILES * P:EDGE_ROWS, :].rearrange("(p k) c -> p k c", p=P), none[:, :, :]).then_inc(s_stored, 16)
                sp.wait_ge(s_stored, 32)

            @block.vector
            def _(dve):
                v, st = nc.vector, Steps(dve, s_link)
                v.memset(none[:, :, :], -1.0)
                v.memset(rec[:, :, 3], 0.0)
                st.link(v.memset(counts[:, :], 0.0))
                dve.wait_ge(s_edges, 16)
                bits = SW.bit_length() - 1
                v.tensor_scalar(ints[:, :, 0], ed[:, :, 0], P - 1, None, ALU.bitwise_and)
                v.tensor_scalar(ints[:, :, 1], ed[:, :, 0], P.bit_length() - 1, bits, ALU.arith_shift_right, ALU.logical_shift_left)
                v.tensor_scalar(ints[:, :, 2], ed[:, :, 1], bits, None, ALU.arith_shift_right)
                st.link(v.tensor_scalar(ints[:, :, 3], ed[:, :, 1], SW - 1, None, ALU.bitwise_and))
                v.tensor_copy(low[:, :], ints[:, :, 3])
                v.tensor_copy(key[:, :], ints[:, :, 2])
                v.tensor_copy(rec[:, :, 0], ints[:, :, 0])
                v.tensor_copy(rec[:, :, 2], ints[:, :, 2])
                st.link(v.tensor_scalar_add(rec[:, :, 1], ints[:, :, 1], 1.0))
                v.tensor_tensor(rec[:, :, 1], rec[:, :, 1], low[:, :], ALU.add).then_inc(s_rec, 1)
                st.link(v.engine_nop())
                with dve.Fori(0, STRIPS) as b, st.each(b, STRIPS, 1):
                    st.link(v.tensor_scalar(hit[:, :], key[:, :], c.iota[:, bass.ds(b, 1)], 0.0, ALU.is_equal, ALU.add,
                                            accum_out=counts[:, bass.ds(b, 1)]))
                v.tensor_reduce(tile_counts[:, :], counts[:, :].rearrange("p (t s) -> p t s", t=NT), AX.X, ALU.add)

        group_tables(nc, c, "ga", counts, STRIPS, GAE, GROUPS_A, c.tab["a_strip"], 1.0, c.tab["a_start"], c.tab["a_col"], SW, LAG_A)
        group_tables(nc, c, "gt", tile_counts, NT, GE, GROUPS, c.tab["g_base"], float(P), c.tab["g_start"], c.tab["g_tile"], 1, 1)


def group_tables(nc, c, name, counts, n, size, groups, class_out, factor, start_out, place_out, step, lag):
    with Core(nc) as k:
        col = k.sb(f"{name}_col", [n, 6])
        col_i = k.sb(f"{name}_col_i", [n, 2], I32)
        ended = k.sb(f"{name}_ended", [n, groups])
        less = k.sb(f"{name}_less", [n, P])
        start_f = k.sb(f"{name}_start_f", [1, groups])
        tot = k.ps(f"{name}_tot", [P, 512])
        cum = k.ps(f"{name}_cum", [P, 512])
        cls = k.ps(f"{name}_cls", [P, 512])
        pos = k.ps(f"{name}_pos", [P, 512])
        s_link, s_tot, s_c, s_cum, s_u, s_out = (k.sem(f"{name}_{x}") for x in ("link", "tot", "c", "cum", "u", "out"))
        with nc.Block() as block:

            @block.tensor
            def _(pe):
                nc.tensor.matmul(tot[0:n, 0:1], counts[:, 0:n], c.ones[:, 0:1], start=True, stop=True).then_inc(s_tot, 1)
                pe.wait_ge(s_c, 1)
                nc.tensor.matmul(cum[0:n, 0:1], c.before[0:n, 0:n], col[:, 2:3], start=True, stop=True).then_inc(s_cum, 1)
                pe.wait_ge(s_u, 1)
                nc.tensor.matmul(cls[:, 0:groups], c.ones[0:n, :], ended[:, :], start=True, stop=True)
                nc.tensor.matmul(pos[:, 0:groups], less[:, :], ended[:, :], start=True, stop=True).then_inc(s_out, 1)

            @block.vector
            def _(dve):
                v, st = nc.vector, Steps(dve, s_link)
                bits = size.bit_length() - 1
                dve.wait_ge(s_tot, 1)
                v.tensor_copy(col[:, 0:1], tot[0:n, 0:1])
                st.link(v.tensor_scalar_add(col[:, 1:2], tot[0:n, 0:1], float(size - 1)))
                st.link(v.tensor_copy(col_i[:, 0:1], col[:, 1:2]))
                st.link(v.tensor_scalar(col_i[:, 1:2], col_i[:, 0:1], bits, bits, ALU.arith_shift_right, ALU.logical_shift_left))
                st.link(v.tensor_copy(col[:, 1:2], col_i[:, 1:2]))
                v.tensor_tensor(col[:, 4:5], col[:, 0:1], col[:, 1:2], ALU.subtract)
                v.tensor_scalar_mul(col[:, 2:3], col[:, 1:2], 1.0 / size).then_inc(s_c, 1)
                dve.wait_ge(s_cum, 1)
                st.link(v.tensor_tensor(col[:, 3:4], cum[0:n, 0:1], col[:, 2:3], ALU.add))
                v.tensor_scalar(ended[:, :], c.iota[0:n, 0:groups], col[:, 3:4], None, ALU.is_ge)
                v.tensor_scalar(less[:, :], c.ones[0:n, :], col[:, 4:5], None, ALU.mult).then_inc(s_u, 1)
                dve.wait_ge(s_out, 1)
                v.tensor_scalar_mul(class_out[:, :], cls[:, 0:groups], factor)
                v.tensor_scalar_mul(place_out[:, lag:lag + groups], cls[0:1, 0:groups], float(step))
                v.memset(place_out[:, 0:lag], n * step)
                st.link(v.scalar_tensor_tensor(start_f[:, :], c.iota[0:1, 0:groups], float(size), pos[0:1, 0:groups], ALU.mult, ALU.add))
                v.tensor_scalar_min(start_out[:, :], start_f[:, :], float(EDGE_TILES * P))


def group_table(v, st, per, per_i, n, size):
    st.link(v.tensor_scalar_add(per[:, 1, 0:n], per[:, 0, 0:n], float(size - 1)))
    st.link(v.tensor_copy(per_i[:, 0, 0:n], per[:, 1, 0:n]))
    bits = size.bit_length() - 1
    st.link(v.tensor_scalar(per_i[:, 1, 0:n], per_i[:, 0, 0:n], bits, bits, ALU.arith_shift_right, ALU.logical_shift_left))
    st.link(v.tensor_copy(per[:, 1, 0:n], per_i[:, 1, 0:n]))
    st.link(v.tensor_tensor(per[:, 4, 0:n], per[:, 0, 0:n], per[:, 1, 0:n], ALU.subtract))
    st.link(v.tensor_scalar_mul(per[:, 1, 0:n], per[:, 1, 0:n], 1.0 / size))
    st.link(v.memset(per[:, 2, 0:n], 0.0))
    st.link(v.tensor_tensor_scan(per[:, 3, 0:n], per[:, 1, 0:n], per[:, 2, 0:n], 0.0, ALU.add, ALU.add))
    st.link(v.tensor_tensor(per[:, 5, 0:n], per[:, 3, 0:n], per[:, 1, 0:n], ALU.subtract))
    st.link(v.tensor_scalar_mul(per[:, 5, 0:n], per[:, 5, 0:n], float(size)))


def layernorm(nc, c, name, src, dst, after=None, NT=NT):
    with Core(nc) as k:
        stats = k.sb(f"{name}_stats", [P, NT, 6])
        mean = k.sb(f"{name}_mean", [P, NT])
        var = k.sb(f"{name}_var", [P, NT])
        tmp = k.sb(f"{name}_tmp", [P, NT])
        s_link, s_var, s_root, s_done, s_store = (k.sem(f"{name}_{x}") for x in ("link", "var", "root", "done", "store"))
        with nc.Block() as block:

            @block.vector
            def _(dve):
                v, st = nc.vector, Steps(dve, s_link)
                with dve.Fori(0, NT) as t:
                    last = v.bn_stats(stats[:, bass.ds(t, 1), :].rearrange("p a s -> p (a s)"),
                                      src[:, bass.ds(t, 1), :].rearrange("p a d -> p (a d)"))
                v.drain().then_inc(s_done, 1)
                dve.wait_ge(s_done, 1)
                v.tensor_tensor(mean[:, :], stats[:, :, 1], stats[:, :, 4], ALU.add)
                v.tensor_tensor(tmp[:, :], stats[:, :, 1], stats[:, :, 4], ALU.subtract)
                st.link(v.tensor_tensor(var[:, :], stats[:, :, 2], stats[:, :, 5], ALU.add))
                v.tensor_scalar_mul(mean[:, :], mean[:, :], 0.5)
                st.link(v.tensor_tensor(tmp[:, :], tmp[:, :], tmp[:, :], ALU.mult))
                st.link(v.tensor_scalar(var[:, :], var[:, :], 1.0 / D, EPS, ALU.mult, ALU.add))
                v.scalar_tensor_tensor(var[:, :], tmp[:, :], 0.25, var[:, :], ALU.mult, ALU.add).then_inc(s_var, 1)
                dve.wait_ge(s_root, 1)
                st.link(v.reciprocal(var[:, :], tmp[:, :]))
                with dve.Fori(0, NT) as t:
                    v.tensor_scalar(dst[:, bass.ds(t, 1), 0:D].rearrange("p a d -> p (a d)"),
                                    src[:, bass.ds(t, 1), :].rearrange("p a d -> p (a d)"),
                                    mean[:, bass.ds(t, 1)], var[:, bass.ds(t, 1)], ALU.subtract, ALU.mult)
                if after:
                    v.drain().then_inc(s_done, 1)

            @block.scalar
            def _(act):
                act.wait_ge(s_var, 1)
                nc.scalar.activation(tmp[:, :], var[:, :], ACT.Sqrt).then_inc(s_root, 1)

            if after:

                @block.sync
                def _(sp):
                    sp.wait_ge(s_done, 2)
                    after(sp, s_store)


def aggregate(nc, c, name, edges, table, width, acc, relation_rows):
    used = D + 1
    with Core(nc) as k:
        ed = k.sb(f"{name}_ed", [P, RING, G, 4], I32)
        dst_f = k.sb(f"{name}_dst_f", [P, RING, G])
        rows = k.sb(f"{name}_rows", [P, RING, G, width])
        rel = k.sb(f"{name}_rel", [P, RING, G, width])
        onehot = k.sb(f"{name}_onehot", [P, RING, G, P])
        sums = k.ps(f"{name}_sums", [P, 2, 512])
        s_edges = [k.sem(f"{name}_edges{s}") for s in range(RING)]
        s_rel = [k.sem(f"{name}_rel{s}") for s in range(RING)]
        s_rows = [c.pool_sem(f"{name}_rows{s}") for s in range(RING)]
        s_link, s_ready, s_sum, s_acc, s_gate = (k.sem(f"{name}_{x}") for x in ("link", "ready", "sum", "acc", "gate"))
        LENT = RING + 1
        with nc.Block() as block:

            @block.sync
            def _(sp):
                with sp.Fori(0, GROUPS // RING) as i:
                    for s in range(RING):
                        start = sp.value_load(c.tab["g_start"][0:1, bass.ds(i * RING + s, 1)], min_val=0, max_val=EDGE_TILES * P)
                        src = edges[bass.ds(start, GE), :].rearrange("(p k) c -> p k c", p=P)
                        rel_src = relation_rows[bass.ds(start, GE), :].rearrange("(p k) c -> p (k c)", p=P)
                        sp.wait_ge(s_sum, i * RING + s + 2)
                        sp.dma_start(ed[:, s, :, :], src).then_inc(s_edges[s], 16)
                        sp.dma_start(rel[:, s, :, :].rearrange("p k c -> p (k c)"), rel_src).then_inc(s_rel[s], 16)

            @block.gpsimd
            def _(pool):
                with pool.Fori(0, GROUPS // RING) as i:
                    for s in range(RING):
                        pool.wait_ge(s_edges[s], i * 16 + 16)
                        pool.sem_inc(s_gate, 1)
                        for g in range(G):
                            pool.indirect_dma_start(rows[:, s, g, :], None, table,
                                                    bass.IndirectOffsetOnAxis(ap=ed[:, s, g, 0:1], axis=0))\
                                .then_inc(s_rows[s], 16)

            @block.vector
            def _(dve):
                v, st = nc.vector, Steps(dve, s_link)

                def add(g, bank, tile):
                    dve.wait_ge(s_acc, g + 1)
                    dve.wait_ge(s_sum, g + LENT)
                    here = acc[:, bass.ds(tile, 1), 0:used].rearrange("p a d -> p (a d)")
                    v.tensor_tensor(here, here, sums[:, bank, 0:used], ALU.add).then_inc(s_acc, 1)

                v.memset(acc[:, :, :], 0.0).then_inc(s_acc, 1)
                with dve.Fori(0, GROUPS // RING) as i, st.each(i, GROUPS // RING, 2 * RING):
                    for s in range(RING):
                        g = i * RING + s
                        tile = dve.value_load(c.tab["g_tile"][0:1, bass.ds(g, 1)], min_val=0, max_val=NT)
                        dve.wait_ge(s_edges[s], i * 16 + 16)
                        st.link(v.tensor_copy(dst_f[:, s, :], ed[:, s, :, 1]))
                        st.link(v.tensor_scalar(dst_f[:, s, :], dst_f[:, s, :], c.tab["g_base"][:, bass.ds(g, 1)], None, ALU.subtract))
                        for t in range(G):
                            v.tensor_scalar(onehot[:, s, t, :], c.iota[:, 0:P], dst_f[:, s, t:t + 1], None, ALU.is_equal)
                        dve.wait_ge(s_rel[s], i * 16 + 16)
                        dve.wait_ge(s_rows[s], i * (16 * G) + 16 * G)
                        v.tensor_tensor(rows[:, s, :, 0:used], rows[:, s, :, 0:used], rel[:, s, :, 0:used], ALU.mult)\
                            .then_inc(s_ready, 1)
                        add(g, (s + 1) % 2, tile)
                add(GROUPS, (GROUPS - 1) % 2, dve.value_load(c.tab["g_tile"][0:1, GROUPS:GROUPS + 1], min_val=0, max_val=NT))

            @block.tensor
            def _(pe):
                nc.tensor.matmul(sums[:, 1, 0:used], c.zero_b[:, 0:P], c.zero_b[:, 0:used], start=True, stop=True).then_inc(s_sum, LENT)
                with pe.Fori(0, GROUPS // RING) as i:
                    for s in range(RING):
                        pe.wait_ge(s_ready, i * RING + s + 1)
                        pe.wait_ge(s_acc, i * RING + s + 1)
                        for t in range(G):
                            last = nc.tensor.matmul(sums[:, s % 2, 0:used], onehot[:, s, t, :], rows[:, s, t, 0:used],
                                                    start=t == 0, stop=t == G - 1)
                        last.then_inc(s_sum, 1)


def dense(nc, c, name, sources, M, finish, steps, after=None):
    with Core(nc) as k:
        n = len(sources)
        own = [k.sb(f"{name}_own{q}", [P, J, D]) for q in range(n)]
        turned = [k.sb(f"{name}_turned{q}", [P, J, KD, P]) for q in range(n)]
        bank = [k.ps(f"{name}_bank{q}", [P, 3 * 512]) for q in range(n)]
        s_own, s_t, s_turned, s_z, s_free, s_link, s_store = (
            k.sem(f"{name}_{x}") for x in ("own", "t", "turned", "z", "free", "link", "store"))
        with nc.Block() as block:

            @block.scalar
            def _(act):
                with act.Fori(0, NJ) as i:
                    for q, (rows, _, factor) in enumerate(sources):
                        act.wait_ge(s_t, i * n + q + 1)
                        for j in range(J):
                            at = bass.ds(i * J + j, 1)
                            last = nc.scalar.activation(own[q][:, j, :], rows[:, at, 0:D].rearrange("p a d -> p (a d)"), ACT.Copy,
                                                        scale=1.0 if factor is None else factor[:, at])
                        last.then_inc(s_own, 1)

            @block.tensor
            def _(pe):
                pe.sem_inc(s_t, n)
                with pe.Fori(0, NJ) as i:
                    pe.wait_ge(s_free, i + 1)
                    for q in range(n):
                        pe.wait_ge(s_own, i * n + q + 1)
                        for j in range(J):
                            for h in range(KD):
                                at = (j * KD + h) * P
                                last = nc.tensor.transpose(bank[q][:, at:at + P], own[q][:, j, h * P:(h + 1) * P], c.ident[:, :])
                        last.then_inc(s_t, 1)
                    pe.wait_ge(s_turned, i + 1)
                    for j in range(J):
                        for q, (_, weight, _) in enumerate(sources):
                            for h in range(KD):
                                last = nc.tensor.matmul(bank[0][:, j * D:j * D + M], turned[q][:, j, h, :], weight[:, h, :],
                                                        start=q == 0 and h == 0, stop=q == n - 1 and h == KD - 1)
                    last.then_inc(s_z, 1)

            @block.vector
            def _(dve):
                v, st = nc.vector, Steps(dve, s_link)
                dve.sem_inc(s_free, 1)
                with dve.Fori(0, NJ) as i, st.each(i, NJ, steps):
                    for q in range(n):
                        dve.wait_ge(s_t, i * n + q + 1 + n)
                        last = v.tensor_copy(turned[q][:, :, :, :].rearrange("p j h c -> p (j h c)"), bank[q][:, 0:J * D])
                    last.then_inc(s_turned, 1)
                    dve.wait_ge(s_z, i + 1)
                    z = bank[0][:, 0:J * D].rearrange("p (j d) -> p j d", d=D)[:, :, 0:M]
                    finish(v, st, i * J, z).then_inc(s_free, 1)
                if after:
                    dve.wait_ge(s_free, NJ + 1)

            if after:

                @block.sync
                def _(sp):
                    sp.wait_ge(s_free, NJ + 1)
                    after(sp, s_store)


def load_all(nc, name, loads):
    with Core(nc) as k:
        s = k.sem(f"{name}_loads")
        with nc.Block() as block:

            @block.sync
            def _(sp):
                for out, src in loads:
                    sp.dma_start(out, src, allow_slow_non_contiguous=True).then_inc(s, 16)
                sp.wait_ge(s, 16 * len(loads))


def row(ap):
    return ap.rearrange("(a n) -> a n", a=1).to_broadcast([P, ap.shape[0]])


def split_rows(v, st, dst, src, rest):
    st.link(v.tensor_copy(dst[0], src))
    st.link(v.tensor_tensor(rest, src, dst[0], ALU.subtract))
    st.link(v.tensor_copy(dst[1], rest))
    st.link(v.tensor_tensor(rest, rest, dst[1], ALU.subtract))
    return v.tensor_copy(dst[2], rest)


def gnn0_start(nc, c, I, x_dram, h_table, parts):
    with Core(nc) as k:
        x = k.sb("x0", [P, NTP, D])
        s_x = k.sem("x0_load")
        with nc.Block() as block:

            @block.sync
            def _(sp):
                sp.dma_start(x[:, :, :], x_dram.rearrange("(t p) d -> p t d", p=P)).then_inc(s_x, 16)
                sp.wait_ge(s_x, 16)

        h = k.sb("h0", [P, NTP, D])
        s_mask = k.sem("mask_row")

        def mask_row(sp, s_store):
            sp.dma_start(h[0:1, 0, :], I["L0_gnn_mask_embed"].rearrange("(a n) -> a n", a=1)).then_inc(s_mask, 16)
            sp.wait_ge(s_mask, 16)
            sp.dma_start(h_table.rearrange("(t p) d -> p t d", p=P), h[:, :, :]).then_inc(s_store, 16)
            sp.wait_ge(s_store, 16)

        layernorm(nc, c, "ln0", x, h, mask_row, NTP)
        T = 4
        part = k.sb("part0", [P, 2, T, 3, D], BF16)
        rest = k.sb("rest0", [P, T, D])
        s_link, s_part, s_save, s_free = (k.sem(f"split_{x}") for x in ("link", "part", "save", "free"))
        with nc.Block() as block:

            @block.vector
            def _(dve):
                v, st = nc.vector, Steps(dve, s_link)
                for b in range(NTP // T):
                    if b >= 2:
                        dve.wait_ge(s_free, b - 1)
                    split_rows(v, st, [part[:, b % 2, :, q, :] for q in range(3)], h[:, b * T:b * T + T, :], rest[:, :, :])\
                        .then_inc(s_part, 1)

            @block.sync
            def _(sp):
                for b in range(NTP // T):
                    sp.wait_ge(s_part, b + 1)
                    sp.dma_start(parts[b * T:b * T + T].rearrange("t p f -> p t f"),
                                 part[:, b % 2, :, :, :].rearrange("p t q d -> p t (q d)")).then_inc(s_save, 16)
                    sp.wait_ge(s_save, 16 * b + 16)
                    sp.sem_inc(s_free, 1)


def build_matrix(nc, c, records, m, relation_work):
    with Core(nc) as k:
        R = RING
        rec = k.sb("b_rec", [P, R, GA, 4])
        code = k.sb("b_code", [P, R, GA])
        at = k.sb("b_at", [P, R, GA, P], BF16)
        oh = k.sb("b_oh", [P, R, GA, CODES], BF16)
        got = k.sb("b_got", [P, LAG_A, CODES], BF16)
        numbers = k.sb("b_numbers", [P, CODES], mybir.dt.float16)
        with Core(nc) as kk:
            whole = kk.sb("b_whole", [P, CODES], I32)
            s_n = kk.sem("b_whole_set")
            with nc.Block() as block:

                @block.gpsimd
                def _(pool):
                    pool.iota(whole[:, :], pattern=[[1, CODES]], base=0, channel_multiplier=0).then_inc(s_n, 1)

                @block.vector
                def _(dve):
                    dve.wait_ge(s_n, 1)
                    nc.vector.tensor_scalar_add(numbers[:, :], whole[:, :], 1.0)
                    for t in range(NT):
                        nc.vector.memset(m[:, t, :], 0.0)

        half = CODES // 2
        strips = k.ps("b_strips", [P, 2 * R, 512])
        s_rec = [k.sem(f"b_rec{s}") for s in range(R)]
        s_link, s_oh, s_sum, s_got, s_m = (k.sem(f"b_{x}") for x in ("link", "onehot", "sum", "got", "m"))
        iota_low = k.sb("b_iota", [P, P], BF16)
        with nc.Block() as block:

            @block.sync
            def _(sp):
                with sp.Fori(0, GROUPS_A // R) as i:
                    for s in range(R):
                        start = sp.value_load(c.tab["a_start"][0:1, bass.ds(i * R + s, 1)], min_val=0, max_val=EDGE_TILES * P)
                        src = records[bass.ds(start, GAE), :].rearrange("(p k) c -> p k c", p=P)
                        sp.wait_ge(s_sum, i * R + s + 1)
                        sp.dma_start(rec[:, s, :, :], src).then_inc(s_rec[s], 16)

            @block.vector
            def _(dve):
                v, st = nc.vector, Steps(dve, s_link)

                def place(g, s, col):
                    dve.wait_ge(s_m, g + 1)
                    dve.wait_ge(s_got, g + 1)
                    here = m[:, :, bass.ds(col, SW)]
                    v.tensor_tensor(here, here, got[:, s, :].rearrange("p (t w) -> p t w", w=SW), ALU.add).then_inc(s_m, 1)

                v.tensor_copy(iota_low[:, :], c.iota[:, 0:P])
                st.link(v.memset(got[:, :, :], 0.0))
                dve.sem_inc(s_got, LAG_A)
                dve.sem_inc(s_m, 1)
                with dve.Fori(0, GROUPS_A // R) as i, st.each(i, GROUPS_A // R, R):
                    for s in range(R):
                        g = i * R + s
                        col = dve.value_load(c.tab["a_col"][0:1, bass.ds(g, 1)], min_val=0, max_val=MW - SW)
                        dve.wait_ge(s_rec[s], i * 16 + 16)
                        v.scalar_tensor_tensor(code[:, s, :], rec[:, s, :, 2], c.tab["a_strip"][:, bass.ds(g, 1)], rec[:, s, :, 1],
                                               ALU.is_equal, ALU.mult).then_inc(s_link, 1)
                        st.n += 1
                        for t in range(GA):
                            v.tensor_scalar(at[:, s, t, :], iota_low[:, :], rec[:, s, t, 0:1], None, ALU.is_equal)
                        dve.wait_ge(s_link, st.base + st.n)
                        for t in range(GA):
                            last = v.tensor_scalar(oh[:, s, t, :], numbers[:, :], code[:, s, t:t + 1], None, ALU.is_equal)
                        last.then_inc(s_oh, 1)
                        place(g, s, col)
                for s in range(LAG_A):
                    g = GROUPS_A + s
                    place(g, s, dve.value_load(c.tab["a_col"][0:1, g:g + 1], min_val=0, max_val=MW - SW))

            @block.tensor
            def _(pe):
                pe.sem_inc(s_sum, R)
                with pe.Fori(0, GROUPS_A // R) as i:
                    for s in range(R):
                        pe.wait_ge(s_oh, i * R + s + 1)
                        pe.wait_ge(s_got, i * R + s + 1)
                        for t in range(GA):
                            for b in range(2):
                                last = nc.tensor.matmul(strips[:, 2 * s + b, 0:half], at[:, s, t, :],
                                                        oh[:, s, t, b * half:(b + 1) * half], start=t == 0, stop=t == GA - 1)
                        last.then_inc(s_sum, 1)

            @block.scalar
            def _(act):
                with act.Fori(0, GROUPS_A // R) as i:
                    for s in range(R):
                        act.wait_ge(s_sum, i * R + s + 1 + R)
                        act.wait_ge(s_m, i * R + s + 2)
                        nc.scalar.activation(got[:, s, :].rearrange("p (b c) -> p b c", b=2), strips[:, 2 * s:2 * s + 2, 0:half],
                                             ACT.Copy).then_inc(s_got, 1)

            @block.gpsimd
            def _(pool):
                relation_work(pool)


def node_degrees(nc, c, m):
    with Core(nc) as k:
        junk = k.sb("nd_junk", [P, MW], BF16)
        deg = k.sb("nd_deg", [P, 2, NTP])
        root = k.sb("nd_root", [P, 2, NTP])
        cols = k.ps("nd_cols", [P, 512])
        s_zero, s_in, s_out, s_clip, s_root, s_ones = (k.sem(f"nd_{x}") for x in ("zero", "in", "out", "clip", "root", "ones"))
        ones = k.sb("nd_ones", [P, 1], BF16)
        with nc.Block() as block:

            @block.tensor
            def _(pe):
                pe.wait_ge(s_ones, 1)
                for t in range(NT):
                    w = min(P, MW - t * P)
                    for q in range(NT):
                        last = nc.tensor.matmul(cols[0:w, t:t + 1], m[:, q, t * P:t * P + w], ones[:, :], start=q == 0, stop=q == NT - 1)
                last.then_inc(s_in, 1)

            @block.scalar
            def _(act):
                act.wait_ge(s_zero, 1)
                for q in range(NT):
                    nc.scalar.activation(junk[:, :], m[:, q, :], ACT.Copy, accum_out=deg[:, 0, q:q + 1]).then_inc(s_out, 1)
                    act.wait_ge(s_out, q + 1)
                act.wait_ge(s_clip, 1)
                nc.scalar.activation(root[:, :, :], deg[:, :, :], ACT.Sqrt).then_inc(s_root, 1)

            @block.vector
            def _(dve):
                v = nc.vector
                v.memset(deg[:, :, :], 0.0).then_inc(s_zero, 1)
                v.memset(ones[:, :], 1.0).then_inc(s_ones, 1)
                dve.wait_ge(s_zero, 1)
                dve.wait_ge(s_in, 1)
                w = MW - (NT - 1) * P
                v.tensor_copy(deg[:, 1, 0:NT - 1], cols[:, 0:NT - 1])
                v.tensor_copy(deg[0:w, 1, NT - 1:NT], cols[0:w, NT - 1:NT]).then_inc(s_zero, 1)
                dve.wait_ge(s_out, NT)
                dve.wait_ge(s_zero, 2)
                v.tensor_scalar_max(deg[:, :, :], deg[:, :, :], 1.0).then_inc(s_clip, 1)
                dve.wait_ge(s_clip, 1)
                v.reciprocal(c.rdeg[:, :], deg[:, 1, :])
                dve.wait_ge(s_root, 1)
                v.reciprocal(c.norm_src[:, :], root[:, 0, 0:NT])
                v.reciprocal(c.norm_dst[:, :], root[:, 1, 0:NT])


def gnn0_layer(nc, c, I, layer, m, h_table, parts, next_parts, x_dram, out_table):
    final = out_table is not None
    with Core(nc) as k:
        n = f"l{layer}"
        wl, wr, shift = k.sb(f"{n}_wl", [P, KD, D]), k.sb(f"{n}_wr", [P, KD, D]), k.sb(f"{n}_shift", [P, D])
        with Core(nc) as kk:
            vecs, mul = kk.sb(f"{n}_vecs", [P, 5, D]), kk.sb(f"{n}_mul", [P, D])
            load_all(nc, n, [
                (wl[:, :, :], I["L0_gnn_Wl"][layer].rearrange("(k p) n -> p k n", p=P)),
                (wr[:, :, :], I["L0_gnn_Wr"][layer].rearrange("(k p) n -> p k n", p=P)),
                *[(vecs[:, q, :], row(I[f"L0_gnn_{v}"][layer])) for q, v in enumerate(("b", "gamma", "beta", "rmean", "rvar"))]])
            s_link, s_var, s_root = (kk.sem(f"{n}_bn_{x}") for x in ("link", "var", "root"))
            with nc.Block() as block:

                @block.vector
                def _(dve):
                    v, st = nc.vector, Steps(dve, s_link)
                    v.tensor_scalar_add(vecs[:, 4, :], vecs[:, 4, :], EPS).then_inc(s_var, 1)
                    dve.wait_ge(s_root, 1)
                    st.link(v.reciprocal(mul[:, :], shift[:, :]))
                    st.link(v.tensor_tensor(mul[:, :], mul[:, :], vecs[:, 1, :], ALU.mult))
                    st.link(v.tensor_tensor(shift[:, :], vecs[:, 0, :], vecs[:, 3, :], ALU.subtract))
                    st.link(v.tensor_tensor(shift[:, :], shift[:, :], mul[:, :], ALU.mult))
                    v.tensor_tensor(shift[:, :], shift[:, :], vecs[:, 2, :], ALU.add)
                    for w in (wl, wr):
                        v.tensor_tensor(w[:, :, :], w[:, :, :], bc(mul[:, :].unsqueeze(1), [P, KD, D]), ALU.mult)

                @block.scalar
                def _(act):
                    act.wait_ge(s_var, 1)
                    nc.scalar.activation(shift[:, :], vecs[:, 4, :], ACT.Sqrt).then_inc(s_root, 1)

        U = 5
        part = k.sb(f"{n}_part", [P, U, 3, D], BF16)
        aggT = k.sb(f"{n}_aggT", [P, KD, 2048])
        h = k.sb(f"{n}_h", [P, 2, J2, D])
        z = k.sb(f"{n}_z", [P, 2, J2, D])
        aT = k.sb(f"{n}_aT", [P, KD, J2 * P])
        hT = k.sb(f"{n}_hT", [P, J2, KD, P])
        extra = k.sb(f"{n}_extra", [P, 2, J2, D])
        nxt = extra[:, :, :, :].rearrange("p a j d -> p (a j d)")[:, 0:J2 * 3 * D // 2].bitcast(BF16)\
            .rearrange("p (j q d) -> p j q d", j=J2, q=3)
        bank = k.ps(f"{n}_bank", [P, 8, 512])
        s_part = [k.sem(f"{n}_part{u}") for u in range(U)]
        s_h = [k.sem(f"{n}_hrow{s}") for s in range(2)]
        (s_mm, s_sum, s_evac_a, s_evac_v, s_turn, s_hT, s_aT, s_z, s_zused, s_new, s_save, s_saved, s_link) = (
            k.sem(f"{n}_{x}") for x in ("mm", "sum", "evac_a", "evac_v", "turn", "hT", "aT", "z", "zused", "new", "save",
                                        "saved", "link"))
        loads = 2 if final else 1
        stores = 1 if final else 2
        batches = [p[2] // J2 for p in PORTIONS]
        with nc.Block() as block:

            @block.sync
            def _(sp):
                def load(b, t0, s):
                    rows = h_table[bass.ds(t0 * P, J2 * P), :].rearrange("(j p) d -> p j d", p=P)
                    sp.dma_start(h[:, s, :, :], rows).then_inc(s_h[s], 16)
                    if final:
                        rows = x_dram[bass.ds(t0 * P, J2 * P), :].rearrange("(j p) d -> p j d", p=P)
                        sp.dma_start(extra[:, s, :, :], rows).then_inc(s_h[s], 16)

                def save(b, t0, s):
                    out = (out_table if final else h_table)[bass.ds(t0 * P, J2 * P), :].rearrange("(j p) d -> p j d", p=P)
                    ahead = None if final else next_parts[bass.ds(t0, J2), :, :].rearrange("t p f -> p t f")
                    sp.wait_ge(s_new, b + 1)
                    sp.dma_start(out, h[:, s, :, :]).then_inc(s_save, 16)
                    if not final:
                        sp.dma_start(ahead, nxt.rearrange("p j q d -> p j (q d)")).then_inc(s_save, 16)
                    sp.wait_ge(s_save, b * (16 * stores) + 16 * stores)
                    sp.sem_inc(s_saved, 1)

                b0 = t0 = 0
                for p, (_, _, tiles) in enumerate(PORTIONS):
                    with sp.Fori(0, NT // U) as i:
                        for u in range(U):
                            src = parts[bass.ds(i * U + u, 1), :, :].rearrange("a p f -> p (a f)")
                            sp.wait_ge(s_mm, i * U + u + p * NT + 1)
                            sp.dma_start(part[:, u, :, :].rearrange("p q d -> p (q d)"), src).then_inc(s_part[u], 16)
                    for s in range(2):
                        load(b0 + s, t0 + s * J2, s)
                    with sp.Fori(0, batches[p] // 2 - 1) as i:
                        for s in range(2):
                            b = 2 * i + s
                            save(b0 + b, t0 + b * J2, s)
                            load(b0 + b + 2, t0 + b * J2 + 2 * J2, s)
                    for s in range(2):
                        b = batches[p] - 2 + s
                        save(b0 + b, t0 + b * J2, s)
                    b0 += batches[p]
                    t0 += tiles

            @block.tensor
            def _(pe):
                pe.sem_inc(s_mm, U)
                b0 = 0
                for p, (col0, widths, _) in enumerate(PORTIONS):
                    nb = len(widths)
                    if p:
                        pe.wait_ge(s_zused, b0 + 2)
                    for b in range(2 * nb):
                        w = widths[b % nb]
                        nc.tensor.matmul(bank[:, b, 0:w], c.zero_b[:, 0:P], c.zero_b[:, 0:w], start=True, stop=False)
                    with pe.Fori(0, NT // U) as i:
                        for u in range(U):
                            pe.wait_ge(s_part[u], i * 16 + p * (NT // U) * 16 + 16)
                            for q in range(3):
                                for hf in range(KD):
                                    at = col0
                                    for b, w in enumerate(widths):
                                        last = nc.tensor.matmul(
                                            bank[:, hf * nb + b, 0:w], part[:, u, q, hf * P:(hf + 1) * P],
                                            m[:, bass.ds(i * U + u, 1), at:at + w].rearrange("p a w -> p (a w)"),
                                            start=False, stop=False)
                                        at += w
                            last.then_inc(s_mm, 1)
                    for b in range(2 * nb):
                        w = widths[b % nb]
                        last = nc.tensor.matmul(bank[:, b, 0:w], c.zero_b[:, 0:P], c.zero_b[:, 0:w], start=False, stop=True)
                    last.then_inc(s_sum, 1)
                    pe.wait_ge(s_evac_a, p + 1)
                    pe.wait_ge(s_evac_v, p + 1)
                    with pe.Fori(0, batches[p] // 2) as i:
                        for s in range(2):
                            b = 2 * i + s + b0
                            pe.wait_ge(s_h[s], i * (16 * loads) + (b0 // 2 + 1) * 16 * loads)
                            for j in range(J2):
                                for hf in range(KD):
                                    at = (j * KD + hf) * P
                                    last = nc.tensor.transpose(bank[:, s, at:at + P], h[:, s, j, hf * P:(hf + 1) * P], c.ident[:, :])
                            last.then_inc(s_turn, 1)
                            pe.wait_ge(s_zused, b + 1)
                            pe.wait_ge(s_hT, b + 1)
                            for j in range(J2):
                                for hf in range(KD):
                                    nc.tensor.matmul(bank[:, 2 + s, j * D:(j + 1) * D], hT[:, j, hf, :], wr[:, hf, :],
                                                     start=hf == 0, stop=hf == KD - 1)
                            pe.wait_ge(s_aT, b + 1)
                            for j in range(J2):
                                for hf in range(KD):
                                    last = nc.tensor.matmul(bank[:, 4 + s, j * D:(j + 1) * D], aT[:, hf, j * P:(j + 1) * P],
                                                            wl[:, hf, :], start=hf == 0, stop=hf == KD - 1)
                            last.then_inc(s_z, 1)
                    b0 += batches[p]

            @block.scalar
            def _(act):
                act.sem_inc(s_z, 1)
                b0 = 0
                for p, (_, widths, _) in enumerate(PORTIONS):
                    act.wait_ge(s_sum, p + 1)
                    at = 0
                    for b, w in enumerate(widths):
                        last = nc.scalar.activation(aggT[:, 0, at:at + w], bank[:, b, 0:w], ACT.Copy)
                        at += w
                    last.then_inc(s_evac_a, 1)
                    act.wait_ge(s_evac_a, p + 1)
                    act.wait_ge(s_evac_v, p + 1)
                    with act.Fori(0, batches[p] // 2) as i:
                        for s in range(2):
                            b = 2 * i + s + b0
                            act.wait_ge(s_turn, b + 1)
                            act.wait_ge(s_z, b + 1)
                            nc.scalar.activation(hT[:, :, :, :].rearrange("p j h c -> p (j h c)"), bank[:, s, :], ACT.Copy).then_inc(s_hT, 1)
                            nc.scalar.activation(aT[:, :, :], aggT[:, :, bass.ds((2 * i + s) * (J2 * P), J2 * P)], ACT.Copy).then_inc(s_aT, 1)
                    b0 += batches[p]

            @block.vector
            def _(dve):
                v, st = nc.vector, Steps(dve, s_link)
                dve.sem_inc(s_zused, 2)
                dve.sem_inc(s_saved, 1)
                b0 = t0 = 0
                for p, (_, widths, tiles) in enumerate(PORTIONS):
                    nb = len(widths)
                    dve.wait_ge(s_sum, p + 1)
                    at = 0
                    for b, w in enumerate(widths):
                        last = v.tensor_copy(aggT[:, 1, at:at + w], bank[:, nb + b, 0:w])
                        at += w
                    last.then_inc(s_evac_v, 1)
                    with dve.Fori(0, batches[p] // 2) as i, st.each(i, batches[p] // 2, 2 * (2 if final else 6)):
                        for s in range(2):
                            b = 2 * i + s + b0
                            dve.wait_ge(s_z, b + 2)
                            zs, hs = z[:, s, :, :], h[:, s, :, :]
                            st.link(v.tensor_tensor(zs, bank[:, 2 + s, :].rearrange("p (j d) -> p j d", d=D),
                                                    bc(shift[:, :].unsqueeze(1), [P, J2, D]), ALU.add))
                            for j in range(J2):
                                last = v.scalar_tensor_tensor(z[:, s, j, :], bank[:, 4 + s, j * D:(j + 1) * D],
                                                              c.rdeg[:, bass.ds((2 * i + s) * J2 + t0 + j, 1)], z[:, s, j, :],
                                                              ALU.mult, ALU.add)
                            last.then_inc(s_zused, 1)
                            dve.wait_ge(s_zused, b + 3)
                            if final:
                                st.link(v.tensor_tensor(zs, zs, hs, ALU.add))
                                v.tensor_tensor(hs, zs, extra[:, s, :, :], ALU.add).then_inc(s_new, 1)
                            else:
                                st.link(v.scalar_tensor_tensor(hs, zs, 0.0, hs, ALU.max, ALU.add))
                                dve.wait_ge(s_saved, b + 1)
                                split_rows(v, st, [nxt[:, :, q, :] for q in range(3)], hs, zs).then_inc(s_new, 1)
                    b0 += batches[p]
                    t0 += tiles


def relation_tables(nc, c, I, r_table):
    with Core(nc) as m:
        rel = m.sb("rel", [P, RT, W1])
        raw = m.sb("rel_raw", [P, RT, D])
        gw, gb = m.sb("rel_gw", [P, D]), m.sb("rel_gb", [P, 1])
        prod = m.sb("rel_prod", [P, RT, D])
        gate = m.sb("rel_gate", [P, RT])
        s_l, s_link, s_a, s_b, s_r, s_st = (m.sem(f"rel_{x}") for x in ("load", "link", "a", "b", "done", "st"))
        last_rel = RELATIONS - (RT - 1) * P
        with nc.Block() as block:

            @block.sync
            def _(sp):
                src = I["L1_gnn_relation_emb"]
                sp.wait_ge(s_a, 1)
                sp.dma_start(raw[:, 0:RT - 1, :], src[0:(RT - 1) * P, :].rearrange("(t p) d -> p t d", p=P)).then_inc(s_l, 16)
                sp.dma_start(raw[0:last_rel, RT - 1, :], src[(RT - 1) * P:RELATIONS, :]).then_inc(s_l, 16)
                sp.dma_start(gw[:, :], row(I["L1_gnn_gate_w"].rearrange("a n -> (a n)"))).then_inc(s_l, 16)
                sp.dma_start(gb[:, :], row(I["L1_gnn_gate_b"])).then_inc(s_l, 16)
                sp.wait_ge(s_r, 1)
                sp.dma_start(r_table.rearrange("(t p) d -> p t d", p=P), rel[:, :, :]).then_inc(s_st, 16)
                sp.wait_ge(s_st, 16)

            @block.vector
            def _(dve):
                v, st = nc.vector, Steps(dve, s_link)
                v.memset(rel[:, :, :], 0.0)
                v.memset(raw[:, :, :], 0.0).then_inc(s_a, 1)
                dve.wait_ge(s_l, 64)
                st.link(v.tensor_tensor(prod[:, :, :].rearrange("p t (b c) -> p t b c", b=4),
                                        raw[:, :, :].rearrange("p t (b c) -> p t b c", b=4),
                                        bc(gw[:, :].rearrange("p (c b) -> p b c", b=4).unsqueeze(1), [P, RT, 4, D // 4]), ALU.mult))
                st.link(v.tensor_reduce(gate[:, :], prod[:, :, :], AX.X, ALU.add))
                v.tensor_scalar(gate[:, :], gate[:, :], gb[:, 0:1], None, ALU.add).then_inc(s_a, 1)
                dve.wait_ge(s_b, 1)
                v.tensor_tensor(rel[:, :, 0:D], raw[:, :, :], bc(gate[:, :].unsqueeze(2), [P, RT, D]), ALU.mult)
                v.tensor_copy(rel[:, :, D], gate[:, :]).then_inc(s_r, 1)

            @block.scalar
            def _(act):
                act.wait_ge(s_a, 2)
                nc.scalar.activation(gate[:, :], gate[:, :], ACT.Sigmoid).then_inc(s_b, 1)


class RelationRows:

    def __init__(self, nc, c, k, name, edges, r_table, out, first, count):
        self.nc, self.edges, self.table, self.out, self.first, self.count = nc, edges, r_table, out, first, count
        assert count % 2 == 0
        self.kind = k.sb(f"{name}_kind", [P, 2, CH, 4], I32)
        self.buf = k.sb(f"{name}_buf", [P, 2, CH, W1])
        self.s_kind = [c.pool_sem(f"{name}_kind{s}") for s in range(2)]
        self.s_row = [c.pool_sem(f"{name}_row{s}") for s in range(2)]
        self.s_out = [c.pool_sem(f"{name}_out{s}") for s in range(2)]
        self.s_gate = k.sem(f"{name}_gate")

    def __call__(self, pool):
        by_edge = self.edges[0:EDGE_TILES * P, :].rearrange("(p k) c -> p k c", p=P)
        out = self.out[0:EDGE_TILES * P, :].rearrange("(p k) c -> p k c", p=P)

        def fetch(at, s):
            pool.dma_start(self.kind[:, s, :, :], by_edge[:, bass.ds(at * CH, CH), :]).then_inc(self.s_kind[s], 16)

        def gather(s, uses):
            pool.wait_ge(self.s_kind[s], uses * 16)
            pool.sem_inc(self.s_gate, 1)
            for g in range(CH):
                pool.indirect_dma_start(self.buf[:, s, g, :], None, self.table,
                                        bass.IndirectOffsetOnAxis(ap=self.kind[:, s, g, 2:3], axis=0)).then_inc(self.s_row[s], 16)

        def store(at, s, uses):
            pool.wait_ge(self.s_row[s], uses * (16 * CH))
            pool.sem_inc(self.s_gate, 1)
            pool.dma_start(out[:, bass.ds(at * CH, CH), :], self.buf[:, s, :, :]).then_inc(self.s_out[s], 16)

        f = self.first
        fetch(f, 0)
        fetch(f + 1, 1)
        gather(0, 1)
        gather(1, 1)
        with pool.Fori(0, self.count // 2 - 1) as i:
            for s in range(2):
                at = 2 * i + s + f
                store(at, s, i + 1)
                fetch(at + 2, s)
                pool.wait_ge(self.s_out[s], i * 16 + 16)
                pool.sem_inc(self.s_gate, 1)
                gather(s, i + 2)
        for s in range(2):
            store(f + self.count - 2 + s, s, self.count // 2)
        for s in range(2):
            pool.wait_ge(self.s_out[s], 16 * (self.count // 2))


def gnn0(nc, c, I, edges, r_table, relation_rows):
    h_table = c.dram("h_table", [NTP * P, D])
    x1 = c.dram("x1", [NTP * P, D])
    parts = [c.dram(f"parts{q}", [NTP, P, 3 * D], BF16) for q in range(2)]
    gnn0_start(nc, c, I, I["x"], h_table, parts[0])
    with Core(nc) as k:
        m = k.sb("matrix", [P, NT, MW], BF16)
        with Core(nc) as kk:
            c.tab["a_strip"] = kk.sb("a_strip", [P, GROUPS_A])
            c.tab["a_start"] = kk.sb("a_start", [1, GROUPS_A], I32)
            c.tab["a_col"] = kk.sb("a_col", [1, GROUPS_A + LAG_A], I32)
            s_t = kk.sem("a_tables")
            with nc.Block() as block:

                @block.sync
                def _(sp):
                    for t, d in ((c.tab["a_strip"], c.tab["a_strip_d"]), (c.tab["a_start"], c.tab["a_start_d"]), (c.tab["a_col"], c.tab["a_col_d"])):
                        sp.dma_start(t[:, :], d).then_inc(s_t, 16)
                    sp.wait_ge(s_t, 48)

            work = RelationRows(nc, c, kk, "rr", edges, r_table, relation_rows, 0, EDGE_TILES // CH)
            build_matrix(nc, c, c.records, m, work)
        node_degrees(nc, c, m)
        for layer in range(3):
            gnn0_layer(nc, c, I, layer, m, h_table, parts[layer % 2], parts[1 - layer % 2], I["x"], x1 if layer == 2 else None)
    return x1


def experts(nc, c, I, name, ne, nf, tiles, which, w1, b1, w2, b2, gate_w, gate_b, norm, act_fn, finish_rows):
    FC = nf // P
    xs = c.dram(f"{name}_xs", [(tiles + 1) * P, D])
    ys = c.dram(f"{name}_ys", [tiles * P, D])
    with Core(nc) as k:
        xn = k.sb(f"{name}_xn", [P, NT, D])
        layernorm(nc, c, f"{name}_ln", c.x, xn)
        gate = k.sb(f"{name}_gate", [P, KD, ne])
        gate_bias = k.sb(f"{name}_gate_bias", [P, ne])
        logits = k.sb(f"{name}_logits", [P, NT, ne])
        load_all(nc, f"{name}_g", [(gate[:, :, :], gate_w.rearrange("(k p) n -> p k n", p=P)),
                                   (gate_bias[:, :], row(gate_b))])

        def keep(v, st, t0, z):
            return v.tensor_tensor(logits[:, bass.ds(t0, J), :], z, bc(gate_bias[:, :].unsqueeze(1), [P, J, ne]), ALU.add)

        dense(nc, c, f"{name}_gd", [(xn, gate, None)], ne, keep, 0)
        weight = k.sb(f"{name}_weight", [P, 2, NT])
        slot = k.sb(f"{name}_slot", [P, 2, NT], I32)
        e_tab = k.sb(f"{name}_etab", [1, tiles], I32)
        route(nc, c, name, ne, tiles, which, logits, weight, slot, e_tab, xn, xs)
        run_experts(nc, c, name, ne, nf, FC, tiles, xs, ys, e_tab, w1, b1, w2, b2, norm, act_fn)
        combine(nc, c, name, ys, weight, slot, c.x if norm else xn, xn, finish_rows)


def route(nc, c, name, ne, tiles, softmax_first, logits, weight, slot, e_tab, xn, xs):
    with Core(nc) as k:
        top = k.sb(f"{name}_top", [P, NT, 8])
        idx = k.sb(f"{name}_idx", [P, NT, 8], U32)
        idx_f = k.sb(f"{name}_idx_f", [P, 2, NT])
        pick = k.sb(f"{name}_pick", [P, 2, NT, ne])
        both = k.sb(f"{name}_both", [P, NT, ne])
        place = k.sb(f"{name}_place", [P, NT, ne])
        sums = k.sb(f"{name}_sums", [P, NT + 1, ne])
        small = k.sb(f"{name}_small", [P, 4, NT])
        per = k.sb(f"{name}_per", [P, 6, ne])
        per_i = k.sb(f"{name}_per_i", [P, 2, ne], I32)
        done = k.sb(f"{name}_done", [1, tiles, ne])
        done_f = k.sb(f"{name}_done_f", [1, tiles])
        slot_f = k.sb(f"{name}_slot_f", [P, 2, NT])
        zero = k.sb(f"{name}_zero", [P, 2048])
        rank = k.ps(f"{name}_rank", [P, 512])
        total = k.ps(f"{name}_total", [P, 512])
        s_link, s_a, s_b, s_m, s_rank, s_slot, s_z, s_zd = (
            k.sem(f"{name}_r{x}") for x in ("link", "to_act", "to_dve", "both", "rank", "slot", "zero", "zeroed"))
        s_sc = c.pool_sem(f"{name}_scatter")
        wide = [P, NT, ne]
        rows_total = (tiles + 1) * P * D
        with nc.Block() as block:

            @block.vector
            def _(dve):
                v, st = nc.vector, Steps(dve, s_link)
                v.memset(zero[:, :], 0.0).then_inc(s_z, 1)
                if softmax_first:
                    st.link(v.tensor_reduce(small[:, 0, :], logits[:, :, :], AX.X, ALU.max))
                    v.tensor_tensor(logits[:, :, :], logits[:, :, :], bc(small[:, 0, :].unsqueeze(2), wide), ALU.subtract)\
                        .then_inc(s_a, 1)
                    dve.wait_ge(s_b, 1)
                    st.link(v.tensor_reduce(small[:, 1, :], logits[:, :, :], AX.X, ALU.add))
                    st.link(v.reciprocal(small[:, 2, :], small[:, 1, :]))
                    st.link(v.tensor_tensor(logits[:, :, :], logits[:, :, :], bc(small[:, 2, :].unsqueeze(2), wide), ALU.mult))
                for t in range(NT):
                    last = v.max(top[:, t, :], logits[:, t, :])
                st.link(last)
                for t in range(NT):
                    last = v.max_index(idx[:, t, :], top[:, t, :], logits[:, t, :])
                st.link(last)
                if softmax_first:
                    st.link(v.tensor_tensor(small[:, 0, :], top[:, :, 0], top[:, :, 1], ALU.add))
                    st.link(v.reciprocal(small[:, 1, :], small[:, 0, :]))
                    for q in range(2):
                        v.tensor_tensor(weight[:, q, :], top[:, :, q], small[:, 1, :], ALU.mult)
                else:
                    v.tensor_tensor(small[:, 0, :], top[:, :, 1], top[:, :, 0], ALU.subtract).then_inc(s_a, 1)
                    dve.wait_ge(s_b, 1)
                    st.link(v.tensor_scalar_add(small[:, 2, :], small[:, 1, :], 1.0))
                    st.link(v.reciprocal(weight[:, 0, :], small[:, 2, :]))
                    v.tensor_tensor(weight[:, 1, :], weight[:, 0, :], small[:, 1, :], ALU.mult)
                for q in range(2):
                    last = v.tensor_copy(idx_f[:, q, :], idx[:, :, q])
                st.link(last)
                for q in range(2):
                    last = v.tensor_tensor(pick[:, q, :, :], bc(c.iota[:, 0:ne].unsqueeze(1), wide),
                                           bc(idx_f[:, q, :].unsqueeze(2), wide), ALU.is_equal)
                st.link(last)
                st.link(v.tensor_tensor(both[:, :, :], pick[:, 0, :, :], pick[:, 1, :, :], ALU.add))
                v.tensor_scalar(both[:, NT - 1, :], both[:, NT - 1, :], c.alive[:, 0:1], None, ALU.mult).then_inc(s_m, 1)
                dve.wait_ge(s_rank, 1)
                st.link(v.memset(sums[:, 0, :], 0.0))
                for t in range(NT):
                    st.link(v.tensor_tensor(sums[:, t + 1, :], sums[:, t, :], total[:, t * ne:(t + 1) * ne], ALU.add))
                st.link(v.tensor_copy(per[:, 0, :], sums[:, NT, :]))
                group_table(v, st, per, per_i, ne, P)
                st.link(v.tensor_tensor(place[:, :, :], rank[:, 0:NT * ne].rearrange("p (t e) -> p t e", e=ne), sums[:, 0:NT, :], ALU.add))
                st.link(v.tensor_tensor(place[:, :, :], place[:, :, :], bc(per[:, 5, :].unsqueeze(1), wide), ALU.add))
                for q in range(2):
                    last = v.tensor_tensor(pick[:, q, :, :], pick[:, q, :, :], place[:, :, :], ALU.mult)
                st.link(last)
                st.link(v.tensor_reduce(slot_f[:, :, :], pick[:, :, :, :], AX.X, ALU.add))
                v.tensor_copy(slot[:, :, :], slot_f[:, :, :]).then_inc(s_slot, 1)
                st.link(v.tensor_tensor(done[:, :, :], bc(c.iota[0:1, 0:tiles].unsqueeze(2), [1, tiles, ne]),
                                        bc(per[0:1, 3, :].unsqueeze(1), [1, tiles, ne]), ALU.is_ge))
                st.link(v.tensor_reduce(done_f[:, :], done[:, :, :], AX.X, ALU.add))
                st.link(v.tensor_scalar_min(done_f[:, :], done_f[:, :], float(ne - 1)))
                v.tensor_copy(e_tab[:, :], done_f[:, :])

            @block.scalar
            def _(act):
                act.wait_ge(s_a, 1)
                if softmax_first:
                    nc.scalar.activation(logits[:, :, :], logits[:, :, :], ACT.Exp).then_inc(s_b, 1)
                else:
                    nc.scalar.activation(small[:, 1, :], small[:, 0, :], ACT.Exp).then_inc(s_b, 1)

            @block.tensor
            def _(pe):
                pe.wait_ge(s_m, 1)
                flat = both[:, :, :].rearrange("p t e -> p (t e)")
                nc.tensor.matmul(rank[:, 0:NT * ne], c.before[:, :], flat, start=True, stop=True)
                nc.tensor.matmul(total[:, 0:NT * ne], c.ones[:, :], flat, start=True, stop=True).then_inc(s_rank, 1)

            @block.sync
            def _(sp):
                sp.wait_ge(s_z, 1)
                view = xs.rearrange("(p a) d -> p (a d)", p=P)
                n, at = rows_total // P, 0
                for at in range(0, n, 2048):
                    w = min(2048, n - at)
                    sp.dma_start(view[:, at:at + w], zero[:, 0:w]).then_inc(s_zd, 16)

            @block.gpsimd
            def _(pool):
                pool.wait_ge(s_zd, 16 * -(-(rows_total // P) // 2048))
                pool.wait_ge(s_slot, 1)
                for t in range(NT):
                    n = P if t < NT - 1 else TAIL
                    for q in range(2):
                        pool.indirect_dma_start(xs, bass.IndirectOffsetOnAxis(ap=slot[0:n, q, t:t + 1], axis=0),
                                                xn[0:n, t, :], None).then_inc(s_sc, 16)
                pool.wait_ge(s_sc, 16 * 2 * NT)


def run_experts(nc, c, name, ne, nf, FC, tiles, xs, ys, e_tab, w1, b1, w2, b2, norm, act_fn):
    with Core(nc) as k:
        w1b = k.sb(f"{name}_w1", [P, 2, KD, nf])
        w2b = k.sb(f"{name}_w2", [P, 2, FC, D])
        xb = k.sb(f"{name}_xb", [P, 2, D])
        xT = k.sb(f"{name}_xT", [P, 2, KD, P])
        hT = k.sb(f"{name}_hT", [P, 2, FC, P])
        yb = k.sb(f"{name}_yb", [P, 2, D])
        b1s = k.sb(f"{name}_b1", [P, ne, FC])
        b2s = k.sb(f"{name}_b2", [P, ne, D])
        pX = [k.ps(f"{name}_pX{s}", [P, 512]) for s in range(2)]
        pH = [k.ps(f"{name}_pH{s}", [P, max(nf, 512)]) for s in range(2)]
        pY = [k.ps(f"{name}_pY{s}", [P, 512]) for s in range(2)]
        loads = [(b1s[:, :, :], b1), (b2s[:, :, :], b2.rearrange("(a e) d -> a e d", a=1).to_broadcast([P, ne, D]))]
        if norm:
            lg, lb = k.sb(f"{name}_lg", [P, ne, KD]), k.sb(f"{name}_lb", [P, ne, KD])
            loads += [(lg[:, :, :], norm[0]), (lb[:, :, :], norm[1])]
        load_all(nc, f"{name}_b", loads)
        s_w1 = [k.sem(f"{name}_w1_{s}") for s in range(2)]
        s_w2 = [k.sem(f"{name}_w2_{s}") for s in range(2)]
        s_x = [k.sem(f"{name}_x{s}") for s in range(2)]
        s_st = [c.pool_sem(f"{name}_st{s}") for s in range(2)]
        s_xt, s_xT, s_h, s_hT, s_y, s_yb, s_yfree, s_gate = (
            k.sem(f"{name}_e{x}") for x in ("xt", "xT", "h", "hT", "y", "yb", "yfree", "gate"))
        BF = 512 // P
        HB = FC // BF
        with nc.Block() as block:

            @block.sync
            def _(sp):
                sp.dma_start(xb[:, 0, :], xs[0:P, :]).then_inc(s_x[0], 16)
                with sp.Fori(0, tiles // 2) as i:
                    for s in range(2):
                        t = 2 * i + s
                        e = sp.value_load(e_tab[0:1, bass.ds(t, 1)], min_val=0, max_val=ne - 1)
                        a1 = w1[bass.ds(e, 1), :, :].rearrange("a (k p) f -> p (a k) f", p=P)
                        a2 = w2[bass.ds(e, 1), :, :].rearrange("a (k p) f -> p (a k) f", p=P)
                        ax = xs[bass.ds(t * P + P, P), :]
                        sp.wait_ge(s_h, t * HB + HB)
                        sp.dma_start(w1b[:, s, :, :], a1).then_inc(s_w1[s], 16)
                        sp.wait_ge(s_xt, t + 1)
                        sp.dma_start(xb[:, 1 - s, :], ax).then_inc(s_x[1 - s], 16)
                        sp.wait_ge(s_y, t + 1)
                        sp.dma_start(w2b[:, s, :, :], a2).then_inc(s_w2[s], 16)

            @block.tensor
            def _(pe):
                def turn(t, s, u):
                    pe.wait_ge(s_x[s], u * 16)
                    for h in range(KD):
                        last = nc.tensor.transpose(pX[s][:, h * P:(h + 1) * P], xb[:, s, h * P:(h + 1) * P], c.ident[:, :])
                    last.then_inc(s_xt, 1)

                def hidden(t, s, u):
                    pe.wait_ge(s_w1[s], u * 16)
                    pe.wait_ge(s_xT, t + 1)
                    for f in range(FC):
                        for h in range(KD):
                            last = nc.tensor.matmul(pH[s][:, f * P:(f + 1) * P], w1b[:, s, h, f * P:(f + 1) * P],
                                                    xT[:, s, h, :], start=h == 0, stop=h == KD - 1)
                        if f % BF == BF - 1:
                            last.then_inc(s_h, 1)

                def result(t, s, u):
                    pe.wait_ge(s_w2[s], u * 16)
                    pe.wait_ge(s_yb, t + 1)
                    for f in range(FC):
                        pe.wait_ge(s_hT, t * FC + f + 1)
                        last = nc.tensor.matmul(pY[s][:, 0:D], hT[:, s, f, :], w2b[:, s, f, :], start=f == 0, stop=f == FC - 1)
                    last.then_inc(s_y, 1)

                pe.sem_inc(s_xt, 1)
                pe.sem_inc(s_h, 2 * HB)
                pe.sem_inc(s_y, 2)
                turn(0, 0, 1)
                hidden(0, 0, 1)
                turn(1, 1, 1)
                with pe.Fori(0, tiles // 2 - 1) as i:
                    t = 2 * i
                    hidden(t + 1, 1, i + 1)
                    turn(t + 2, 0, i + 2)
                    result(t, 0, i + 1)
                    hidden(t + 2, 0, i + 2)
                    turn(t + 3, 1, i + 2)
                    result(t + 1, 1, i + 1)
                hidden(tiles - 1, 1, tiles // 2)
                turn(tiles, 0, tiles // 2 + 1)
                result(tiles - 2, 0, tiles // 2)
                result(tiles - 1, 1, tiles // 2)

            @block.scalar
            def _(act):
                with act.Fori(0, tiles // 2) as i:
                    for s in range(2):
                        t = 2 * i + s
                        e = act.value_load(e_tab[0:1, bass.ds(t, 1)], min_val=0, max_val=ne - 1)
                        act.wait_ge(s_xt, t + 2)
                        for h in range(KD):
                            src = pX[s][:, h * P:(h + 1) * P]
                            if norm:
                                last = nc.scalar.activation(xT[:, s, h, :], src, ACT.Identity, bias=lb[:, bass.ds(e, 1), h],
                                                            scale=lg[:, bass.ds(e, 1), h])
                            else:
                                last = nc.scalar.activation(xT[:, s, h, :], src, ACT.Copy)
                        last.then_inc(s_xT, 1)
                        for f in range(FC):
                            if f % BF == 0:
                                act.wait_ge(s_h, t * HB + f // BF + 1 + 2 * HB)
                            nc.scalar.activation(hT[:, s, f, :], pH[s][:, f * P:(f + 1) * P], act_fn,
                                                 bias=b1s[:, bass.ds(e, 1), f]).then_inc(s_hT, 1)

            @block.vector
            def _(dve):
                dve.sem_inc(s_yb, 2)
                with dve.Fori(0, tiles // 2) as i:
                    for s in range(2):
                        t = 2 * i + s
                        e = dve.value_load(e_tab[0:1, bass.ds(t, 1)], min_val=0, max_val=ne - 1)
                        dve.wait_ge(s_y, t + 3)
                        dve.wait_ge(s_yfree, t + 1)
                        nc.vector.tensor_tensor(yb[:, s, :], pY[s][:, 0:D], b2s[:, bass.ds(e, 1), :].rearrange("p a d -> p (a d)"), ALU.add)\
                            .then_inc(s_yb, 1)

            @block.gpsimd
            def _(pool):
                pool.sem_inc(s_yfree, 2)
                with pool.Fori(0, tiles // 2) as i:
                    for s in range(2):
                        t = 2 * i + s
                        pool.wait_ge(s_yb, t + 3)
                        pool.sem_inc(s_gate, 1)
                        pool.dma_start(ys[bass.ds(t * P, P), :], yb[:, s, :]).then_inc(s_st[s], 16)
                        pool.wait_ge(s_st[s], i * 16 + 16)
                        pool.sem_inc(s_yfree, 1)


def combine(nc, c, name, ys, weight, slot, base, xn, finish_rows):
    with Core(nc) as k:
        got = k.sb(f"{name}_got", [P, 2, NT, D])
        s_got, s_done = c.pool_sem(f"{name}_cgot"), k.sem(f"{name}_cdone")
        with nc.Block() as block:

            @block.gpsimd
            def _(pool):
                for q in range(2):
                    for t in range(NT):
                        n = P if t < NT - 1 else TAIL
                        pool.indirect_dma_start(got[0:n, q, t, :], None, ys,
                                                bass.IndirectOffsetOnAxis(ap=slot[0:n, q, t:t + 1], axis=0)).then_inc(s_got, 16)

            @block.vector
            def _(dve):
                v = nc.vector
                start = TAIL // 32 * 32
                dve.wait_ge(s_got, 16 * 2 * NT)
                wide = [P, NT, D]
                v.tensor_tensor(got[:, 0, 0:NT - 1, :], got[:, 0, 0:NT - 1, :], bc(weight[:, 0, 0:NT - 1].unsqueeze(2), [P, NT - 1, D]), ALU.mult)
                v.tensor_tensor(got[0:TAIL, 0, NT - 1, :], got[0:TAIL, 0, NT - 1, :], bc(weight[0:TAIL, 0, NT - 1:NT], [TAIL, D]), ALU.mult)
                v.tensor_tensor(got[:, 1, 0:NT - 1, :], got[:, 1, 0:NT - 1, :], bc(weight[:, 1, 0:NT - 1].unsqueeze(2), [P, NT - 1, D]), ALU.mult)
                v.tensor_tensor(got[0:TAIL, 1, NT - 1, :], got[0:TAIL, 1, NT - 1, :], bc(weight[0:TAIL, 1, NT - 1:NT], [TAIL, D]), ALU.mult).then_inc(s_done, 1)
                dve.wait_ge(s_done, 1)
                for n, a, b in ((P, 0, NT - 1), (TAIL, NT - 1, NT)):
                    last = v.tensor_tensor(got[0:n, 0, a:b, :], got[0:n, 0, a:b, :], got[0:n, 1, a:b, :], ALU.add)
                last.then_inc(s_done, 1)
                dve.wait_ge(s_done, 2)
                for n, a, b in ((P, 0, NT - 1), (TAIL, NT - 1, NT)):
                    v.tensor_tensor(xn[0:n, a:b, :], base[0:n, a:b, :], got[0:n, 0, a:b, :], ALU.add)
        finish_rows(xn)


def clifford(nc, c, name, w, bias, out, bias_out, split):
    C = D // 4
    table = ((0, 1, 2, -3), (1, 0, -3, 2), (2, 3, 0, -1), (3, 2, 1, 0))
    with Core(nc) as k:
        raw = k.sb(f"{name}_raw", [P, KD, 4, C])
        raw_b = k.sb(f"{name}_raw_b", [P, D])
        s_l = k.sem(f"{name}_load")
        with nc.Block() as block:

            @block.sync
            def _(sp):
                for bo in range(4):
                    for bi in range(4):
                        at = (bi % 2) * C
                        sp.dma_start(raw[at:at + C, bi // 2, bo, :], w[abs(table[bo][bi])]).then_inc(s_l, 16)
                sp.dma_start(raw_b[:, :], row(bias)).then_inc(s_l, 16)

            @block.vector
            def _(dve):
                dve.wait_ge(s_l, 16 * 17)
                v = nc.vector
                for h in range(KD):
                    view = out[:, h, :]
                    view = view.rearrange("p (c b) -> p b c", b=4) if split else view.rearrange("p (b c) -> p b c", b=4)
                    for bo in range(4):
                        for half in range(2):
                            at = half * C
                            sign = -1.0 if table[bo][2 * h + half] < 0 else 1.0
                            v.tensor_scalar_mul(view[at:at + C, bo, :], raw[at:at + C, h, bo, :], sign)
                b = bias_out[:, :].rearrange("p (c b) -> p b c", b=4) if split else bias_out[:, :].rearrange("p (b c) -> p b c", b=4)
                v.tensor_copy(b, raw_b[:, :].rearrange("p (b c) -> p b c", b=4))


def gnn1(nc, c, I, edges, relation_rows):
    h_table = c.dram("h1_table", [NP, W1])
    with Core(nc) as k:
        h = k.sb("h1", [P, NT, D])
        layernorm(nc, c, "ln1", c.x, h)
        with Core(nc) as m:
            out = m.sb("h1_out", [P, NT, W1])
            s_h, s_st = m.sem("h1_scaled"), m.sem("h1_saved")
            with nc.Block() as block:

                @block.sync
                def _(sp):
                    sp.wait_ge(s_h, 2)
                    sp.dma_start(h_table.rearrange("(t p) d -> p t d", p=P), out[:, :, :]).then_inc(s_st, 16)
                    sp.wait_ge(s_st, 16)

                @block.vector
                def _(dve):
                    v = nc.vector
                    v.memset(out[:, :, D:W1], 0.0).then_inc(s_h, 1)
                    v.tensor_tensor(out[:, :, 0:D], h[:, :, :], bc(c.norm_src[:, :].unsqueeze(2), [P, NT, D]), ALU.mult)
                    dve.wait_ge(s_h, 1)
                    v.tensor_copy(out[:, :, D], c.norm_src[:, :]).then_inc(s_h, 1)

        acc = k.sb("acc1", [P, NT + 1, D + 1])
        aggregate(nc, c, "agg_r", edges, h_table, W1, acc, relation_rows)
        wm, bm = k.sb("msg", [P, KD, D]), k.sb("msg_bias", [P, D])
        wu, bu = k.sb("upd", [P, KD, D]), k.sb("upd_bias", [P, D])
        tmp = k.sb("g1_tmp", [P, J, D])
        weighted = k.sb("g1_weighted", [P, NT])
        clifford(nc, c, "cm", I["L1_gnn_msg_w"], I["L1_gnn_msg_b"].rearrange("b c -> (b c)"), wm, bm, False)
        clifford(nc, c, "cu", I["L1_gnn_upd_w"], I["L1_gnn_upd_b"].rearrange("b c -> (b c)"), wu, bu, True)

        with nc.Block() as block:

            @block.vector
            def _(dve):
                nc.vector.tensor_tensor(weighted[:, :], acc[:, 0:NT, D], c.norm_dst[:, :], ALU.mult)

        def messages(v, st, t0, z):
            wide = [P, J, D]
            now = h[:, bass.ds(t0, J), :]
            flat = now.rearrange("p j d -> p (j d)")
            st.link(v.tensor_tensor(tmp[:, :, :], bc(bm[:, :].unsqueeze(1), wide),
                                    bc(weighted[:, bass.ds(t0, J)].unsqueeze(2), wide), ALU.mult))
            st.link(v.tensor_tensor(tmp[:, :, :], tmp[:, :, :], z, ALU.add))
            return v.tensor_tensor(flat, flat, tmp[:, :, :].rearrange("p j d -> p (j d)"), ALU.add)

        dense(nc, c, "msgs", [(acc, wm, c.norm_dst)], D, messages, 2)

        def update(v, st, t0, z):
            wide = [P, J, D]
            out = c.x[:, bass.ds(t0, J), :].rearrange("p j d -> p (j d)")
            st.link(v.tensor_tensor(tmp[:, :, :], z, bc(bu[:, :].unsqueeze(1), wide), ALU.add))
            return v.tensor_tensor(out, out, tmp[:, :, :].rearrange("p j d -> p (j d)"), ALU.add)

        dense(nc, c, "updg", [(h, wu, None)], D, update, 1)


def build(nc, I, out):
    with Core(nc) as c:
        c.rdeg = c.sb("rdeg", [P, NTP])
        c.norm_src, c.norm_dst = c.sb("norm_src", [P, NT]), c.sb("norm_dst", [P, NT])
        c.alive = c.sb("alive", [P, 1])
        c.zero_b = c.sb("zero_b", [P, 512], BF16)
        c.records = c.dram("records", [EDGE_ROWS, 4])
        relation_rows = c.dram("relation_rows", [EDGE_ROWS, W1])
        r_table = c.dram("r1_table", [RT * P, W1])
        edges = I["edges"]
        constants(nc, c)
        s_al, s_none, s_tail = c.sem("alive_set"), c.sem("none_set"), c.sem("tail_saved")
        tables = {"a_strip": ([P, GROUPS_A], F32), "a_start": ([1, GROUPS_A], I32), "a_col": ([1, GROUPS_A + LAG_A], I32),
                  "g_base": ([P, GROUPS], F32), "g_start": ([1, GROUPS], I32), "g_tile": ([1, GROUPS + 1], I32)}
        c.tab = {}
        for name, (shape, dt) in tables.items():
            c.tab[name + "_d"] = c.dram(name + "_d", shape, dt)
        relation_tables(nc, c, I, r_table)
        with Core(nc) as k:
            none = k.sb("none_rows", [P, 8, W1])
            for name, (shape, dt) in tables.items():
                c.tab[name] = k.sb(name + "_work", shape, dt)
            with nc.Block() as block:

                @block.vector
                def _(dve):
                    nc.vector.memset(none[:, :, :], 0.0).then_inc(s_none, 1)
                    nc.vector.memset(c.zero_b[:, :], 0.0)

                @block.gpsimd
                def _(pool):
                    pool.memset(c.alive[:, :], 1.0).then_inc(s_al, 1)
                    pool.wait_ge(s_al, 1)
                    pool.affine_select(out=c.alive[:, :], in_=c.alive[:, :], compare_op=ALU.is_gt, fill=0.0,
                                       base=TAIL, pattern=[[0, 1]], channel_multiplier=-1)

                @block.sync
                def _(sp):
                    sp.wait_ge(s_none, 1)
                    sp.dma_start(relation_rows[EDGE_TILES * P:EDGE_ROWS, :].rearrange("(p k) c -> p k c", p=P), none[:, :, :])\
                        .then_inc(s_tail, 16)
                    sp.wait_ge(s_tail, 16)

            prepare_edges(nc, c, edges, c.records)
            s_tab = k.sem("tables_saved")
            with nc.Block() as block:

                @block.sync
                def _(sp):
                    for name in tables:
                        sp.dma_start(c.tab[name + "_d"], c.tab[name][:, :]).then_inc(s_tab, 16)
                    sp.wait_ge(s_tab, 16 * len(tables))

        x1 = gnn0(nc, c, I, edges, r_table, relation_rows)
        c.x = c.sb("x", [P, NT, D])
        for name in ("g_base", "g_start", "g_tile"):
            c.tab[name] = c.sb(name, *tables[name])
        load_all(nc, "again", [(c.x[:, :, :], x1[0:NP, :].rearrange("(t p) d -> p t d", p=P)),
                               *[(c.tab[n][:, :], c.tab[n + "_d"]) for n in ("g_base", "g_start", "g_tile")]])

        def norm_and_add(y):
            with Core(nc) as m:
                g, b = m.sb("ffn0_gamma", [P, D]), m.sb("ffn0_beta", [P, D])
                load_all(nc, "ffn0_gb", [(g[:, :], row(I["L0_ffn_gamma"])), (b[:, :], row(I["L0_ffn_beta"]))])
                layernorm(nc, c, "ln_y", y, y)
                s_link = m.sem("ffn0_link")
                with nc.Block() as block:

                    @block.vector
                    def _(dve):
                        v, st = nc.vector, Steps(dve, s_link)
                        wide = [P, NT, D]
                        st.link(v.tensor_tensor(y[:, :, :], y[:, :, :], bc(g[:, :].unsqueeze(1), wide), ALU.mult))
                        st.link(v.tensor_tensor(y[:, :, :], y[:, :, :], bc(b[:, :].unsqueeze(1), wide), ALU.add))
                        v.tensor_tensor(c.x[:, :, :], c.x[:, :, :], y[:, :, :], ALU.add)

        experts(nc, c, I, "f0", E0, F0, TILES0, False, I["L0_ffn_w1"], I["L0_ffn_b1"], I["L0_ffn_w2"], I["L0_ffn_b2"],
                I["L0_ffn_gate_w"], I["L0_ffn_gate_b"], None, ACT.Relu, norm_and_add)
        gnn1(nc, c, I, edges, relation_rows)

        def store(y):
            with Core(nc) as inner:
                s_out = inner.sem("stored")
                with nc.Block() as block:

                    @block.sync
                    def _(sp):
                        full = (NT - 1) * P
                        sp.dma_start(out[0:full, :].rearrange("(t p) d -> p t d", p=P), y[:, 0:NT - 1, :]).then_inc(s_out, 16)
                        sp.dma_start(out[full:N, :], y[0:TAIL, NT - 1, :]).then_inc(s_out, 16)
                        sp.wait_ge(s_out, 32)

        experts(nc, c, I, "f1", E1, F1, TILES1, True, I["L1_ffn_W1"], I["L1_ffn_b1"], I["L1_ffn_W2"], I["L1_ffn_b2"],
                I["L1_ffn_Wr"], I["L1_ffn_br"], (I["L1_ffn_ln_g"], I["L1_ffn_ln_b"]), ACT.Gelu, store)


def kernel(**inputs):
    import concourse.bacc as _bacc
    from concourse.bass_utils import run_bass_kernel_spmd as _run

    nc = _bacc.Bacc("TRN2", target_bir_lowering=False, num_devices=1)
    arrays = {}
    edges = np.zeros((EDGE_ROWS, 4), np.int32)
    edges[:, 1] = edges[:, 3] = NOWHERE
    for col, name in ((0, "src"), (1, "dst"), (2, "edge_type_500"), (3, "src")):
        edges[:E, col] = np.asarray(inputs[name])
    arrays["edges"] = edges
    for name, a in inputs.items():
        a = np.asarray(a)
        if name in ("src", "dst", "edge_type_500"):
            continue
        if name in ("L0_ffn_b1", "L1_ffn_b1", "L1_ffn_ln_g", "L1_ffn_ln_b"):
            a = a.reshape(a.shape[0], -1, P).transpose(2, 0, 1)
        if name in ("L1_gnn_msg_w", "L1_gnn_upd_w"):
            a = a.transpose(0, 2, 1)
        if name == "x":
            a = np.concatenate([a, np.zeros((NTP * P - N, D), a.dtype)])
        arrays[name] = np.ascontiguousarray(a)
    args = {n: nc.dram_tensor(f"in_{n}", a.shape, mybir.dt.from_np(a.dtype), kind="ExternalInput").ap() for n, a in arrays.items()}
    out = nc.dram_tensor("out_0", (N, D), F32, kind="ExternalOutput").ap()
    build(nc, args, out)
    r = _run(nc, [{f"in_{n}": a for n, a in arrays.items()}], core_ids=[0])
    return r.results[0]["out_0"]
```

```python
from contextlib import ExitStack, contextmanager

import numpy as np

import concourse.bass as bass
from concourse import mybir

ALU = mybir.AluOpType
ACT = mybir.ActivationFunctionType
AX = mybir.AxisListType
F32 = mybir.dt.float32
BF16 = mybir.dt.bfloat16
I32 = mybir.dt.int32
I16 = mybir.dt.int16
U32 = mybir.dt.uint32

P = 128
N, E, D = 3125, 103125, 256
NT = -(-N // P)
TAIL = N - (NT - 1) * P
NP = NT * P
KD = D // P
J = 5
NJ = NT // J
EPS = 1e-5

EDGE_TILES = -(-E // (4 * P)) * 4
EDGE_ROWS = EDGE_TILES * P + 1024
NOWHERE = 1 << 20
RING = 8


def groups_for(classes, size):
    return -(-((E + classes * (size - 1)) // size) // RING) * RING


G = 2
GE = G * P
GROUPS = groups_for(NT, GE)
SW = 32
STRIPS = -(-N // SW)
GA = 2
GAE = GA * P
GROUPS_A = groups_for(STRIPS, GAE)
CODES = NT * SW
ND = STRIPS * SW
NCH = 7
DC = ND // NCH
STREAMS = 4
LARGEST = (GROUPS_A // STREAMS - 4) * GAE
assert GROUPS_A % STREAMS == 0
assert GROUPS_A - E // GAE < GROUPS_A // STREAMS
assert NCH * DC == ND and DC <= 512 and CODES // 2 <= 512 and GROUPS_A <= 512

E0, F0, TILES0 = 16, 512, (2 * N + 16 * (P - 1)) // P
E1, F1, TILES1 = 8, 1024, (2 * N + 8 * (P - 1)) // P
TILES0 += TILES0 % 2
TILES1 += TILES1 % 2
RELATIONS = 500
RT = -(-RELATIONS // P)
NTP = 28
PORTIONS = ((0, (512, 512, 512, 512), 16), (2048, (384, 384, 352), 12))
MW = 3168
SHARES = (384, 144, 140, 140)
assert sum(SHARES) == EDGE_TILES
J2 = 2
W1 = 260


class Steps:

    def __init__(self, engine, sem):
        self.engine, self.sem, self.base, self.n = engine, sem, 0, 0

    def link(self, instruction):
        instruction.then_inc(self.sem, 1)
        self.n += 1
        self.engine.wait_ge(self.sem, self.base + self.n)
        return instruction

    @contextmanager
    def each(self, i, count, steps):
        start, self.base, self.n = self.base + self.n, self.base + self.n + i * steps, 0
        yield
        assert self.n == steps, (self.n, steps)
        self.base, self.n = start + count * steps, 0


class Core:

    def __init__(self, nc):
        self.nc, self.ctx, self.sems = nc, ExitStack(), []

    def __enter__(self):
        return self

    def __exit__(self, kind, *_):
        if kind is None and self.sems:
            with self.nc.Block() as block:

                @block.gpsimd
                def _(pool):
                    for sem in self.sems:
                        pool.sem_clear(sem)

        self.ctx.close()

    def sb(self, name, shape, dt=F32):
        return self.ctx.enter_context(self.nc.sbuf_tensor(name, shape, dt))

    def ps(self, name, shape, dt=F32):
        return self.ctx.enter_context(self.nc.psum_tensor(name, shape, dt))

    def sem(self, name):
        self.sems.append(self.ctx.enter_context(self.nc.semaphore(name)))
        return self.sems[-1]

    def pool_sem(self, name):
        return self.ctx.enter_context(self.nc.semaphore(name))

    def dram(self, name, shape, dt=F32):
        return self.nc.dram_tensor(name, shape, dt).ap()


def bc(ap, shape):
    return ap.to_broadcast(shape)


def constants(nc, c):
    c.ident = c.sb("ident", [P, P])
    c.ones = c.sb("ones", [P, P])
    c.before = c.sb("before", [P, P])
    c.iota = c.sb("iota", [P, P])
    c.ident_b = c.sb("ident_b", [P, P], BF16)
    with Core(nc) as k:
        iota_i = k.sb("iota_i", [P, P], I32)
        constants_set(nc, c, iota_i, k.sem("const_set"), k.sem("const_iota"))


def constants_set(nc, c, iota_i, s_set, s_iota):
    with nc.Block() as block:

        @block.gpsimd
        def _(pool):
            pool.memset(c.ident[:, :], 0.0).then_inc(s_set, 1)
            pool.memset(c.ones[:, :], 1.0).then_inc(s_set, 1)
            pool.memset(c.before[:, :], 1.0).then_inc(s_set, 1)
            pool.iota(iota_i[:, :], pattern=[[1, P]], base=0, channel_multiplier=0).then_inc(s_iota, 1)
            pool.wait_ge(s_set, 3)
            pool.affine_select(out=c.ident[:, :], in_=c.ident[:, :], compare_op=ALU.not_equal, fill=1.0,
                               base=0, pattern=[[-1, P]], channel_multiplier=1).then_inc(s_iota, 1)
            pool.affine_select(out=c.before[:, :], in_=c.before[:, :], compare_op=ALU.is_gt, fill=0.0,
                               base=0, pattern=[[1, P]], channel_multiplier=-1)

        @block.vector
        def _(dve):
            dve.wait_ge(s_iota, 1)
            nc.vector.tensor_copy(c.iota[:, :], iota_i[:, :])
            dve.wait_ge(s_iota, 2)
            nc.vector.tensor_copy(c.ident_b[:, :], c.ident[:, :])


def load_rows(dma, sem, dst, dram):
    full = (NT - 1) * P
    dma.dma_start(dst[:, 0:NT - 1, :], dram[0:full, :].rearrange("(t p) d -> p t d", p=P)).then_inc(sem, 16)
    dma.dma_start(dst[0:TAIL, NT - 1, :], dram[full:N, :]).then_inc(sem, 16)


def prepare_edges(nc, c, given, edges, records):
    bits = SW.bit_length() - 1
    by_edge = "(p k) c -> p k c"
    last_row = EDGE_TILES * P
    with Core(nc) as k:
        ed = k.sb("ed", [P, EDGE_TILES + 1, 4], I32)
        ints = k.sb("ed_ints", [P, EDGE_TILES + 1, 4], I32)
        rec = k.sb("rec", [P, EDGE_TILES, 4])
        low = k.sb("low", [P, EDGE_TILES])
        key = k.sb("key", [P, EDGE_TILES + 1], BF16)
        HITS = 7
        assert STRIPS % HITS == 0
        hit = k.sb("hit", [P, HITS, EDGE_TILES], BF16)
        falls = k.sb("falls", [P, 1])
        counts = k.sb("counts", [P, NT * P // SW])
        tile_counts = k.sb("tile_counts", [P, NT])
        none = k.sb("none", [P, 8, 4])
        hit_f, run, zeros, pos = (k.sb(x, [P, EDGE_TILES]) for x in ("hit_f", "run", "zeros", "pos"))
        pos_i = k.sb("pos_i", [P, EDGE_TILES], I32)
        first = k.sb("first", [P, STRIPS])
        strip_ends = k.sb("strip_ends", [P, STRIPS])
        SCAT = 8
        slot_pos = k.sb("slot_pos", [P, SCAT], I32)
        slot_edge = k.sb("slot_edge", [P, SCAT, 4], I32)
        fell = k.ps("fell", [P, 512])
        before = k.ps("edges_before", [P, 512])
        total = k.ps("edges_total", [P, 512])
        s_edges, s_link, s_rec, s_stored, s_falls, s_fell, s_flag, s_iota, s_count, s_prefix, s_pos, s_order, s_sorted, s_gate = (
            k.sem(f"prep_{x}") for x in ("edges", "link", "rec", "stored", "falls", "fell", "flag", "iota", "count", "prefix",
                                         "pos", "order", "sorted", "gate"))
        s_scat, s_copy = c.pool_sem("prep_scattered"), c.pool_sem("prep_copied")
        with nc.Block() as block:

            @block.sync
            def _(sp):
                sp.dma_start(ed[:, 0:EDGE_TILES, :], given[0:last_row, :].rearrange(by_edge, p=P)).then_inc(s_edges, 16)
                sp.dma_start(ed[0:P - 1, EDGE_TILES, :], given[EDGE_TILES:last_row, :].rearrange(by_edge, p=P - 1)[:, 0, :])\
                    .then_inc(s_edges, 16)
                sp.dma_start(ed[P - 1:P, EDGE_TILES, :], given[last_row:last_row + 1, :]).then_inc(s_edges, 16)
                sp.wait_ge(s_sorted, 1)
                sp.dma_start(ed[:, 0:EDGE_TILES, :], edges[0:last_row, :].rearrange(by_edge, p=P)).then_inc(s_edges, 16)
                sp.wait_ge(s_rec, 1)
                sp.dma_start(records[0:last_row, :].rearrange(by_edge, p=P), rec[:, :, :]).then_inc(s_stored, 16)
                sp.dma_start(records[last_row:EDGE_ROWS, :].rearrange(by_edge, p=P), none[:, :, :]).then_inc(s_stored, 16)
                sp.wait_ge(s_stored, 32)

            @block.tensor
            def _(pe):
                pe.wait_ge(s_falls, 1)
                nc.tensor.matmul(fell[0:1, 0:1], falls[:, 0:1], c.ones[:, 0:1], start=True, stop=True).then_inc(s_fell, 1)
                pe.wait_ge(s_count, 1)
                nc.tensor.matmul(before[:, 0:STRIPS], c.before[:, :], counts[:, 0:STRIPS], start=True, stop=True)
                nc.tensor.matmul(total[:, 0:STRIPS], c.ones[:, :], counts[:, 0:STRIPS], start=True, stop=True).then_inc(s_prefix, 1)

            @block.vector
            def _(dve):
                v, st = nc.vector, Steps(dve, s_link)
                v.memset(none[:, :, :], -1.0)
                v.memset(rec[:, :, 3], 0.0)
                v.memset(zeros[:, :], 0.0)
                st.link(v.memset(counts[:, :], 0.0))
                dve.wait_ge(s_edges, 48)
                st.link(v.tensor_scalar(ints[:, :, 2], ed[:, :, 1], bits, None, ALU.arith_shift_right))
                st.link(v.tensor_scalar_min(key[:, :], ints[:, :, 2], float(STRIPS)))
                st.link(v.tensor_tensor(hit[:, 0, :], key[:, 0:EDGE_TILES], key[:, 1:EDGE_TILES + 1], ALU.is_gt))
                v.tensor_reduce(falls[:, :], hit[:, 0, :], AX.X, ALU.add).then_inc(s_falls, 1)
                dve.wait_ge(s_fell, 1)
                v.tensor_scalar_min(c.flags[:, 0:1], fell[0:1, 0:1], 1.0).then_inc(s_flag, 1)
                with dve.Fori(0, STRIPS // HITS) as b, st.each(b, STRIPS // HITS, 1):
                    for q in range(HITS):
                        last = v.tensor_scalar(hit[:, q, :], key[:, 0:EDGE_TILES], c.iota[:, bass.ds(b * HITS + q, 1)], 0.0,
                                               ALU.is_equal, ALU.add, accum_out=counts[:, bass.ds(b * HITS + q, 1)])
                    st.link(last)
                v.tensor_reduce(tile_counts[:, :], counts[:, :].rearrange("p (t s) -> p t s", t=NT), AX.X, ALU.add).then_inc(s_count, 1)
                dve.wait_ge(s_flag, 1)
                unsorted = dve.value_load(c.flags[0:1, 0:1], min_val=0, max_val=1)
                dve.wait_ge(s_prefix, 1)
                st.link(v.tensor_reduce(c.largest[:, :], total[0:1, 0:STRIPS], AX.X, ALU.max))
                with dve.If(unsorted):
                    order = Steps(dve, s_order)
                    order.link(v.tensor_copy(first[:, :], total[:, 0:STRIPS]))
                    order.link(v.tensor_tensor_scan(strip_ends[:, :], first[:, :], zeros[:, 0:STRIPS], 0.0, ALU.add, ALU.add))
                    order.link(v.tensor_tensor(strip_ends[:, :], strip_ends[:, :], first[:, :], ALU.subtract))
                    order.link(v.tensor_tensor(first[:, :], strip_ends[:, :], before[:, 0:STRIPS], ALU.add))
                    order.link(v.tensor_scalar_add(first[:, :], first[:, :], -1.0))
                    dve.wait_ge(s_iota, 1)
                    order.link(v.tensor_copy(run[:, :], pos_i[:, :]))
                    order.link(v.tensor_scalar(hit_f[:, :], key[:, 0:EDGE_TILES], float(STRIPS), None, ALU.is_equal))
                    order.link(v.tensor_tensor(pos[:, :], run[:, :], hit_f[:, :], ALU.mult))
                    with dve.Fori(0, STRIPS) as b, order.each(b, STRIPS, 4):
                        order.link(v.tensor_scalar(hit_f[:, :], key[:, 0:EDGE_TILES], c.iota[:, bass.ds(b, 1)], None, ALU.is_equal))
                        order.link(v.tensor_tensor_scan(run[:, :], hit_f[:, :], zeros[:, :], 0.0, ALU.add, ALU.add))
                        order.link(v.scalar_tensor_tensor(run[:, :], run[:, :], first[:, bass.ds(b, 1)], hit_f[:, :], ALU.add, ALU.mult))
                        order.link(v.tensor_tensor(pos[:, :], pos[:, :], run[:, :], ALU.add))
                    v.tensor_copy(pos_i[:, :], pos[:, :]).then_inc(s_pos, 1)
                dve.wait_ge(s_edges, 64)
                v.tensor_scalar(ints[:, :, 0], ed[:, :, 0], P - 1, None, ALU.bitwise_and)
                v.tensor_scalar(ints[:, :, 1], ed[:, :, 0], P.bit_length() - 1, bits, ALU.arith_shift_right, ALU.logical_shift_left)
                v.tensor_scalar(ints[:, :, 2], ed[:, :, 1], bits, None, ALU.arith_shift_right)
                st.link(v.tensor_scalar(ints[:, :, 3], ed[:, :, 1], SW - 1, None, ALU.bitwise_and))
                v.tensor_copy(c.kinds[:, :], ed[:, 0:EDGE_TILES, 2])
                v.tensor_copy(low[:, :], ints[:, 0:EDGE_TILES, 3])
                v.tensor_copy(rec[:, :, 0], ints[:, 0:EDGE_TILES, 0])
                v.tensor_copy(rec[:, :, 2], ints[:, 0:EDGE_TILES, 2])
                st.link(v.tensor_scalar_add(rec[:, :, 1], ints[:, 0:EDGE_TILES, 1], 1.0))
                v.tensor_tensor(rec[:, :, 1], rec[:, :, 1], low[:, :], ALU.add).then_inc(s_rec, 1)

            @block.gpsimd
            def _(pool):
                pool.iota(pos_i[:, :], pattern=[[1, EDGE_TILES]], base=0, channel_multiplier=EDGE_TILES).then_inc(s_iota, 1)
                pool.wait_ge(s_flag, 1)
                unsorted = pool.value_load(c.flags[0:1, 0:1], min_val=0, max_val=1)
                pool.dma_start(edges[last_row:EDGE_ROWS, :].rearrange("(p k) c -> p (k c)", p=P),
                               given[last_row:EDGE_ROWS, :].rearrange("(p k) c -> p (k c)", p=P)).then_inc(s_copy, 16)
                with pool.If(unsorted):
                    pool.wait_ge(s_pos, 1)
                    with pool.Fori(0, EDGE_TILES // SCAT) as i:
                        pool.tensor_copy(slot_pos[:, :], pos_i[:, bass.ds(i * SCAT, SCAT)]).then_inc(s_gate, 1)
                        pool.tensor_copy(slot_edge[:, :, :], ed[:, bass.ds(i * SCAT, SCAT), :]).then_inc(s_gate, 1)
                        pool.wait_ge(s_gate, i * 4 + 2)
                        pool.sem_inc(s_gate, 1)
                        for q in range(SCAT):
                            pool.indirect_dma_start(edges, bass.IndirectOffsetOnAxis(ap=slot_pos[:, q:q + 1], axis=0),
                                                    slot_edge[:, q, :], None).then_inc(s_scat, 16)
                        pool.wait_ge(s_scat, i * (16 * SCAT) + 16 * SCAT)
                        pool.sem_inc(s_gate, 1)
                with pool.Else():
                    pool.dma_start(edges[0:last_row, :].rearrange("(p k) c -> p (k c)", p=P),
                                   given[0:last_row, :].rearrange("(p k) c -> p (k c)", p=P)).then_inc(s_scat, 16)
                    pool.wait_ge(s_scat, 16)
                pool.wait_ge(s_copy, 16)
                pool.sem_inc(s_sorted, 1)

        group_tables(nc, c, "ga", counts, STRIPS, GAE, GROUPS_A, c.tab["a_strip"], 1.0, c.tab["a_start"], c.tab["a_col"], SW, 0)
        group_tables(nc, c, "gt", tile_counts, NT, GE, GROUPS, c.tab["g_base"], float(P), c.tab["g_start"], c.tab["g_tile"], 1, 1)


def group_tables(nc, c, name, counts, n, size, groups, class_out, factor, start_out, place_out, step, lag):
    with Core(nc) as k:
        col = k.sb(f"{name}_col", [n, 6])
        col_i = k.sb(f"{name}_col_i", [n, 2], I32)
        ended = k.sb(f"{name}_ended", [n, groups])
        less = k.sb(f"{name}_less", [n, P])
        start_f = k.sb(f"{name}_start_f", [1, groups])
        tot = k.ps(f"{name}_tot", [P, 512])
        cum = k.ps(f"{name}_cum", [P, 512])
        cls = k.ps(f"{name}_cls", [P, 512])
        pos = k.ps(f"{name}_pos", [P, 512])
        s_link, s_tot, s_c, s_cum, s_u, s_out = (k.sem(f"{name}_{x}") for x in ("link", "tot", "c", "cum", "u", "out"))
        with nc.Block() as block:

            @block.tensor
            def _(pe):
                nc.tensor.matmul(tot[0:n, 0:1], counts[:, 0:n], c.ones[:, 0:1], start=True, stop=True).then_inc(s_tot, 1)
                pe.wait_ge(s_c, 1)
                nc.tensor.matmul(cum[0:n, 0:1], c.before[0:n, 0:n], col[:, 2:3], start=True, stop=True).then_inc(s_cum, 1)
                pe.wait_ge(s_u, 1)
                nc.tensor.matmul(cls[:, 0:groups], c.ones[0:n, :], ended[:, :], start=True, stop=True)
                nc.tensor.matmul(pos[:, 0:groups], less[:, :], ended[:, :], start=True, stop=True).then_inc(s_out, 1)

            @block.vector
            def _(dve):
                v, st = nc.vector, Steps(dve, s_link)
                bits = size.bit_length() - 1
                dve.wait_ge(s_tot, 1)
                v.tensor_copy(col[:, 0:1], tot[0:n, 0:1])
                st.link(v.tensor_scalar_add(col[:, 1:2], tot[0:n, 0:1], float(size - 1)))
                st.link(v.tensor_copy(col_i[:, 0:1], col[:, 1:2]))
                st.link(v.tensor_scalar(col_i[:, 1:2], col_i[:, 0:1], bits, bits, ALU.arith_shift_right, ALU.logical_shift_left))
                st.link(v.tensor_copy(col[:, 1:2], col_i[:, 1:2]))
                v.tensor_tensor(col[:, 4:5], col[:, 0:1], col[:, 1:2], ALU.subtract)
                v.tensor_scalar_mul(col[:, 2:3], col[:, 1:2], 1.0 / size).then_inc(s_c, 1)
                dve.wait_ge(s_cum, 1)
                st.link(v.tensor_tensor(col[:, 3:4], cum[0:n, 0:1], col[:, 2:3], ALU.add))
                v.tensor_scalar(ended[:, :], c.wide_iota[0:n, 0:groups], col[:, 3:4], None, ALU.is_ge)
                v.tensor_scalar(less[:, :], c.ones[0:n, :], col[:, 4:5], None, ALU.mult).then_inc(s_u, 1)
                dve.wait_ge(s_out, 1)
                v.tensor_scalar_mul(class_out[:, :], cls[:, 0:groups], factor)
                v.tensor_scalar_mul(place_out[:, lag:lag + groups], cls[0:1, 0:groups], float(step))
                if lag:
                    v.memset(place_out[:, 0:lag], n * step)
                st.link(v.scalar_tensor_tensor(start_f[:, :], c.wide_iota[0:1, 0:groups], float(size), pos[0:1, 0:groups], ALU.mult, ALU.add))
                v.tensor_scalar_min(start_out[:, :], start_f[:, :], float(EDGE_TILES * P))


def group_table(v, st, per, per_i, n, size):
    st.link(v.tensor_scalar_add(per[:, 1, 0:n], per[:, 0, 0:n], float(size - 1)))
    st.link(v.tensor_copy(per_i[:, 0, 0:n], per[:, 1, 0:n]))
    bits = size.bit_length() - 1
    st.link(v.tensor_scalar(per_i[:, 1, 0:n], per_i[:, 0, 0:n], bits, bits, ALU.arith_shift_right, ALU.logical_shift_left))
    st.link(v.tensor_copy(per[:, 1, 0:n], per_i[:, 1, 0:n]))
    st.link(v.tensor_tensor(per[:, 4, 0:n], per[:, 0, 0:n], per[:, 1, 0:n], ALU.subtract))
    st.link(v.tensor_scalar_mul(per[:, 1, 0:n], per[:, 1, 0:n], 1.0 / size))
    st.link(v.memset(per[:, 2, 0:n], 0.0))
    st.link(v.tensor_tensor_scan(per[:, 3, 0:n], per[:, 1, 0:n], per[:, 2, 0:n], 0.0, ALU.add, ALU.add))
    st.link(v.tensor_tensor(per[:, 5, 0:n], per[:, 3, 0:n], per[:, 1, 0:n], ALU.subtract))
    st.link(v.tensor_scalar_mul(per[:, 5, 0:n], per[:, 5, 0:n], float(size)))


def layernorm(nc, c, name, src, dst, after=None, NT=NT, beside=None):
    with Core(nc) as k:
        stats = k.sb(f"{name}_stats", [P, NT, 6])
        mean = k.sb(f"{name}_mean", [P, NT])
        var = k.sb(f"{name}_var", [P, NT])
        tmp = k.sb(f"{name}_tmp", [P, NT])
        s_link, s_var, s_root, s_done, s_store = (k.sem(f"{name}_{x}") for x in ("link", "var", "root", "done", "store"))
        with nc.Block() as block:

            @block.vector
            def _(dve):
                v, st = nc.vector, Steps(dve, s_link)
                with dve.Fori(0, NT) as t:
                    last = v.bn_stats(stats[:, bass.ds(t, 1), :].rearrange("p a s -> p (a s)"),
                                      src[:, bass.ds(t, 1), :].rearrange("p a d -> p (a d)"))
                v.drain().then_inc(s_done, 1)
                dve.wait_ge(s_done, 1)
                v.tensor_tensor(mean[:, :], stats[:, :, 1], stats[:, :, 4], ALU.add)
                v.tensor_tensor(tmp[:, :], stats[:, :, 1], stats[:, :, 4], ALU.subtract)
                st.link(v.tensor_tensor(var[:, :], stats[:, :, 2], stats[:, :, 5], ALU.add))
                v.tensor_scalar_mul(mean[:, :], mean[:, :], 0.5)
                st.link(v.tensor_tensor(tmp[:, :], tmp[:, :], tmp[:, :], ALU.mult))
                st.link(v.tensor_scalar(var[:, :], var[:, :], 1.0 / D, EPS, ALU.mult, ALU.add))
                v.scalar_tensor_tensor(var[:, :], tmp[:, :], 0.25, var[:, :], ALU.mult, ALU.add).then_inc(s_var, 1)
                dve.wait_ge(s_root, 1)
                st.link(v.reciprocal(var[:, :], tmp[:, :]))
                with dve.Fori(0, NT) as t:
                    v.tensor_scalar(dst[:, bass.ds(t, 1), 0:D].rearrange("p a d -> p (a d)"),
                                    src[:, bass.ds(t, 1), :].rearrange("p a d -> p (a d)"),
                                    mean[:, bass.ds(t, 1)], var[:, bass.ds(t, 1)], ALU.subtract, ALU.mult)
                if after:
                    v.drain().then_inc(s_done, 1)

            @block.scalar
            def _(act):
                act.wait_ge(s_var, 1)
                nc.scalar.activation(tmp[:, :], var[:, :], ACT.Sqrt).then_inc(s_root, 1)

            if beside:

                @block.gpsimd
                def _(pool):
                    beside(pool)

            if after:

                @block.sync
                def _(sp):
                    sp.wait_ge(s_done, 2)
                    after(sp, s_store)


def aggregate(nc, c, name, edges, table, width, acc, relation_rows):
    used = D + 1
    with Core(nc) as k:
        ed = k.sb(f"{name}_ed", [P, RING, G, 4], I32)
        dst_f = k.sb(f"{name}_dst_f", [P, RING, G])
        rows = k.sb(f"{name}_rows", [P, RING, G, width])
        rel = k.sb(f"{name}_rel", [P, RING, G, width])
        onehot = k.sb(f"{name}_onehot", [P, RING, G, P])
        sums = k.ps(f"{name}_sums", [P, 2, 512])
        s_edges = [k.sem(f"{name}_edges{s}") for s in range(RING)]
        s_rel = [k.sem(f"{name}_rel{s}") for s in range(RING)]
        s_rows = [c.pool_sem(f"{name}_rows{s}") for s in range(RING)]
        s_link, s_ready, s_sum, s_acc, s_gate = (k.sem(f"{name}_{x}") for x in ("link", "ready", "sum", "acc", "gate"))
        LENT = RING + 1
        with nc.Block() as block:

            @block.sync
            def _(sp):
                with sp.Fori(0, GROUPS // RING) as i:
                    for s in range(RING):
                        start = sp.value_load(c.tab["g_start"][0:1, bass.ds(i * RING + s, 1)], min_val=0, max_val=EDGE_TILES * P)
                        src = edges[bass.ds(start, GE), :].rearrange("(p k) c -> p k c", p=P)
                        rel_src = relation_rows[bass.ds(start, GE), :].rearrange("(p k) c -> p (k c)", p=P)
                        sp.wait_ge(s_sum, i * RING + s + 2)
                        sp.dma_start(ed[:, s, :, :], src).then_inc(s_edges[s], 16)
                        sp.dma_start(rel[:, s, :, :].rearrange("p k c -> p (k c)"), rel_src).then_inc(s_rel[s], 16)

            @block.gpsimd
            def _(pool):
                with pool.Fori(0, GROUPS // RING) as i:
                    for s in range(RING):
                        pool.wait_ge(s_edges[s], i * 16 + 16)
                        pool.sem_inc(s_gate, 1)
                        for g in range(G):
                            pool.indirect_dma_start(rows[:, s, g, :], None, table,
                                                    bass.IndirectOffsetOnAxis(ap=ed[:, s, g, 0:1], axis=0))\
                                .then_inc(s_rows[s], 16)

            @block.vector
            def _(dve):
                v, st = nc.vector, Steps(dve, s_link)

                def add(g, bank, tile):
                    dve.wait_ge(s_acc, g + 1)
                    dve.wait_ge(s_sum, g + LENT)
                    here = acc[:, bass.ds(tile, 1), 0:used].rearrange("p a d -> p (a d)")
                    v.tensor_tensor(here, here, sums[:, bank, 0:used], ALU.add).then_inc(s_acc, 1)

                v.memset(acc[:, :, :], 0.0).then_inc(s_acc, 1)
                with dve.Fori(0, GROUPS // RING) as i, st.each(i, GROUPS // RING, 2 * RING):
                    for s in range(RING):
                        g = i * RING + s
                        tile = dve.value_load(c.tab["g_tile"][0:1, bass.ds(g, 1)], min_val=0, max_val=NT)
                        dve.wait_ge(s_edges[s], i * 16 + 16)
                        st.link(v.tensor_copy(dst_f[:, s, :], ed[:, s, :, 1]))
                        st.link(v.tensor_scalar(dst_f[:, s, :], dst_f[:, s, :], c.tab["g_base"][:, bass.ds(g, 1)], None, ALU.subtract))
                        for t in range(G):
                            v.tensor_scalar(onehot[:, s, t, :], c.iota[:, 0:P], dst_f[:, s, t:t + 1], None, ALU.is_equal)
                        dve.wait_ge(s_rel[s], i * 16 + 16)
                        dve.wait_ge(s_rows[s], i * (16 * G) + 16 * G)
                        v.tensor_tensor(rows[:, s, :, 0:used], rows[:, s, :, 0:used], rel[:, s, :, 0:used], ALU.mult)\
                            .then_inc(s_ready, 1)
                        add(g, (s + 1) % 2, tile)
                add(GROUPS, (GROUPS - 1) % 2, dve.value_load(c.tab["g_tile"][0:1, GROUPS:GROUPS + 1], min_val=0, max_val=NT))

            @block.tensor
            def _(pe):
                nc.tensor.matmul(sums[:, 1, 0:used], c.zero_b[:, 0:P], c.zero_b[:, 0:used], start=True, stop=True).then_inc(s_sum, LENT)
                with pe.Fori(0, GROUPS // RING) as i:
                    for s in range(RING):
                        pe.wait_ge(s_ready, i * RING + s + 1)
                        pe.wait_ge(s_acc, i * RING + s + 1)
                        for t in range(G):
                            last = nc.tensor.matmul(sums[:, s % 2, 0:used], onehot[:, s, t, :], rows[:, s, t, 0:used],
                                                    start=t == 0, stop=t == G - 1)
                        last.then_inc(s_sum, 1)


def dense(nc, c, name, rows, weight, M, finish):
    with Core(nc) as k:
        turned = k.sb(f"{name}_turned", [P, 2, J * KD * P])
        turns, result = k.ps(f"{name}_turns", [P, 3 * 512]), k.ps(f"{name}_result", [P, 3 * 512])
        s_t, s_turned, s_z, s_free, s_link = (k.sem(f"{name}_{x}") for x in ("t", "turned", "z", "free", "link"))
        with nc.Block() as block:

            @block.tensor
            def _(pe):
                def turn(i):
                    if i:
                        pe.wait_ge(s_turned, i)
                    for j in range(J):
                        for h in range(KD):
                            at = (j * KD + h) * P
                            last = nc.tensor.transpose(turns[:, at:at + P], rows[:, i * J + j, h * P:(h + 1) * P], c.ident[:, :])
                    last.then_inc(s_t, 1)

                turn(0)
                for i in range(NJ):
                    if i + 1 < NJ:
                        turn(i + 1)
                    else:
                        pe.wait_ge(s_turned, NJ)
                    if i:
                        pe.wait_ge(s_free, i)
                    for j in range(J):
                        for h in range(KD):
                            at = (j * KD + h) * P
                            last = nc.tensor.matmul(result[:, j * D:j * D + M], turned[:, i % 2, at:at + P], weight[:, h, :],
                                                    start=h == 0, stop=h == KD - 1)
                    last.then_inc(s_z, 1)

            @block.scalar
            def _(act):
                for i in range(NJ):
                    act.wait_ge(s_t, i + 1)
                    if i >= 2:
                        act.wait_ge(s_z, i - 1)
                    nc.scalar.activation(turned[:, i % 2, :], turns[:, 0:J * D], ACT.Copy).then_inc(s_turned, 1)

            @block.vector
            def _(dve):
                v, st = nc.vector, Steps(dve, s_link)
                for i in range(NJ):
                    dve.wait_ge(s_z, i + 1)
                    z = result[:, 0:J * D].rearrange("p (j d) -> p j d", d=D)[:, :, 0:M]
                    finish(v, st, i * J, z).then_inc(s_free, 1)
                    dve.wait_ge(s_free, i + 1)


def load_all(nc, name, loads):
    with Core(nc) as k:
        s = k.sem(f"{name}_loads")
        with nc.Block() as block:

            @block.sync
            def _(sp):
                for out, src in loads:
                    sp.dma_start(out, src, allow_slow_non_contiguous=True).then_inc(s, 16)
                sp.wait_ge(s, 16 * len(loads))


def row(ap):
    return ap.rearrange("(a n) -> a n", a=1).to_broadcast([P, ap.shape[0]])


def split_rows(v, st, dst, src, rest):
    st.link(v.tensor_copy(dst[0], src))
    st.link(v.tensor_tensor(rest, src, dst[0], ALU.subtract))
    st.link(v.tensor_copy(dst[1], rest))
    st.link(v.tensor_tensor(rest, rest, dst[1], ALU.subtract))
    return v.tensor_copy(dst[2], rest)


def gnn0_start(nc, c, I, x_dram, h_table, parts, m):
    with Core(nc) as k:
        h = k.sb("h0", [P, NTP, D])
        s_mask = k.sem("mask_row")
        load_all(nc, "x0", [(h[:, :, :], x_dram.rearrange("(t p) d -> p t d", p=P))])

        def mask_row(sp, s_store):
            sp.dma_start(h[0:1, 0, :], I["L0_gnn_mask_embed"].rearrange("(a n) -> a n", a=1)).then_inc(s_mask, 16)
            sp.wait_ge(s_mask, 16)
            sp.dma_start(h_table.rearrange("(t p) d -> p t d", p=P), h[:, :, :]).then_inc(s_store, 16)
            sp.wait_ge(s_store, 16)

        def zero_matrix(pool):
            for t in range(NT):
                pool.memset(m[:, t, :], 0.0)

        layernorm(nc, c, "ln0", h, h, mask_row, NTP, zero_matrix)
        T = 2
        part = k.sb("part0", [P, 2, T, 3, D], BF16)
        rest = k.sb("rest0", [P, T, D])
        s_link, s_part, s_free = (k.sem(f"split_{x}") for x in ("link", "part", "free"))
        s_save = [k.sem(f"split_save{q}") for q in range(2)]
        with nc.Block() as block:

            @block.vector
            def _(dve):
                v, st = nc.vector, Steps(dve, s_link)
                for b in range(NTP // T):
                    if b >= 2:
                        dve.wait_ge(s_free, b - 1)
                    split_rows(v, st, [part[:, b % 2, :, q, :] for q in range(3)], h[:, b * T:b * T + T, :], rest[:, :, :])\
                        .then_inc(s_part, 1)
                    dve.wait_ge(s_part, b + 1)

            @block.sync
            def _(sp):
                for b in range(NTP // T):
                    sp.wait_ge(s_part, b + 1)
                    sp.dma_start(parts[b * T:b * T + T].rearrange("t p f -> p t f"),
                                 part[:, b % 2, :, :, :].rearrange("p t q d -> p t (q d)")).then_inc(s_save[b % 2], 16)
                    if b >= 1:
                        sp.wait_ge(s_save[(b - 1) % 2], (b + 1) // 2 * 16)
                        sp.sem_inc(s_free, 1)
                last = NTP // T - 1
                sp.wait_ge(s_save[last % 2], (last // 2 + 1) * 16)


def build_matrix(nc, c, records, m, relation_work):
    with Core(nc) as k:
        R = STREAMS
        rec = k.sb("b_rec", [P, R, GA, 4])
        code = k.sb("b_code", [P, R, GA])
        at = k.sb("b_at", [P, R, GA, P], BF16)
        oh = k.sb("b_oh", [P, R, GA, CODES], BF16)
        numbers = k.sb("b_numbers", [P, CODES], mybir.dt.float16)
        with Core(nc) as kk:
            whole = kk.sb("b_whole", [P, CODES], I32)
            s_n = kk.sem("b_whole_set")
            with nc.Block() as block:

                @block.gpsimd
                def _(pool):
                    pool.iota(whole[:, :], pattern=[[1, CODES]], base=0, channel_multiplier=0).then_inc(s_n, 1)

                @block.vector
                def _(dve):
                    dve.wait_ge(s_n, 1)
                    nc.vector.tensor_scalar_add(numbers[:, :], whole[:, :], 1.0)

        halves = ((0, NT // 2 + 1), (NT // 2 + 1, NT))
        strips = k.ps("b_strips", [P, 2 * R, 512])
        s_rec = [k.sem(f"b_rec{s}") for s in range(R)]
        s_link, s_oh, s_sum, s_m = (k.sem(f"b_{x}") for x in ("link", "onehot", "sum", "m"))
        iota_low = k.sb("b_iota", [P, P], BF16)
        rounds = GROUPS_A // R
        with nc.Block() as block:

            @block.sync
            def _(sp):
                with sp.Fori(0, rounds) as i:
                    for s in range(R):
                        start = sp.value_load(c.tab["a_start"][0:1, bass.ds(i + s * rounds, 1)], min_val=0, max_val=EDGE_TILES * P)
                        src = records[bass.ds(start, GAE), :].rearrange("(p k) c -> p k c", p=P)
                        sp.wait_ge(s_oh, i * R + s + 1)
                        sp.dma_start(rec[:, s, :, :], src).then_inc(s_rec[s], 16)

            @block.vector
            def _(dve):
                v, st = nc.vector, Steps(dve, s_link)
                st.link(v.tensor_copy(iota_low[:, :], c.iota[:, :]))
                dve.sem_inc(s_oh, R)
                with dve.Fori(0, rounds) as i, st.each(i, rounds, R):
                    for s in range(R):
                        dve.wait_ge(s_rec[s], i * 16 + 16)
                        dve.wait_ge(s_sum, i * R + s + 1)
                        v.scalar_tensor_tensor(code[:, s, :], rec[:, s, :, 2], c.tab["a_strip"][:, bass.ds(i + s * rounds, 1)],
                                               rec[:, s, :, 1], ALU.is_equal, ALU.mult).then_inc(s_link, 1)
                        st.n += 1
                        for t in range(GA):
                            v.tensor_scalar(at[:, s, t, :], iota_low[:, :], rec[:, s, t, 0:1], None, ALU.is_equal)
                        dve.wait_ge(s_link, st.base + st.n)
                        for t in range(GA):
                            last = v.tensor_scalar(oh[:, s, t, :], numbers[:, :], code[:, s, t:t + 1], None, ALU.is_equal)
                        last.then_inc(s_oh, 1)

            @block.tensor
            def _(pe):
                pe.sem_inc(s_sum, R)
                with pe.Fori(0, rounds) as i:
                    for s in range(R):
                        col = pe.value_load(c.tab["a_col"][0:1, bass.ds(i + s * rounds, 1)], min_val=0, max_val=MW - SW)
                        pe.wait_ge(s_m, i * R + s + 1)
                        for b, (t0, t1) in enumerate(halves):
                            nc.tensor.matmul(strips[:, 2 * s + b, 0:(t1 - t0) * SW], c.ident_b[:, :], m[:, t0:t1, bass.ds(col, SW)],
                                             start=True, stop=False)
                        pe.wait_ge(s_oh, i * R + s + 1 + R)
                        for t in range(GA):
                            for b, (t0, t1) in enumerate(halves):
                                last = nc.tensor.matmul(strips[:, 2 * s + b, 0:(t1 - t0) * SW], at[:, s, t, :],
                                                        oh[:, s, t, t0 * SW:t1 * SW], start=False, stop=t == GA - 1)
                        last.then_inc(s_sum, 1)

            @block.scalar
            def _(act):
                act.sem_inc(s_m, R)
                with act.Fori(0, rounds) as i:
                    for s in range(R):
                        col = act.value_load(c.tab["a_col"][0:1, bass.ds(i + s * rounds, 1)], min_val=0, max_val=MW - SW)
                        act.wait_ge(s_sum, i * R + s + 1 + R)
                        for b, (t0, t1) in enumerate(halves):
                            last = nc.scalar.activation(m[:, t0:t1, bass.ds(col, SW)],
                                                        strips[:, 2 * s + b, 0:(t1 - t0) * SW].rearrange("p (t w) -> p t w", w=SW), ACT.Copy)
                        last.then_inc(s_m, 1)

            @block.gpsimd
            def _(pool):
                relation_work(pool)


def node_degrees(nc, c, m):
    with Core(nc) as k:
        clip = k.sb("nd_clip", [P, NTP])
        most, over, wide = k.sb("nd_most", [P, 1]), k.sb("nd_over", [P, 1]), k.sb("nd_wide", [1, 1])
        cols = k.ps("nd_cols", [P, 512])
        number = k.ps("nd_number", [P, 512])
        s_deg, s_in, s_ones, s_over, s_flag = (k.sem(f"nd_{x}") for x in ("deg", "in", "ones", "over", "flag"))
        ones = k.sb("nd_ones", [P, 1], BF16)
        with nc.Block() as block:

            @block.tensor
            def _(pe):
                pe.wait_ge(s_ones, 1)
                for t in range(NT):
                    w = min(P, MW - t * P)
                    for q in range(NT):
                        last = nc.tensor.matmul(cols[0:w, t:t + 1], m[:, q, t * P:t * P + w], ones[:, :], start=q == 0, stop=q == NT - 1)
                last.then_inc(s_in, 1)
                pe.wait_ge(s_over, 1)
                nc.tensor.matmul(number[0:1, 0:1], over[:, :], c.ones[:, 0:1], start=True, stop=True).then_inc(s_over, 1)

            @block.vector
            def _(dve):
                v = nc.vector
                v.memset(c.deg[:, 1, :], 0.0).then_inc(s_deg, 1)
                v.memset(ones[:, :], 1.0).then_inc(s_ones, 1)
                dve.wait_ge(s_deg, 1)
                dve.wait_ge(s_in, 1)
                w = MW - (NT - 1) * P
                v.tensor_copy(c.deg[:, 1, 0:NT - 1], cols[:, 0:NT - 1])
                v.tensor_copy(c.deg[0:w, 1, NT - 1:NT], cols[0:w, NT - 1:NT]).then_inc(s_deg, 1)
                dve.wait_ge(s_deg, 2)
                v.tensor_reduce(most[:, :], c.deg[:, 1, :], AX.X, ALU.max)
                v.tensor_scalar_max(clip[:, :], c.deg[:, 1, :], 1.0)
                v.tensor_scalar(wide[:, :], c.largest[:, :], float(LARGEST), None, ALU.is_gt).then_inc(s_deg, 1)
                dve.wait_ge(s_deg, 3)
                v.tensor_scalar(over[:, :], most[:, :], 255.5, None, ALU.is_gt).then_inc(s_over, 1)
                v.reciprocal(c.rdeg[:, :], clip[:, :])
                dve.wait_ge(s_over, 2)
                v.tensor_tensor(wide[:, :], wide[:, :], number[0:1, 0:1], ALU.add).then_inc(s_flag, 1)
                dve.wait_ge(s_flag, 1)
                v.tensor_scalar_min(c.flags[:, 1:2], wide[:, :], 1.0)


def gnn0_layer(nc, c, I, layer, m, h_table, h_next, parts, next_parts, x_dram, out_table, r_table, relation_rows):
    final = out_table is not None
    with Core(nc) as k:
        n = f"l{layer}"
        wl, wr, shift = k.sb(f"{n}_wl", [P, KD, D]), k.sb(f"{n}_wr", [P, KD, D]), k.sb(f"{n}_shift", [P, D])
        with Core(nc) as kk:
            vecs, mul = kk.sb(f"{n}_vecs", [P, 5, D]), kk.sb(f"{n}_mul", [P, D])
            load_all(nc, n, [
                (wl[:, :, :], I["L0_gnn_Wl"][layer].rearrange("(k p) n -> p k n", p=P)),
                (wr[:, :, :], I["L0_gnn_Wr"][layer].rearrange("(k p) n -> p k n", p=P)),
                *[(vecs[:, q, :], row(I[f"L0_gnn_{v}"][layer])) for q, v in enumerate(("b", "gamma", "beta", "rmean", "rvar"))]])
            s_link, s_var, s_root = (kk.sem(f"{n}_bn_{x}") for x in ("link", "var", "root"))
            with nc.Block() as block:

                @block.vector
                def _(dve):
                    v, st = nc.vector, Steps(dve, s_link)
                    v.tensor_scalar_add(vecs[:, 4, :], vecs[:, 4, :], EPS).then_inc(s_var, 1)
                    dve.wait_ge(s_root, 1)
                    st.link(v.reciprocal(mul[:, :], shift[:, :]))
                    st.link(v.tensor_tensor(mul[:, :], mul[:, :], vecs[:, 1, :], ALU.mult))
                    st.link(v.tensor_tensor(shift[:, :], vecs[:, 0, :], vecs[:, 3, :], ALU.subtract))
                    st.link(v.tensor_tensor(shift[:, :], shift[:, :], mul[:, :], ALU.mult))
                    v.tensor_tensor(shift[:, :], shift[:, :], vecs[:, 2, :], ALU.add)
                    for w in (wl, wr):
                        v.tensor_tensor(w[:, :, :], w[:, :, :], bc(mul[:, :].unsqueeze(1), [P, KD, D]), ALU.mult)

                @block.scalar
                def _(act):
                    act.wait_ge(s_var, 1)
                    nc.scalar.activation(shift[:, :], vecs[:, 4, :], ACT.Sqrt).then_inc(s_root, 1)

        U = 5
        part = k.sb(f"{n}_part", [P, U, 3, D], BF16)
        aggT = k.sb(f"{n}_aggT", [P, KD, 2048])
        h = k.sb(f"{n}_h", [P, 2, J2, D])
        z = k.sb(f"{n}_z", [P, J2, D])
        aT = k.sb(f"{n}_aT", [P, KD, J2 * P])
        hT = k.sb(f"{n}_hT", [P, J2, KD, P])
        if final:
            extra, nxt = k.sb(f"{n}_extra", [P, 2, J2, D]), None
        else:
            extra, nxt = None, k.sb(f"{n}_next", [P, J2, 3, D], BF16)
        bank = k.ps(f"{n}_bank", [P, 8, 512])
        s_part = [k.sem(f"{n}_part{u}") for u in range(U)]
        s_h = [k.sem(f"{n}_hrow{s}") for s in range(2)]
        (s_mm, s_sum, s_evac_a, s_evac_v, s_turn, s_hT, s_aT, s_z, s_zused, s_new, s_save, s_saved, s_link, s_deg) = (
            k.sem(f"{n}_{x}") for x in ("mm", "sum", "evac_a", "evac_v", "turn", "hT", "aT", "z", "zused", "new", "save",
                                        "saved", "link", "deg"))
        relation_work = RelationRows(nc, c, k, n, r_table, relation_rows, sum(SHARES[:layer + 1]), SHARES[layer + 1], 1)
        loads = 2 if final else 1
        stores = 1 if final else 2
        batches = [p[2] // J2 for p in PORTIONS]
        with nc.Block() as block:

            @block.sync
            def _(sp):
                def load(b, t0, s):
                    rows = h_table[bass.ds(t0 * P, J2 * P), :].rearrange("(j p) d -> p j d", p=P)
                    sp.dma_start(h[:, s, :, :], rows).then_inc(s_h[s], 16)
                    if final:
                        rows = x_dram[bass.ds(t0 * P, J2 * P), :].rearrange("(j p) d -> p j d", p=P)
                        sp.dma_start(extra[:, s, :, :], rows).then_inc(s_h[s], 16)

                def save(b, t0, s):
                    out = (out_table if final else h_next)[bass.ds(t0 * P, J2 * P), :].rearrange("(j p) d -> p j d", p=P)
                    ahead = None if final else next_parts[bass.ds(t0, J2), :, :].rearrange("t p f -> p t f")
                    sp.wait_ge(s_new, b + 2)
                    sp.dma_start(out, h[:, s, :, :]).then_inc(s_save, 16)
                    if not final:
                        sp.dma_start(ahead, nxt[:, :, :, :].rearrange("p j q d -> p j (q d)")).then_inc(s_save, 16)
                    sp.wait_ge(s_save, b * (16 * stores) + 16 * stores)
                    sp.sem_inc(s_saved, 1)

                b0 = t0 = 0
                for p, (_, _, tiles) in enumerate(PORTIONS):
                    with sp.Fori(0, NT // U) as i:
                        for u in range(U):
                            src = parts[bass.ds(i * U + u, 1), :, :].rearrange("a p f -> p (a f)")
                            sp.wait_ge(s_mm, i * U + u + p * NT + 1)
                            sp.dma_start(part[:, u, :, :].rearrange("p q d -> p (q d)"), src).then_inc(s_part[u], 16)
                    for s in range(2):
                        load(b0 + s, t0 + s * J2, s)
                    with sp.Fori(0, batches[p] // 2 - 1) as i:
                        for s in range(2):
                            b = 2 * i + s
                            save(b0 + b, t0 + b * J2, s)
                            load(b0 + b + 2, t0 + b * J2 + 2 * J2, s)
                    for s in range(2):
                        b = batches[p] - 2 + s
                        save(b0 + b, t0 + b * J2, s)
                    b0 += batches[p]
                    t0 += tiles

            @block.tensor
            def _(pe):
                pe.sem_inc(s_mm, U)
                b0 = 0
                for p, (col0, widths, _) in enumerate(PORTIONS):
                    nb = len(widths)
                    if p:
                        pe.wait_ge(s_zused, b0 + 2)
                    for b in range(2 * nb):
                        w = widths[b % nb]
                        nc.tensor.matmul(bank[:, b, 0:w], c.zero_b[:, 0:P], c.zero_b[:, 0:w], start=True, stop=False)
                    with pe.Fori(0, NT // U) as i:
                        for u in range(U):
                            pe.wait_ge(s_part[u], i * 16 + p * (NT // U) * 16 + 16)
                            for q in range(3):
                                for hf in range(KD):
                                    at = col0
                                    for b, w in enumerate(widths):
                                        last = nc.tensor.matmul(
                                            bank[:, hf * nb + b, 0:w], part[:, u, q, hf * P:(hf + 1) * P],
                                            m[:, bass.ds(i * U + u, 1), at:at + w].rearrange("p a w -> p (a w)"),
                                            start=False, stop=False)
                                        at += w
                            last.then_inc(s_mm, 1)
                    for b in range(2 * nb):
                        w = widths[b % nb]
                        last = nc.tensor.matmul(bank[:, b, 0:w], c.zero_b[:, 0:P], c.zero_b[:, 0:w], start=False, stop=True)
                    last.then_inc(s_sum, 1)
                    pe.wait_ge(s_evac_a, p + 1)
                    pe.wait_ge(s_evac_v, p + 1)
                    with pe.Fori(0, batches[p] // 2) as i:
                        for s in range(2):
                            b = 2 * i + s + b0
                            pe.wait_ge(s_h[s], i * (16 * loads) + (b0 // 2 + 1) * 16 * loads)
                            for j in range(J2):
                                for hf in range(KD):
                                    at = (j * KD + hf) * P
                                    last = nc.tensor.transpose(bank[:, s, at:at + P], h[:, s, j, hf * P:(hf + 1) * P], c.ident[:, :])
                            last.then_inc(s_turn, 1)
                            pe.wait_ge(s_zused, b + 1)
                            pe.wait_ge(s_hT, b + 1)
                            for j in range(J2):
                                for hf in range(KD):
                                    nc.tensor.matmul(bank[:, 2 + s, j * D:(j + 1) * D], hT[:, j, hf, :], wr[:, hf, :],
                                                     start=hf == 0, stop=hf == KD - 1)
                            pe.wait_ge(s_aT, b + 1)
                            for j in range(J2):
                                for hf in range(KD):
                                    last = nc.tensor.matmul(bank[:, 4 + s, j * D:(j + 1) * D], aT[:, hf, j * P:(j + 1) * P],
                                                            wl[:, hf, :], start=hf == 0, stop=hf == KD - 1)
                            last.then_inc(s_z, 1)
                    b0 += batches[p]

            @block.scalar
            def _(act):
                act.sem_inc(s_z, 1)
                if layer == 0:
                    junk = aggT[:, 0, 0:MW // 2].bitcast(BF16)
                    for q in range(NT):
                        nc.scalar.activation(junk, m[:, q, :], ACT.Copy, accum_out=c.deg[:, 0, q:q + 1]).then_inc(s_deg, 1)
                        act.wait_ge(s_deg, q + 1)
                b0 = 0
                for p, (_, widths, _) in enumerate(PORTIONS):
                    act.wait_ge(s_sum, p + 1)
                    at = 0
                    for b, w in enumerate(widths):
                        last = nc.scalar.activation(aggT[:, 0, at:at + w], bank[:, b, 0:w], ACT.Copy)
                        at += w
                    last.then_inc(s_evac_a, 1)
                    act.wait_ge(s_evac_a, p + 1)
                    act.wait_ge(s_evac_v, p + 1)
                    with act.Fori(0, batches[p] // 2) as i:
                        for s in range(2):
                            b = 2 * i + s + b0
                            act.wait_ge(s_turn, b + 1)
                            act.wait_ge(s_z, b + 1)
                            nc.scalar.activation(hT[:, :, :, :].rearrange("p j h c -> p (j h c)"), bank[:, s, :], ACT.Copy).then_inc(s_hT, 1)
                            nc.scalar.activation(aT[:, :, :], aggT[:, :, bass.ds((2 * i + s) * (J2 * P), J2 * P)], ACT.Copy).then_inc(s_aT, 1)
                    b0 += batches[p]

            @block.vector
            def _(dve):
                v, st = nc.vector, Steps(dve, s_link)
                dve.sem_inc(s_zused, 2)
                dve.sem_inc(s_saved, 1)
                dve.sem_inc(s_new, 1)
                b0 = t0 = 0
                for p, (_, widths, tiles) in enumerate(PORTIONS):
                    nb = len(widths)
                    dve.wait_ge(s_sum, p + 1)
                    at = 0
                    for b, w in enumerate(widths):
                        last = v.tensor_copy(aggT[:, 1, at:at + w], bank[:, nb + b, 0:w])
                        at += w
                    last.then_inc(s_evac_v, 1)
                    with dve.Fori(0, batches[p] // 2) as i, st.each(i, batches[p] // 2, 2 * (2 if final else 6)):
                        for s in range(2):
                            b = 2 * i + s + b0
                            dve.wait_ge(s_z, b + 2)
                            zs, hs = z[:, :, :], h[:, s, :, :]
                            dve.wait_ge(s_new, b + 1)
                            st.link(v.tensor_tensor(zs, bank[:, 2 + s, :].rearrange("p (j d) -> p j d", d=D),
                                                    bc(shift[:, :].unsqueeze(1), [P, J2, D]), ALU.add))
                            for j in range(J2):
                                last = v.scalar_tensor_tensor(z[:, j, :], bank[:, 4 + s, j * D:(j + 1) * D],
                                                              c.rdeg[:, bass.ds((2 * i + s) * J2 + t0 + j, 1)], z[:, j, :],
                                                              ALU.mult, ALU.add)
                            last.then_inc(s_zused, 1)
                            dve.wait_ge(s_zused, b + 3)
                            if final:
                                st.link(v.tensor_tensor(zs, zs, hs, ALU.add))
                                v.tensor_tensor(hs, zs, extra[:, s, :, :], ALU.add).then_inc(s_new, 1)
                            else:
                                st.link(v.scalar_tensor_tensor(hs, zs, 0.0, hs, ALU.max, ALU.add))
                                dve.wait_ge(s_saved, b + 1)
                                split_rows(v, st, [nxt[:, :, q, :] for q in range(3)], hs, zs).then_inc(s_new, 1)
                    b0 += batches[p]
                    t0 += tiles

            @block.gpsimd
            def _(pool):
                relation_work(pool)


def relation_tables(nc, c, I, r_table):
    with Core(nc) as m:
        rel = m.sb("rel", [P, RT, W1])
        raw = m.sb("rel_raw", [P, RT, D])
        gw, gb = m.sb("rel_gw", [P, D]), m.sb("rel_gb", [P, 1])
        prod = m.sb("rel_prod", [P, RT, D])
        gate = m.sb("rel_gate", [P, RT])
        s_l, s_link, s_a, s_b, s_r, s_st = (m.sem(f"rel_{x}") for x in ("load", "link", "a", "b", "done", "st"))
        last_rel = RELATIONS - (RT - 1) * P
        with nc.Block() as block:

            @block.sync
            def _(sp):
                src = I["L1_gnn_relation_emb"]
                sp.wait_ge(s_a, 1)
                sp.dma_start(raw[:, 0:RT - 1, :], src[0:(RT - 1) * P, :].rearrange("(t p) d -> p t d", p=P)).then_inc(s_l, 16)
                sp.dma_start(raw[0:last_rel, RT - 1, :], src[(RT - 1) * P:RELATIONS, :]).then_inc(s_l, 16)
                sp.dma_start(gw[:, :], row(I["L1_gnn_gate_w"].rearrange("a n -> (a n)"))).then_inc(s_l, 16)
                sp.dma_start(gb[:, :], row(I["L1_gnn_gate_b"])).then_inc(s_l, 16)
                sp.wait_ge(s_r, 1)
                sp.dma_start(r_table.rearrange("(t p) d -> p t d", p=P), rel[:, :, :]).then_inc(s_st, 16)
                sp.wait_ge(s_st, 16)

            @block.vector
            def _(dve):
                v, st = nc.vector, Steps(dve, s_link)
                v.memset(rel[:, :, :], 0.0)
                v.memset(raw[:, :, :], 0.0).then_inc(s_a, 1)
                dve.wait_ge(s_l, 64)
                st.link(v.tensor_tensor(prod[:, :, :].rearrange("p t (b c) -> p t b c", b=4),
                                        raw[:, :, :].rearrange("p t (b c) -> p t b c", b=4),
                                        bc(gw[:, :].rearrange("p (c b) -> p b c", b=4).unsqueeze(1), [P, RT, 4, D // 4]), ALU.mult))
                st.link(v.tensor_reduce(gate[:, :], prod[:, :, :], AX.X, ALU.add))
                v.tensor_scalar(gate[:, :], gate[:, :], gb[:, 0:1], None, ALU.add).then_inc(s_a, 1)
                dve.wait_ge(s_b, 1)
                v.tensor_tensor(rel[:, :, 0:D], raw[:, :, :], bc(gate[:, :].unsqueeze(2), [P, RT, D]), ALU.mult)
                v.tensor_copy(rel[:, :, D], gate[:, :]).then_inc(s_r, 1)

            @block.scalar
            def _(act):
                act.wait_ge(s_a, 2)
                nc.scalar.activation(gate[:, :], gate[:, :], ACT.Sigmoid).then_inc(s_b, 1)


class RelationRows:

    def __init__(self, nc, c, k, name, r_table, out, first, tiles, size):
        self.nc, self.c, self.table, self.out, self.first, self.size = nc, c, r_table, out, first, size
        self.chunks = tiles // size
        assert self.chunks % 4 == 0 and tiles % size == 0
        self.kind = k.sb(f"{name}_kind", [P, 4, size], I32)
        self.buf = k.sb(f"{name}_buf", [P, 4, size, W1])
        self.s_row = [c.pool_sem(f"{name}_row{s}") for s in range(4)]
        self.s_out = [c.pool_sem(f"{name}_out{s}") for s in range(4)]
        self.s_kind, self.s_gate = k.sem(f"{name}_kind"), k.sem(f"{name}_gate")

    def __call__(self, pool):
        size = self.size
        out = self.out[0:EDGE_TILES * P, :].rearrange("(p k) c -> p k c", p=P)

        def gather(chunk, s):
            pool.tensor_copy(self.kind[:, s, :], self.c.kinds[:, bass.ds(chunk * size + self.first, size)]).then_inc(self.s_kind, 1)
            pool.wait_ge(self.s_kind, chunk + 1)
            pool.sem_inc(self.s_gate, 1)
            for g in range(size):
                pool.indirect_dma_start(self.buf[:, s, g, :], None, self.table,
                                        bass.IndirectOffsetOnAxis(ap=self.kind[:, s, g:g + 1], axis=0)).then_inc(self.s_row[s], 16)

        def store(chunk, s, uses):
            pool.wait_ge(self.s_row[s], uses * (16 * size))
            pool.sem_inc(self.s_gate, 1)
            pool.dma_start(out[:, bass.ds(chunk * size + self.first, size), :], self.buf[:, s, :, :]).then_inc(self.s_out[s], 16)

        gather(0, 0)
        gather(1, 1)
        for s in range(4):
            store(s, s, 1)
            if s >= 2:
                pool.wait_ge(self.s_out[s - 2], 16)
            gather(s + 2, (s + 2) % 4)
        with pool.Fori(1, self.chunks // 4 - 1) as i:
            for s in range(4):
                store(i * 4 + s, s, i + 1)
                pool.wait_ge(self.s_out[(s + 2) % 4], i * 16 + (0 if s < 2 else 16))
                pool.sem_inc(self.s_gate, 1)
                gather(i * 4 + (s + 2), (s + 2) % 4)
        last = self.chunks - 4
        for s in range(4):
            store(last + s, s, self.chunks // 4)
            if s < 2:
                pool.wait_ge(self.s_out[s + 2], 16 * (self.chunks // 4 - 1))
                gather(last + s + 2, s + 2)
        for s in range(4):
            pool.wait_ge(self.s_out[s], 16 * (self.chunks // 4))


def gnn0(nc, c, I, edges, r_table, relation_rows):
    h_tables = [c.dram(f"h_table{q}", [NTP * P, D]) for q in range(2)]
    x1 = c.dram("x1", [NTP * P, D])
    parts = [c.dram(f"parts{q}", [NTP, P, 3 * D], BF16) for q in range(2)]
    with Core(nc) as k:
        m = k.sb("matrix", [P, NT, MW], BF16)
        gnn0_start(nc, c, I, I["x"], h_tables[0], parts[0], m)
        with Core(nc) as kk:
            c.tab["a_strip"] = kk.sb("a_strip", [P, GROUPS_A])
            c.tab["a_start"] = kk.sb("a_start", [1, GROUPS_A], I32)
            c.tab["a_col"] = kk.sb("a_col", [1, GROUPS_A], I32)
            s_t = kk.sem("a_tables")
            with nc.Block() as block:

                @block.sync
                def _(sp):
                    for t, d in ((c.tab["a_strip"], c.tab["a_strip_d"]), (c.tab["a_start"], c.tab["a_start_d"]), (c.tab["a_col"], c.tab["a_col_d"])):
                        sp.dma_start(t[:, :], d).then_inc(s_t, 16)
                    sp.wait_ge(s_t, 48)

            work = RelationRows(nc, c, kk, "rr", r_table, relation_rows, 0, SHARES[0], 2)
            build_matrix(nc, c, c.records, m, work)
        node_degrees(nc, c, m)
        for layer in range(3):
            gnn0_layer(nc, c, I, layer, m, h_tables[min(layer, 1)], h_tables[1], parts[layer % 2], parts[1 - layer % 2], I["x"], x1 if layer == 2 else None,
                       r_table, relation_rows)
    return x1, h_tables


def crowded_gnn0(nc, c, I, edges, h_tables, x1):
    with Core(nc) as k:
        h, x = k.sb("w_h", [P, NT, D]), k.sb("w_x", [P, NT, D])
        acc = k.sb("w_acc", [P, NT + 1, D + 1])
        every = k.sb("w_every", [P, EDGE_TILES, 4], I32)
        part_i = k.sb("w_part_i", [P, 2, EDGE_TILES], I32)
        part = k.sb("w_part", [P, 2, EDGE_TILES])
        ed, dst_f = k.sb("w_ed", [P, G, 4], I32), k.sb("w_dst", [P, G])
        onehot, rows = k.sb("w_onehot", [P, G, P]), k.sb("w_rows", [P, G, D + 1])
        wl, wr = k.sb("w_wl", [P, KD, D]), k.sb("w_wr", [P, KD, D])
        vecs, mul, shift, z = k.sb("w_vecs", [P, 5, D]), k.sb("w_mul", [P, D]), k.sb("w_shift", [P, D]), k.sb("w_z", [P, D])
        own, h_now, turned = k.sb("w_own", [P, D]), k.sb("w_h_now", [P, D]), k.sb("w_turned", [P, 4, P])
        low, tile_of = k.sb("w_low", [P, P]), k.sb("w_tile_of", [P, NT])
        clip = k.sb("w_clip", [P, NT])
        sums, turns, result, counted = (k.ps(f"w_{x}", [P, 512]) for x in ("sums", "turns", "result", "counted"))
        (s_start, s_ed, s_w, s_link, s_oh, s_sum, s_added, s_own, s_turn, s_turned, s_z, s_tile, s_saved, s_var, s_root,
         s_one, s_used, s_cnt, s_table) = (k.sem(f"w_{x}") for x in (
             "start", "ed", "weights", "link", "onehot", "sum", "added", "own", "turn", "turned", "z", "tile", "saved", "var",
             "root", "one", "used", "counted", "table"))
        s_rows = c.pool_sem("w_rows")
        by_tile = "(t p) d -> p t d"
        with nc.Block() as block:

            @block.sync
            def _(sp):
                crowded = sp.value_load(c.flags[0:1, 1:2], min_val=0, max_val=1)
                with sp.If(crowded):
                    sp.dma_start(h[:, :, :], h_tables[0][0:NP, :].rearrange(by_tile, p=P)).then_inc(s_start, 16)
                    sp.dma_start(x[:, :, :], I["x"][0:NP, :].rearrange(by_tile, p=P)).then_inc(s_start, 16)
                    sp.dma_start(every[:, :, :], edges[0:EDGE_TILES * P, :].rearrange("(p k) c -> p k c", p=P)).then_inc(s_start, 16)
                    for layer in range(3):
                        with sp.Fori(0, GROUPS) as g:
                            start = sp.value_load(c.tab["g_start"][0:1, bass.ds(g, 1)], min_val=0, max_val=EDGE_TILES * P)
                            src = edges[bass.ds(start, GE), :].rearrange("(p k) c -> p k c", p=P)
                            sp.wait_ge(s_added, g + layer * GROUPS + 1)
                            sp.dma_start(ed[:, :, :], src).then_inc(s_ed, 16)
                        if layer:
                            sp.wait_ge(s_tile, layer * NT)
                        loads = [(wl[:, :, :], I["L0_gnn_Wl"][layer].rearrange("(k p) n -> p k n", p=P)),
                                 (wr[:, :, :], I["L0_gnn_Wr"][layer].rearrange("(k p) n -> p k n", p=P)),
                                 *[(vecs[:, q, :], row(I[f"L0_gnn_{v}"][layer])) for q, v in enumerate(("b", "gamma", "beta", "rmean", "rvar"))]]
                        for out, src in loads:
                            sp.dma_start(out, src, allow_slow_non_contiguous=True).then_inc(s_w, 16)
                        sp.wait_ge(s_tile, (layer + 1) * NT)
                        table = x1 if layer == 2 else h_tables[1]
                        sp.dma_start(table[0:NP, :].rearrange(by_tile, p=P), h[:, :, :]).then_inc(s_saved, 16)
                        sp.wait_ge(s_saved, 16 * (layer + 1))
                        sp.sem_inc(s_table, 1)

            @block.gpsimd
            def _(pool):
                crowded = pool.value_load(c.flags[0:1, 1:2], min_val=0, max_val=1)
                with pool.If(crowded):
                    for layer in range(3):
                        if layer:
                            pool.wait_ge(s_table, layer)
                        with pool.Fori(0, GROUPS) as g:
                            pool.wait_ge(s_ed, g * 16 + layer * GROUPS * 16 + 16)
                            pool.sem_inc(s_one, 1)
                            for t in range(G):
                                pool.indirect_dma_start(rows[:, t, 0:D], None, h_tables[min(layer, 1)],
                                                        bass.IndirectOffsetOnAxis(ap=ed[:, t, 0:1], axis=0)).then_inc(s_rows, 16)

            @block.vector
            def _(dve):
                v, st = nc.vector, Steps(dve, s_link)
                crowded = dve.value_load(c.flags[0:1, 1:2], min_val=0, max_val=1)
                with dve.If(crowded):
                    dve.wait_ge(s_start, 48)
                    v.memset(rows[:, :, D:D + 1], 1.0)
                    v.tensor_scalar(part_i[:, 0, :], every[:, :, 3], P - 1, None, ALU.bitwise_and)
                    st.link(v.tensor_scalar(part_i[:, 1, :], every[:, :, 3], P.bit_length() - 1, None, ALU.arith_shift_right))
                    st.link(v.tensor_copy(part[:, :, :], part_i[:, :, :]))
                    with dve.Fori(0, EDGE_TILES) as e:
                        dve.wait_ge(s_used, e + 1)
                        v.tensor_scalar(low[:, :], c.iota[:, 0:P], part[:, 0, bass.ds(e, 1)], None, ALU.is_equal)
                        v.tensor_scalar(tile_of[:, :], c.iota[:, 0:NT], part[:, 1, bass.ds(e, 1)], None, ALU.is_equal).then_inc(s_cnt, 1)
                    dve.wait_ge(s_used, EDGE_TILES + 2)
                    v.tensor_copy(c.deg[:, 0, 0:NT], counted[:, 0:NT])
                    dve.sem_inc(s_added, 1)
                    for layer in range(3):
                        st.link(v.memset(acc[:, :, :], 0.0))
                        with dve.Fori(0, GROUPS) as g, st.each(g, GROUPS, 2):
                            tile = dve.value_load(c.tab["g_tile"][0:1, bass.ds(g + 1, 1)], min_val=0, max_val=NT)
                            dve.wait_ge(s_ed, g * 16 + layer * GROUPS * 16 + 16)
                            st.link(v.tensor_copy(dst_f[:, :], ed[:, :, 1]))
                            st.link(v.tensor_scalar(dst_f[:, :], dst_f[:, :], c.tab["g_base"][:, bass.ds(g, 1)], None, ALU.subtract))
                            for t in range(G):
                                last = v.tensor_scalar(onehot[:, t, :], c.iota[:, 0:P], dst_f[:, t:t + 1], None, ALU.is_equal)
                            last.then_inc(s_oh, 1)
                            dve.wait_ge(s_sum, g + layer * GROUPS + 1)
                            here = acc[:, bass.ds(tile, 1), :].rearrange("p a d -> p (a d)")
                            v.tensor_tensor(here, here, sums[:, 0:D + 1], ALU.add).then_inc(s_added, 1)
                        dve.wait_ge(s_added, (layer + 1) * GROUPS + 1)
                        if layer == 0:
                            v.tensor_copy(c.deg[:, 1, 0:NT], acc[:, 0:NT, D])
                            st.link(v.tensor_scalar_max(clip[:, :], acc[:, 0:NT, D], 1.0))
                            st.link(v.reciprocal(c.rdeg[:, 0:NT], clip[:, :]))
                        dve.wait_ge(s_w, 16 * 7 * (layer + 1))
                        v.tensor_scalar_add(vecs[:, 4, :], vecs[:, 4, :], EPS).then_inc(s_var, 1)
                        dve.wait_ge(s_root, layer + 1)
                        st.link(v.reciprocal(mul[:, :], shift[:, :]))
                        st.link(v.tensor_tensor(mul[:, :], mul[:, :], vecs[:, 1, :], ALU.mult))
                        st.link(v.tensor_tensor(shift[:, :], vecs[:, 0, :], vecs[:, 3, :], ALU.subtract))
                        st.link(v.tensor_tensor(shift[:, :], shift[:, :], mul[:, :], ALU.mult))
                        st.link(v.tensor_tensor(shift[:, :], shift[:, :], vecs[:, 2, :], ALU.add))
                        with dve.Fori(0, NT) as t, st.each(t, NT, 3 if layer == 2 else 2):
                            hs = h[:, bass.ds(t, 1), :].rearrange("p a d -> p (a d)")
                            v.tensor_copy(h_now[:, :], hs)
                            v.tensor_scalar(own[:, :], acc[:, bass.ds(t, 1), 0:D].rearrange("p a d -> p (a d)"), c.rdeg[:, bass.ds(t, 1)],
                                            None, ALU.mult).then_inc(s_own, 1)
                            dve.wait_ge(s_turn, t + layer * NT + 1)
                            v.tensor_copy(turned[:, :, :].rearrange("p q c -> p (q c)"), turns[:, :]).then_inc(s_turned, 1)
                            dve.wait_ge(s_z, t + layer * NT + 1)
                            st.link(v.tensor_tensor(z[:, :], result[:, 0:D], mul[:, :], ALU.mult))
                            st.link(v.tensor_tensor(z[:, :], z[:, :], shift[:, :], ALU.add))
                            if layer < 2:
                                v.scalar_tensor_tensor(hs, z[:, :], 0.0, hs, ALU.max, ALU.add).then_inc(s_tile, 1)
                            else:
                                st.link(v.tensor_tensor(z[:, :], z[:, :], hs, ALU.add))
                                v.tensor_tensor(hs, z[:, :], x[:, bass.ds(t, 1), :].rearrange("p a d -> p (a d)"), ALU.add).then_inc(s_tile, 1)

            @block.tensor
            def _(pe):
                crowded = pe.value_load(c.flags[0:1, 1:2], min_val=0, max_val=1)
                with pe.If(crowded):
                    nc.tensor.matmul(counted[:, 0:NT], c.zero_b[:, 0:P], c.zero_b[:, 0:NT], start=True, stop=False).then_inc(s_used, 1)
                    with pe.Fori(0, EDGE_TILES) as e:
                        pe.wait_ge(s_cnt, e + 1)
                        nc.tensor.matmul(counted[:, 0:NT], low[:, :], tile_of[:, :], start=False, stop=False).then_inc(s_used, 1)
                    nc.tensor.matmul(counted[:, 0:NT], c.zero_b[:, 0:P], c.zero_b[:, 0:NT], start=False, stop=True).then_inc(s_used, 1)
                    for layer in range(3):
                        with pe.Fori(0, GROUPS) as g:
                            pe.wait_ge(s_oh, g + layer * GROUPS + 1)
                            pe.wait_ge(s_rows, g * (16 * G) + layer * GROUPS * 16 * G + 16 * G)
                            for t in range(G):
                                last = nc.tensor.matmul(sums[:, 0:D + 1], onehot[:, t, :], rows[:, t, :], start=t == 0, stop=t == G - 1)
                            last.then_inc(s_sum, 1)
                        with pe.Fori(0, NT) as t:
                            pe.wait_ge(s_own, t + layer * NT + 1)
                            for hf in range(KD):
                                nc.tensor.transpose(turns[:, hf * P:hf * P + P], own[:, hf * P:hf * P + P], c.ident[:, :])
                            for hf in range(KD):
                                last = nc.tensor.transpose(turns[:, (2 + hf) * P:(3 + hf) * P], h_now[:, hf * P:hf * P + P], c.ident[:, :])
                            last.then_inc(s_turn, 1)
                            pe.wait_ge(s_turned, t + layer * NT + 1)
                            for q, w in enumerate((wl, wr)):
                                for hf in range(KD):
                                    last = nc.tensor.matmul(result[:, 0:D], turned[:, 2 * q + hf, :], w[:, hf, :],
                                                            start=q == 0 and hf == 0, stop=q == 1 and hf == 1)
                            last.then_inc(s_z, 1)

            @block.scalar
            def _(act):
                crowded = act.value_load(c.flags[0:1, 1:2], min_val=0, max_val=1)
                with act.If(crowded):
                    for layer in range(3):
                        act.wait_ge(s_var, layer + 1)
                        nc.scalar.activation(shift[:, :], vecs[:, 4, :], ACT.Sqrt).then_inc(s_root, 1)


def experts(nc, c, I, name, ne, nf, tiles, which, w1, b1, w2, b2, gate_w, gate_b, norm, act_fn, combine_rows):
    FC = nf // P
    xs = c.dram(f"{name}_xs", [(tiles + 1) * P, D])
    ys = c.dram(f"{name}_ys", [tiles * P, D])
    with Core(nc) as k:
        xn = k.sb(f"{name}_xn", [P, NT, D])
        layernorm(nc, c, f"{name}_ln", c.x, xn)
        gate = k.sb(f"{name}_gate", [P, KD, ne])
        gate_bias = k.sb(f"{name}_gate_bias", [P, ne])
        logits = k.sb(f"{name}_logits", [P, NT, ne])
        load_all(nc, f"{name}_g", [(gate[:, :, :], gate_w.rearrange("(k p) n -> p k n", p=P)),
                                   (gate_bias[:, :], row(gate_b))])

        def keep(v, st, t0, z):
            return v.tensor_tensor(logits[:, bass.ds(t0, J), :], z, bc(gate_bias[:, :].unsqueeze(1), [P, J, ne]), ALU.add)

        dense(nc, c, f"{name}_gd", xn, gate, ne, keep)
        weight = k.sb(f"{name}_weight", [P, 2, NT])
        slot = k.sb(f"{name}_slot", [P, 2, NT], I32)
        e_tab = k.sb(f"{name}_etab", [1, tiles], I32)
        route(nc, c, name, ne, tiles, which, logits, weight, slot, e_tab, xn, xs)
        run_experts(nc, c, name, ne, nf, FC, tiles, xs, ys, e_tab, w1, b1, w2, b2, norm, act_fn)
        combine_rows(ys, weight, slot, xn)


def route(nc, c, name, ne, tiles, softmax_first, logits, weight, slot, e_tab, xn, xs):
    with Core(nc) as k:
        top = k.sb(f"{name}_top", [P, NT, 8])
        idx = k.sb(f"{name}_idx", [P, NT, 8], U32)
        idx_f = k.sb(f"{name}_idx_f", [P, 2, NT])
        pick = k.sb(f"{name}_pick", [P, 2, NT, ne])
        both = k.sb(f"{name}_both", [P, NT, ne])
        place = k.sb(f"{name}_place", [P, NT, ne])
        sums = k.sb(f"{name}_sums", [P, NT + 1, ne])
        small = k.sb(f"{name}_small", [P, 4, NT])
        per = k.sb(f"{name}_per", [P, 6, ne])
        per_i = k.sb(f"{name}_per_i", [P, 2, ne], I32)
        done = k.sb(f"{name}_done", [1, tiles, ne])
        done_f = k.sb(f"{name}_done_f", [1, tiles])
        slot_f = k.sb(f"{name}_slot_f", [P, 2, NT])
        zero = k.sb(f"{name}_zero", [P, 2048])
        rank = k.ps(f"{name}_rank", [P, 512])
        total = k.ps(f"{name}_total", [P, 512])
        s_link, s_a, s_b, s_m, s_rank, s_slot, s_z, s_zd = (
            k.sem(f"{name}_r{x}") for x in ("link", "to_act", "to_dve", "both", "rank", "slot", "zero", "zeroed"))
        s_sc = c.pool_sem(f"{name}_scatter")
        wide = [P, NT, ne]
        rows_total = (tiles + 1) * P * D
        with nc.Block() as block:

            @block.vector
            def _(dve):
                v, st = nc.vector, Steps(dve, s_link)
                v.memset(zero[:, :], 0.0).then_inc(s_z, 1)
                if softmax_first:
                    st.link(v.tensor_reduce(small[:, 0, :], logits[:, :, :], AX.X, ALU.max))
                    v.tensor_tensor(logits[:, :, :], logits[:, :, :], bc(small[:, 0, :].unsqueeze(2), wide), ALU.subtract)\
                        .then_inc(s_a, 1)
                    dve.wait_ge(s_b, 1)
                    st.link(v.tensor_reduce(small[:, 1, :], logits[:, :, :], AX.X, ALU.add))
                    st.link(v.reciprocal(small[:, 2, :], small[:, 1, :]))
                    st.link(v.tensor_tensor(logits[:, :, :], logits[:, :, :], bc(small[:, 2, :].unsqueeze(2), wide), ALU.mult))
                for t in range(NT):
                    last = v.max(top[:, t, :], logits[:, t, :])
                st.link(last)
                for t in range(NT):
                    last = v.max_index(idx[:, t, :], top[:, t, :], logits[:, t, :])
                st.link(last)
                if softmax_first:
                    st.link(v.tensor_tensor(small[:, 0, :], top[:, :, 0], top[:, :, 1], ALU.add))
                    st.link(v.reciprocal(small[:, 1, :], small[:, 0, :]))
                    for q in range(2):
                        v.tensor_tensor(weight[:, q, :], top[:, :, q], small[:, 1, :], ALU.mult)
                else:
                    v.tensor_tensor(small[:, 0, :], top[:, :, 1], top[:, :, 0], ALU.subtract).then_inc(s_a, 1)
                    dve.wait_ge(s_b, 1)
                    st.link(v.tensor_scalar_add(small[:, 2, :], small[:, 1, :], 1.0))
                    st.link(v.reciprocal(weight[:, 0, :], small[:, 2, :]))
                    v.tensor_tensor(weight[:, 1, :], weight[:, 0, :], small[:, 1, :], ALU.mult)
                for q in range(2):
                    last = v.tensor_copy(idx_f[:, q, :], idx[:, :, q])
                st.link(last)
                for q in range(2):
                    last = v.tensor_tensor(pick[:, q, :, :], bc(c.iota[:, 0:ne].unsqueeze(1), wide),
                                           bc(idx_f[:, q, :].unsqueeze(2), wide), ALU.is_equal)
                st.link(last)
                st.link(v.tensor_tensor(both[:, :, :], pick[:, 0, :, :], pick[:, 1, :, :], ALU.add))
                v.tensor_scalar(both[:, NT - 1, :], both[:, NT - 1, :], c.alive[:, 0:1], None, ALU.mult).then_inc(s_m, 1)
                dve.wait_ge(s_rank, 1)
                st.link(v.memset(sums[:, 0, :], 0.0))
                for t in range(NT):
                    st.link(v.tensor_tensor(sums[:, t + 1, :], sums[:, t, :], total[:, t * ne:(t + 1) * ne], ALU.add))
                st.link(v.tensor_copy(per[:, 0, :], sums[:, NT, :]))
                group_table(v, st, per, per_i, ne, P)
                st.link(v.tensor_tensor(place[:, :, :], rank[:, 0:NT * ne].rearrange("p (t e) -> p t e", e=ne), sums[:, 0:NT, :], ALU.add))
                st.link(v.tensor_tensor(place[:, :, :], place[:, :, :], bc(per[:, 5, :].unsqueeze(1), wide), ALU.add))
                for q in range(2):
                    last = v.tensor_tensor(pick[:, q, :, :], pick[:, q, :, :], place[:, :, :], ALU.mult)
                st.link(last)
                st.link(v.tensor_reduce(slot_f[:, :, :], pick[:, :, :, :], AX.X, ALU.add))
                v.tensor_copy(slot[:, :, :], slot_f[:, :, :]).then_inc(s_slot, 1)
                st.link(v.tensor_tensor(done[:, :, :], bc(c.iota[0:1, 0:tiles].unsqueeze(2), [1, tiles, ne]),
                                        bc(per[0:1, 3, :].unsqueeze(1), [1, tiles, ne]), ALU.is_ge))
                st.link(v.tensor_reduce(done_f[:, :], done[:, :, :], AX.X, ALU.add))
                st.link(v.tensor_scalar_min(done_f[:, :], done_f[:, :], float(ne - 1)))
                v.tensor_copy(e_tab[:, :], done_f[:, :])

            @block.scalar
            def _(act):
                act.wait_ge(s_a, 1)
                if softmax_first:
                    nc.scalar.activation(logits[:, :, :], logits[:, :, :], ACT.Exp).then_inc(s_b, 1)
                else:
                    nc.scalar.activation(small[:, 1, :], small[:, 0, :], ACT.Exp).then_inc(s_b, 1)

            @block.tensor
            def _(pe):
                pe.wait_ge(s_m, 1)
                flat = both[:, :, :].rearrange("p t e -> p (t e)")
                nc.tensor.matmul(rank[:, 0:NT * ne], c.before[:, :], flat, start=True, stop=True)
                nc.tensor.matmul(total[:, 0:NT * ne], c.ones[:, :], flat, start=True, stop=True).then_inc(s_rank, 1)

            @block.sync
            def _(sp):
                sp.wait_ge(s_z, 1)
                view = xs.rearrange("(p a) d -> p (a d)", p=P)
                n, at = rows_total // P, 0
                for at in range(0, n, 2048):
                    w = min(2048, n - at)
                    sp.dma_start(view[:, at:at + w], zero[:, 0:w]).then_inc(s_zd, 16)

            @block.gpsimd
            def _(pool):
                pool.wait_ge(s_zd, 16 * -(-(rows_total // P) // 2048))
                pool.wait_ge(s_slot, 1)
                for t in range(NT):
                    n = P if t < NT - 1 else TAIL
                    for q in range(2):
                        pool.indirect_dma_start(xs, bass.IndirectOffsetOnAxis(ap=slot[0:n, q, t:t + 1], axis=0),
                                                xn[0:n, t, :], None).then_inc(s_sc, 16)
                pool.wait_ge(s_sc, 16 * 2 * NT)


def run_experts(nc, c, name, ne, nf, FC, tiles, xs, ys, e_tab, w1, b1, w2, b2, norm, act_fn):
    with Core(nc) as k:
        w1b = k.sb(f"{name}_w1", [P, 2, KD, nf])
        w2b = k.sb(f"{name}_w2", [P, 2, FC, D])
        xb = k.sb(f"{name}_xb", [P, 2, D])
        xT = k.sb(f"{name}_xT", [P, 2, KD, P])
        hT = k.sb(f"{name}_hT", [P, 2, FC, P])
        yb = k.sb(f"{name}_yb", [P, 2, D])
        b1s = k.sb(f"{name}_b1", [P, ne, FC])
        b2s = k.sb(f"{name}_b2", [P, ne, D])
        pX = [k.ps(f"{name}_pX{s}", [P, 512]) for s in range(2)]
        pH = [k.ps(f"{name}_pH{s}", [P, max(nf, 512)]) for s in range(2)]
        pY = [k.ps(f"{name}_pY{s}", [P, 512]) for s in range(2)]
        loads = [(b1s[:, :, :], b1), (b2s[:, :, :], b2.rearrange("(a e) d -> a e d", a=1).to_broadcast([P, ne, D]))]
        if norm:
            lg, lb = k.sb(f"{name}_lg", [P, ne, KD]), k.sb(f"{name}_lb", [P, ne, KD])
            loads += [(lg[:, :, :], norm[0]), (lb[:, :, :], norm[1])]
        load_all(nc, f"{name}_b", loads)
        s_w1 = [k.sem(f"{name}_w1_{s}") for s in range(2)]
        s_w2 = [k.sem(f"{name}_w2_{s}") for s in range(2)]
        s_x = [k.sem(f"{name}_x{s}") for s in range(2)]
        s_st = [c.pool_sem(f"{name}_st{s}") for s in range(2)]
        s_xt, s_xT, s_h, s_hT, s_y, s_yb, s_yfree, s_gate = (
            k.sem(f"{name}_e{x}") for x in ("xt", "xT", "h", "hT", "y", "yb", "yfree", "gate"))
        BF = 512 // P
        HB = FC // BF
        with nc.Block() as block:

            @block.sync
            def _(sp):
                sp.dma_start(xb[:, 0, :], xs[0:P, :]).then_inc(s_x[0], 16)
                with sp.Fori(0, tiles // 2) as i:
                    for s in range(2):
                        t = 2 * i + s
                        e = sp.value_load(e_tab[0:1, bass.ds(t, 1)], min_val=0, max_val=ne - 1)
                        a1 = w1[bass.ds(e, 1), :, :].rearrange("a (k p) f -> p (a k) f", p=P)
                        a2 = w2[bass.ds(e, 1), :, :].rearrange("a (k p) f -> p (a k) f", p=P)
                        ax = xs[bass.ds(t * P + P, P), :]
                        sp.wait_ge(s_h, t * HB + HB)
                        sp.dma_start(w1b[:, s, :, :], a1).then_inc(s_w1[s], 16)
                        sp.wait_ge(s_xt, t + 1)
                        sp.dma_start(xb[:, 1 - s, :], ax).then_inc(s_x[1 - s], 16)
                        sp.wait_ge(s_y, t + 1)
                        sp.dma_start(w2b[:, s, :, :], a2).then_inc(s_w2[s], 16)

            @block.tensor
            def _(pe):
                def turn(t, s, u):
                    pe.wait_ge(s_x[s], u * 16)
                    for h in range(KD):
                        last = nc.tensor.transpose(pX[s][:, h * P:(h + 1) * P], xb[:, s, h * P:(h + 1) * P], c.ident[:, :])
                    last.then_inc(s_xt, 1)

                def hidden(t, s, u):
                    pe.wait_ge(s_w1[s], u * 16)
                    pe.wait_ge(s_xT, t + 1)
                    for f in range(FC):
                        for h in range(KD):
                            last = nc.tensor.matmul(pH[s][:, f * P:(f + 1) * P], w1b[:, s, h, f * P:(f + 1) * P],
                                                    xT[:, s, h, :], start=h == 0, stop=h == KD - 1)
                        if f % BF == BF - 1:
                            last.then_inc(s_h, 1)

                def result(t, s, u):
                    pe.wait_ge(s_w2[s], u * 16)
                    pe.wait_ge(s_yb, t + 1)
                    for f in range(FC):
                        pe.wait_ge(s_hT, t * FC + f + 1)
                        last = nc.tensor.matmul(pY[s][:, 0:D], hT[:, s, f, :], w2b[:, s, f, :], start=f == 0, stop=f == FC - 1)
                    last.then_inc(s_y, 1)

                pe.sem_inc(s_xt, 1)
                pe.sem_inc(s_h, 2 * HB)
                pe.sem_inc(s_y, 2)
                turn(0, 0, 1)
                hidden(0, 0, 1)
                turn(1, 1, 1)
                with pe.Fori(0, tiles // 2 - 1) as i:
                    t = 2 * i
                    hidden(t + 1, 1, i + 1)
                    turn(t + 2, 0, i + 2)
                    result(t, 0, i + 1)
                    hidden(t + 2, 0, i + 2)
                    turn(t + 3, 1, i + 2)
                    result(t + 1, 1, i + 1)
                hidden(tiles - 1, 1, tiles // 2)
                turn(tiles, 0, tiles // 2 + 1)
                result(tiles - 2, 0, tiles // 2)
                result(tiles - 1, 1, tiles // 2)

            @block.scalar
            def _(act):
                with act.Fori(0, tiles // 2) as i:
                    for s in range(2):
                        t = 2 * i + s
                        e = act.value_load(e_tab[0:1, bass.ds(t, 1)], min_val=0, max_val=ne - 1)
                        act.wait_ge(s_xt, t + 2)
                        for h in range(KD):
                            src = pX[s][:, h * P:(h + 1) * P]
                            if norm:
                                last = nc.scalar.activation(xT[:, s, h, :], src, ACT.Identity, bias=lb[:, bass.ds(e, 1), h],
                                                            scale=lg[:, bass.ds(e, 1), h])
                            else:
                                last = nc.scalar.activation(xT[:, s, h, :], src, ACT.Copy)
                        last.then_inc(s_xT, 1)
                        for f in range(FC):
                            if f % BF == 0:
                                act.wait_ge(s_h, t * HB + f // BF + 1 + 2 * HB)
                            nc.scalar.activation(hT[:, s, f, :], pH[s][:, f * P:(f + 1) * P], act_fn,
                                                 bias=b1s[:, bass.ds(e, 1), f]).then_inc(s_hT, 1)

            @block.vector
            def _(dve):
                dve.sem_inc(s_yb, 2)
                with dve.Fori(0, tiles // 2) as i:
                    for s in range(2):
                        t = 2 * i + s
                        e = dve.value_load(e_tab[0:1, bass.ds(t, 1)], min_val=0, max_val=ne - 1)
                        dve.wait_ge(s_y, t + 3)
                        dve.wait_ge(s_yfree, t + 1)
                        nc.vector.tensor_tensor(yb[:, s, :], pY[s][:, 0:D], b2s[:, bass.ds(e, 1), :].rearrange("p a d -> p (a d)"), ALU.add)\
                            .then_inc(s_yb, 1)

            @block.gpsimd
            def _(pool):
                pool.sem_inc(s_yfree, 2)
                with pool.Fori(0, tiles // 2) as i:
                    for s in range(2):
                        t = 2 * i + s
                        pool.wait_ge(s_yb, t + 3)
                        pool.sem_inc(s_gate, 1)
                        pool.dma_start(ys[bass.ds(t * P, P), :], yb[:, s, :]).then_inc(s_st[s], 16)
                        pool.wait_ge(s_st[s], i * 16 + 16)
                        pool.sem_inc(s_yfree, 1)


def norm_rows(dve, v, st, k, src, dst, s_var, s_root, n):
    for j in range(J):
        last = v.bn_stats(k.stats[:, j, :], src[:, j, :])
    st.link(last)
    v.tensor_tensor(k.mean[:, :], k.stats[:, :, 1], k.stats[:, :, 4], ALU.add)
    v.tensor_tensor(k.gap[:, :], k.stats[:, :, 1], k.stats[:, :, 4], ALU.subtract)
    st.link(v.tensor_tensor(k.var[:, :], k.stats[:, :, 2], k.stats[:, :, 5], ALU.add))
    v.tensor_scalar_mul(k.mean[:, :], k.mean[:, :], 0.5)
    v.tensor_tensor(k.gap[:, :], k.gap[:, :], k.gap[:, :], ALU.mult)
    st.link(v.tensor_scalar(k.var[:, :], k.var[:, :], 1.0 / D, EPS, ALU.mult, ALU.add))
    v.scalar_tensor_tensor(k.var[:, :], k.gap[:, :], 0.25, k.var[:, :], ALU.mult, ALU.add).then_inc(s_var, 1)
    dve.wait_ge(s_root, n)
    st.link(v.reciprocal(k.rstd[:, :], k.root[:, :]))
    for j in range(J):
        last = v.tensor_scalar(dst[:, j, :], src[:, j, :], k.mean[:, j:j + 1], k.rstd[:, j:j + 1], ALU.subtract, ALU.mult)
    st.link(last)


def gather_results(nc, c, name, k, ys, slot):
    k.got = k.sb(f"{name}_got", [P, 2, NT, D])
    k.s_got = [c.pool_sem(f"{name}_got{i}") for i in range(NJ)]
    k.s_rest = k.sem(f"{name}_rest")

    def work(pool):
        pool.memset(k.got[:, :, NT - 1, :], 0.0).then_inc(k.s_rest, 1)
        for i in range(NJ):
            if i == NJ - 1:
                pool.wait_ge(k.s_rest, 1)
            for t in range(i * J, i * J + J):
                n = P if t < NT - 1 else TAIL
                for q in range(2):
                    pool.indirect_dma_start(k.got[0:n, q, t, :], None, ys,
                                            bass.IndirectOffsetOnAxis(ap=slot[0:n, q, t:t + 1], axis=0)).then_inc(k.s_got[i], 16)

    return work


def weigh(dve, v, st, k, weight, i):
    wide = [P, J, D]
    ts = slice(i * J, i * J + J)
    dve.wait_ge(k.s_got[i], 16 * 2 * J)
    for q in range(2):
        last = v.tensor_tensor(k.got[:, q, ts, :], k.got[:, q, ts, :], bc(weight[:, q, ts].unsqueeze(2), wide), ALU.mult)
    st.link(last)
    st.link(v.tensor_tensor(k.got[:, 0, ts, :], k.got[:, 0, ts, :], k.got[:, 1, ts, :], ALU.add))


def combine_and_store(nc, c, name, ys, weight, slot, xn, out):
    with Core(nc) as k:
        work = gather_results(nc, c, name, k, ys, slot)
        s_link, s_y, s_out = (k.sem(f"{name}_c{x}") for x in ("link", "y", "out"))
        with nc.Block() as block:

            @block.gpsimd
            def _(pool):
                work(pool)

            @block.vector
            def _(dve):
                v, st = nc.vector, Steps(dve, s_link)
                for i in range(NJ):
                    ts = slice(i * J, i * J + J)
                    weigh(dve, v, st, k, weight, i)
                    v.tensor_tensor(xn[:, ts, :], c.x[:, ts, :], k.got[:, 0, ts, :], ALU.add).then_inc(s_y, 1)

            @block.sync
            def _(sp):
                for i in range(NJ):
                    sp.wait_ge(s_y, i + 1)
                    t0, t1 = i * J, min(i * J + J, NT - 1)
                    sp.dma_start(out[t0 * P:t1 * P, :].rearrange("(t p) d -> p t d", p=P), xn[:, t0:t1, :]).then_inc(s_out, 16)
                sp.dma_start(out[(NT - 1) * P:N, :], xn[0:TAIL, NT - 1, :]).then_inc(s_out, 16)
                sp.wait_ge(s_out, 16 * (NJ + 1))


def combine_and_norm(nc, c, name, I, ys, weight, slot, xn, h_table):
    with Core(nc) as k:
        work = gather_results(nc, c, name, k, ys, slot)
        g, b = k.sb(f"{name}_gamma", [P, D]), k.sb(f"{name}_beta", [P, D])
        k.stats, k.mean, k.gap, k.var, k.root, k.rstd = (k.sb(f"{name}_{x}", [P, J] + more) for x, more in (
            ("stats", [6]), ("mean", []), ("gap", []), ("var", []), ("root", []), ("rstd", [])))
        out = k.sb(f"{name}_out", [P, 2, J, W1])
        clip = k.sb(f"{name}_clip", [P, 2, NT])
        s_link, s_gb, s_var, s_root, s_clip, s_h = (k.sem(f"{name}_n{x}") for x in ("link", "gb", "var", "root", "clip", "h"))
        s_saved = [k.sem(f"{name}_saved{q}") for q in range(2)]
        with nc.Block() as block:

            @block.gpsimd
            def _(pool):
                work(pool)

            @block.sync
            def _(sp):
                sp.dma_start(g[:, :], row(I["L0_ffn_gamma"])).then_inc(s_gb, 16)
                sp.dma_start(b[:, :], row(I["L0_ffn_beta"])).then_inc(s_gb, 16)
                for i in range(NJ):
                    sp.wait_ge(s_h, i + 1)
                    sp.dma_start(h_table[i * J * P:(i + 1) * J * P, :].rearrange("(t p) d -> p t d", p=P), out[:, i % 2, :, :])\
                        .then_inc(s_saved[i % 2], 16)
                for q in range(2):
                    sp.wait_ge(s_saved[q], 16 * ((NJ + 1 - q) // 2))

            @block.scalar
            def _(act):
                act.wait_ge(s_clip, 1)
                nc.scalar.activation(clip[:, :, :], clip[:, :, :], ACT.Sqrt).then_inc(s_root, 1)
                for i in range(2 * NJ):
                    act.wait_ge(s_var, i + 1)
                    nc.scalar.activation(k.root[:, :], k.var[:, :], ACT.Sqrt).then_inc(s_root, 1)

            @block.vector
            def _(dve):
                v, st = nc.vector, Steps(dve, s_link)
                wide = [P, J, D]
                v.tensor_scalar_max(clip[:, :, :], c.deg[:, :, 0:NT], 1.0).then_inc(s_clip, 1)
                v.memset(out[:, :, :, D:W1], 0.0)
                dve.wait_ge(s_root, 1)
                v.reciprocal(c.norm_dst[:, :], clip[:, 1, :])
                st.link(v.reciprocal(c.norm_src[:, :], clip[:, 0, :]))
                dve.wait_ge(s_gb, 32)
                for i in range(NJ):
                    ts = slice(i * J, i * J + J)
                    y, x, h = k.got[:, 0, ts, :], c.x[:, ts, :], c.h[:, ts, :]
                    weigh(dve, v, st, k, weight, i)
                    st.link(v.tensor_tensor(y, xn[:, ts, :], y, ALU.add))
                    norm_rows(dve, v, st, k, y, y, s_var, s_root, 2 * i + 2)
                    st.link(v.tensor_tensor(y, y, bc(g[:, :].unsqueeze(1), wide), ALU.mult))
                    st.link(v.tensor_tensor(y, y, bc(b[:, :].unsqueeze(1), wide), ALU.add))
                    st.link(v.tensor_tensor(x, x, y, ALU.add))
                    norm_rows(dve, v, st, k, x, h, s_var, s_root, 2 * i + 3)
                    if i >= 2:
                        dve.wait_ge(s_saved[i % 2], 16 * (i // 2))
                    v.tensor_tensor(out[:, i % 2, :, 0:D], h, bc(c.norm_src[:, ts].unsqueeze(2), wide), ALU.mult)
                    v.tensor_copy(out[:, i % 2, :, D], c.norm_src[:, ts]).then_inc(s_h, 1)


def clifford(nc, c, name, w, bias, out, bias_out, split):
    C = D // 4
    table = ((0, 1, 2, -3), (1, 0, -3, 2), (2, 3, 0, -1), (3, 2, 1, 0))
    with Core(nc) as k:
        raw = k.sb(f"{name}_raw", [P, KD, 4, C])
        raw_b = k.sb(f"{name}_raw_b", [P, D])
        s_l = k.sem(f"{name}_load")
        with nc.Block() as block:

            @block.sync
            def _(sp):
                for bo in range(4):
                    for bi in range(4):
                        at = (bi % 2) * C
                        sp.dma_start(raw[at:at + C, bi // 2, bo, :], w[abs(table[bo][bi])]).then_inc(s_l, 16)
                sp.dma_start(raw_b[:, :], row(bias)).then_inc(s_l, 16)

            @block.vector
            def _(dve):
                dve.wait_ge(s_l, 16 * 17)
                v = nc.vector
                for h in range(KD):
                    view = out[:, h, :]
                    view = view.rearrange("p (c b) -> p b c", b=4) if split else view.rearrange("p (b c) -> p b c", b=4)
                    for bo in range(4):
                        for half in range(2):
                            at = half * C
                            sign = -1.0 if table[bo][2 * h + half] < 0 else 1.0
                            v.tensor_scalar_mul(view[at:at + C, bo, :], raw[at:at + C, h, bo, :], sign)
                b = bias_out[:, :].rearrange("p (c b) -> p b c", b=4) if split else bias_out[:, :].rearrange("p (b c) -> p b c", b=4)
                v.tensor_copy(b, raw_b[:, :].rearrange("p (b c) -> p b c", b=4))


def gnn1(nc, c, I, edges, relation_rows, h_table):
    with Core(nc) as k:
        h = c.h
        acc = k.sb("acc1", [P, NT + 1, D + 1])
        aggregate(nc, c, "agg_r", edges, h_table, W1, acc, relation_rows)
        wm, bm = k.sb("msg", [P, KD, D]), k.sb("msg_bias", [P, D])
        wu, bu = k.sb("upd", [P, KD, D]), k.sb("upd_bias", [P, D])
        tmp = k.sb("g1_tmp", [P, J, D])
        clifford(nc, c, "cm", I["L1_gnn_msg_w"], I["L1_gnn_msg_b"].rearrange("b c -> (b c)"), wm, bm, False)
        clifford(nc, c, "cu", I["L1_gnn_upd_w"], I["L1_gnn_upd_b"].rearrange("b c -> (b c)"), wu, bu, True)

        def messages(v, st, t0, z):
            wide = [P, J, D]
            now = h[:, t0:t0 + J, :]
            st.link(v.tensor_tensor(tmp[:, :, :], bc(bm[:, :].unsqueeze(1), wide), bc(acc[:, t0:t0 + J, D:D + 1], wide), ALU.mult))
            st.link(v.tensor_tensor(tmp[:, :, :], tmp[:, :, :], z, ALU.add))
            st.link(v.tensor_tensor(tmp[:, :, :], tmp[:, :, :], bc(c.norm_dst[:, t0:t0 + J].unsqueeze(2), wide), ALU.mult))
            return v.tensor_tensor(now, now, tmp[:, :, :], ALU.add)

        dense(nc, c, "msgs", acc, wm, D, messages)

        def update(v, st, t0, z):
            wide = [P, J, D]
            out = c.x[:, bass.ds(t0, J), :].rearrange("p j d -> p (j d)")
            st.link(v.tensor_tensor(tmp[:, :, :], z, bc(bu[:, :].unsqueeze(1), wide), ALU.add))
            return v.tensor_tensor(out, out, tmp[:, :, :].rearrange("p j d -> p (j d)"), ALU.add)

        dense(nc, c, "updg", h, wu, D, update)


def build(nc, I, out):
    with Core(nc) as c:
        c.rdeg = c.sb("rdeg", [P, NTP])
        c.deg = c.sb("deg", [P, 2, NTP])
        c.norm_src, c.norm_dst = c.sb("norm_src", [P, NT]), c.sb("norm_dst", [P, NT])
        c.alive = c.sb("alive", [P, 1])
        c.zero_b = c.sb("zero_b", [P, 512], BF16)
        c.records = c.dram("records", [EDGE_ROWS, 4])
        relation_rows = c.dram("relation_rows", [EDGE_ROWS, W1])
        r_table = c.dram("r1_table", [RT * P, W1])
        edges = c.dram("ordered_edges", [EDGE_ROWS, 4], I32)
        c.flags = c.sb("flags", [1, 2], I32)
        c.largest = c.sb("largest", [1, 1])
        c.kinds = c.sb("kinds", [P, EDGE_TILES], I16)
        constants(nc, c)
        s_al, s_none, s_tail = c.sem("alive_set"), c.sem("none_set"), c.sem("tail_saved")
        tables = {"a_strip": ([P, GROUPS_A], F32), "a_start": ([1, GROUPS_A], I32), "a_col": ([1, GROUPS_A], I32),
                  "g_base": ([P, GROUPS], F32), "g_start": ([1, GROUPS], I32), "g_tile": ([1, GROUPS + 1], I32)}
        c.tab = {}
        for name, (shape, dt) in tables.items():
            c.tab[name + "_d"] = c.dram(name + "_d", shape, dt)
        relation_tables(nc, c, I, r_table)
        with Core(nc) as k:
            none = k.sb("none_rows", [P, 8, W1])
            c.wide_iota = k.sb("wide_iota", [P, GROUPS_A])
            wide_i = k.sb("wide_i", [P, GROUPS_A], I32)
            s_wide = k.sem("wide_set")
            for name, (shape, dt) in tables.items():
                c.tab[name] = k.sb(name + "_work", shape, dt)
            with nc.Block() as block:

                @block.vector
                def _(dve):
                    nc.vector.memset(none[:, :, :], 0.0).then_inc(s_none, 1)
                    nc.vector.memset(c.zero_b[:, :], 0.0)
                    dve.wait_ge(s_wide, 1)
                    nc.vector.tensor_copy(c.wide_iota[:, :], wide_i[:, :])

                @block.gpsimd
                def _(pool):
                    pool.iota(wide_i[:, :], pattern=[[1, GROUPS_A]], base=0, channel_multiplier=0).then_inc(s_wide, 1)
                    pool.memset(c.alive[:, :], 1.0).then_inc(s_al, 1)
                    pool.wait_ge(s_al, 1)
                    pool.affine_select(out=c.alive[:, :], in_=c.alive[:, :], compare_op=ALU.is_gt, fill=0.0,
                                       base=TAIL, pattern=[[0, 1]], channel_multiplier=-1)

                @block.sync
                def _(sp):
                    sp.wait_ge(s_none, 1)
                    sp.dma_start(relation_rows[EDGE_TILES * P:EDGE_ROWS, :].rearrange("(p k) c -> p k c", p=P), none[:, :, :])\
                        .then_inc(s_tail, 16)
                    sp.wait_ge(s_tail, 16)

            prepare_edges(nc, c, I["edges"], edges, c.records)
            s_tab = k.sem("tables_saved")
            with nc.Block() as block:

                @block.sync
                def _(sp):
                    for name in tables:
                        sp.dma_start(c.tab[name + "_d"], c.tab[name][:, :]).then_inc(s_tab, 16)
                    sp.wait_ge(s_tab, 16 * len(tables))

        x1, h_tables = gnn0(nc, c, I, edges, r_table, relation_rows)
        for name in ("g_base", "g_start", "g_tile"):
            c.tab[name] = c.sb(name, *tables[name])
        load_all(nc, "groups", [(c.tab[n][:, :], c.tab[n + "_d"]) for n in ("g_base", "g_start", "g_tile")])
        crowded_gnn0(nc, c, I, edges, h_tables, x1)
        c.x = c.sb("x", [P, NT, D])
        load_all(nc, "again", [(c.x[:, :, :], x1[0:NP, :].rearrange("(t p) d -> p t d", p=P))])

        c.h = c.sb("h1", [P, NT, D])
        h1_table = c.dram("h1_table", [NP, W1])

        def finish0(ys, weight, slot, xn):
            combine_and_norm(nc, c, "f0", I, ys, weight, slot, xn, h1_table)

        experts(nc, c, I, "f0", E0, F0, TILES0, False, I["L0_ffn_w1"], I["L0_ffn_b1"], I["L0_ffn_w2"], I["L0_ffn_b2"],
                I["L0_ffn_gate_w"], I["L0_ffn_gate_b"], None, ACT.Relu, finish0)
        gnn1(nc, c, I, edges, relation_rows, h1_table)

        def finish1(ys, weight, slot, xn):
            combine_and_store(nc, c, "f1", ys, weight, slot, xn, out)

        experts(nc, c, I, "f1", E1, F1, TILES1, True, I["L1_ffn_W1"], I["L1_ffn_b1"], I["L1_ffn_W2"], I["L1_ffn_b2"],
                I["L1_ffn_Wr"], I["L1_ffn_br"], (I["L1_ffn_ln_g"], I["L1_ffn_ln_b"]), ACT.Gelu, finish1)


def kernel(**inputs):
    import concourse.bacc as _bacc
    from concourse.bass_utils import run_bass_kernel_spmd as _run

    nc = _bacc.Bacc("TRN2", target_bir_lowering=False, num_devices=1)
    arrays = {}
    edges = np.zeros((EDGE_ROWS, 4), np.int32)
    edges[:, 1] = edges[:, 3] = NOWHERE
    for col, name in ((0, "src"), (1, "dst"), (2, "edge_type_500"), (3, "src")):
        edges[:E, col] = np.asarray(inputs[name])
    arrays["edges"] = edges
    for name, a in inputs.items():
        a = np.asarray(a)
        if name in ("src", "dst", "edge_type_500"):
            continue
        if name in ("L0_ffn_b1", "L1_ffn_b1", "L1_ffn_ln_g", "L1_ffn_ln_b"):
            a = a.reshape(a.shape[0], -1, P).transpose(2, 0, 1)
        if name in ("L1_gnn_msg_w", "L1_gnn_upd_w"):
            a = a.transpose(0, 2, 1)
        if name == "x":
            a = np.concatenate([a, np.zeros((NTP * P - N, D), a.dtype)])
        arrays[name] = np.ascontiguousarray(a)
    args = {n: nc.dram_tensor(f"in_{n}", a.shape, mybir.dt.from_np(a.dtype), kind="ExternalInput").ap() for n, a in arrays.items()}
    out = nc.dram_tensor("out_0", (N, D), F32, kind="ExternalOutput").ap()
    build(nc, args, out)
    r = _run(nc, [{f"in_{n}": a for n, a in arrays.items()}], core_ids=[0])
    return r.results[0]["out_0"]
```
